# Optimizing a Trainium2 kernel written in Bass

```python
import numpy as np
import jax
import jax.numpy as jnp

def _softmax(x, axis=-1):
    return jax.nn.softmax(x, axis=axis)

def _gelu(x):
    return jax.nn.gelu(x, approximate=True)

def _silu(x):
    return jax.nn.silu(x)

def _sigmoid(x):
    return jax.nn.sigmoid(x)

def _layernorm(x, axis=-1, eps=1e-05):
    m = jnp.mean(x, axis=axis, keepdims=True)
    v = jnp.var(x, axis=axis, keepdims=True)
    return (x - m) / jnp.sqrt(v + eps)

def _scatter_add(tgt, idx, src, axis=0):
    return tgt.at[idx].add(src)

def _segment_sum(src, seg, n):
    return jax.ops.segment_sum(src, seg, n)
kernel_name = 'mk_decoder_preln_d2_seqx_r8_a92c1d'

def setup_inputs(seed: int=0):
    np.random.seed(seed)
    _w = jnp.asarray

    def _rec_inputs():
        import jax
        import jax.numpy as jnp
        _rk = jax.random.key(seed)
        x = 2.818e-05 + 1 * jax.random.normal(jax.random.fold_in(_rk, 1), (8, 256, 128), jnp.float32)
        _lenS = 256 - jax.random.randint(jax.random.fold_in(_rk, 7), (8,), 0, max(1, 256 // 4) + 1, jnp.int32)
        _lenS2 = 256 - jax.random.randint(jax.random.fold_in(_rk, 8), (8,), 0, max(1, 256 // 4) + 1, jnp.int32)
        _ctx_2048P = jax.random.normal(jax.random.fold_in(_rk, 11), (8, 16, 256), jnp.float32)
        _ctx_2048c = jax.random.dirichlet(jax.random.fold_in(_rk, 511), 0.3 * jnp.ones((16,), jnp.float32), (8, 256))
        _ctx_2048t = jnp.einsum('bsk,bkd->bsd', _ctx_2048c, _ctx_2048P)
        _ctx_2048t = _ctx_2048t * jax.lax.rsqrt(jnp.mean(jnp.square(_ctx_2048t)) + 1e-12) * 0.953939
        ctx_2048 = -0.000125008 + 0.999885 * (_ctx_2048t + 0.3 * jax.random.normal(jax.random.fold_in(_rk, 611), (8, 256, 256), jnp.float32))
        _validS = jnp.arange(256)[None, :] < _lenS[:, None]
        _validS2 = jnp.arange(256)[None, :] < _lenS2[:, None]
        _causal = jnp.tril(jnp.ones((256, 256), dtype=bool))
        mask_BxS2_fk1 = jnp.where(jnp.broadcast_to(_validS2[:, :], (8, 256)), 1.0, 0.0).astype(jnp.float32)
        mask_BxS2_ik0 = jnp.where(jnp.broadcast_to(_validS2[:, :], (8, 256)), 0, 1).astype(jnp.int32)
        return (x, ctx_2048, mask_BxS2_fk1, mask_BxS2_ik0)
    x, ctx_2048, mask_BxS2_fk1, mask_BxS2_ik0 = _rec_inputs()

    def _L0_attn_setup():
        import jax, jax.numpy as jnp
        import numpy as np
        H = 8
        CHUNK = 64
        GATE_NORM = 16.0
        EPS = 1e-05
        key = jax.random.key(seed)
        ks = jax.random.split(key, 10)
        B, T, D = (8, 512, 128)
        Dk, Dv, LR = (64, 128, 16)
        s = 0.02
        return {'x': jax.random.normal(ks[0], (B, T, D), jnp.float32), 'Wq': jax.random.normal(ks[1], (D, Dk), jnp.float32) * s, 'Wk': jax.random.normal(ks[2], (D, Dk), jnp.float32) * s, 'Wv': jax.random.normal(ks[3], (D, Dv), jnp.float32) * s, 'Wg': jax.random.normal(ks[4], (D, Dv), jnp.float32) * s, 'Wgk1': jax.random.normal(ks[5], (D, LR), jnp.float32) * s, 'Wgk2': jax.random.normal(ks[6], (LR, Dk), jnp.float32) * s, 'bgk2': jnp.zeros((Dk,), jnp.float32), 'norm_w': jnp.ones((Dv // H,), jnp.float32), 'Wo': jax.random.normal(ks[7], (Dv, D), jnp.float32) * s}
    _L0_attn_all = _L0_attn_setup()
    _L0_attn_in = {k: v for k, v in _L0_attn_all.items() if k in ('Wq', 'Wk', 'Wv', 'Wg', 'Wgk1', 'Wgk2', 'bgk2', 'norm_w', 'Wo')}
    del _L0_attn_all

    def _L0_xattn_setup():
        import jax, jax.numpy as jnp
        import numpy as np
        B, S, T = (32, 64, 64)
        SRC_SIZE, TGT_SIZE, OUT_SIZE, NUM_HEAD = (256, 128, 128, 8)
        HEAD_DIM = OUT_SIZE // NUM_HEAD
        key = jax.random.key(seed)
        ks = jax.random.split(key, 12)
        src = jax.random.normal(ks[0], (B, S, SRC_SIZE), dtype=jnp.float32)
        tgt = jax.random.normal(ks[1], (B, T, TGT_SIZE), dtype=jnp.float32)
        src_mask = (jax.random.uniform(ks[2], (B, S)) > 0.3).astype(jnp.float32)
        src_mask = src_mask.at[:, 0].set(1.0)
        tgt_mask = (jax.random.uniform(ks[3], (B, T)) > 0.3).astype(jnp.float32)
        tgt_mask = tgt_mask.at[:, 0].set(1.0)

        def lin(k, out_f, in_f):
            return jax.random.normal(k, (out_f, in_f), dtype=jnp.float32) / np.sqrt(in_f)
        W_src = lin(ks[4], 2 * OUT_SIZE, SRC_SIZE)
        b_src = jnp.zeros((2 * OUT_SIZE,), jnp.float32)
        W_tgt = lin(ks[5], OUT_SIZE, TGT_SIZE)
        b_tgt = jnp.zeros((OUT_SIZE,), jnp.float32)
        W_out = lin(ks[6], OUT_SIZE, OUT_SIZE + TGT_SIZE)
        b_out = jnp.zeros((OUT_SIZE,), jnp.float32)
        return {'src': src, 'tgt': tgt, 'src_mask': src_mask, 'tgt_mask': tgt_mask, 'W_src': W_src, 'b_src': b_src, 'W_tgt': W_tgt, 'b_tgt': b_tgt, 'W_out': W_out, 'b_out': b_out}
    _L0_xattn_all = _L0_xattn_setup()
    _L0_xattn_in = {k: v for k, v in _L0_xattn_all.items() if k in ('W_src', 'b_src', 'W_tgt', 'b_tgt', 'W_out', 'b_out')}
    del _L0_xattn_all

    def _L0_ffn_setup():
        import jax, jax.numpy as jnp
        import numpy as np
        B, S, DIM, FFN, E = (4, 256, 128, 512, 8)
        key = jax.random.key(seed)
        k0, k1, k2, k3 = jax.random.split(key, 4)
        scale = 0.02
        return {'hidden_states': jax.random.normal(k0, (B, S, DIM), jnp.float32), 'router_w': jax.random.normal(k1, (DIM, E), jnp.float32) * scale, 'router_b': jnp.zeros((E,), jnp.float32), 'w1': jax.random.normal(k2, (E, DIM, 2 * FFN), jnp.float32) * scale, 'w2': jax.random.normal(k3, (E, FFN, DIM), jnp.float32) * scale}
    _L0_ffn_all = _L0_ffn_setup()
    _L0_ffn_in = {k: v for k, v in _L0_ffn_all.items() if k in ('router_w', 'router_b', 'w1', 'w2')}
    del _L0_ffn_all

    def _L1_attn_setup():
        import jax, jax.numpy as jnp
        import numpy as np
        D_MODEL, N_HEADS = (128, 16)
        D_H = D_MODEL // N_HEADS
        D_HR = D_H // 2
        D_LATENT = 32
        THETA = 10000.0

        def rope(x, theta=THETA):
            S, d = (x.shape[-2], x.shape[-1])
            inv = theta ** (-jnp.arange(0, d, 2, dtype=jnp.float32) / d)
            ang = jnp.arange(S, dtype=jnp.float32)[:, None] * inv
            cos, sin = (jnp.cos(ang), jnp.sin(ang))
            x1, x2 = (x[..., 0::2], x[..., 1::2])
            r1 = x1 * cos - x2 * sin
            r2 = x1 * sin + x2 * cos
            return jnp.stack([r1, r2], axis=-1).reshape(x.shape)
        key = jax.random.key(seed)
        ks = jax.random.split(key, 9)
        s = lambda fan_in: 1.0 / np.sqrt(fan_in)
        return {'x': jax.random.normal(ks[0], (4, 256, D_MODEL), jnp.float32), 'W_DQ': jax.random.normal(ks[1], (D_MODEL, D_LATENT), jnp.float32) * s(D_MODEL), 'W_UQ': jax.random.normal(ks[2], (D_LATENT, N_HEADS * D_H), jnp.float32) * s(D_LATENT), 'W_QR': jax.random.normal(ks[3], (D_LATENT, N_HEADS * D_HR), jnp.float32) * s(D_LATENT), 'W_DKV': jax.random.normal(ks[4], (D_MODEL, D_LATENT), jnp.float32) * s(D_MODEL), 'W_UK': jax.random.normal(ks[5], (D_LATENT, N_HEADS * D_H), jnp.float32) * s(D_LATENT), 'W_UV': jax.random.normal(ks[6], (D_LATENT, N_HEADS * D_H), jnp.float32) * s(D_LATENT), 'W_KR': jax.random.normal(ks[7], (D_MODEL, D_HR), jnp.float32) * s(D_MODEL), 'W_O': jax.random.normal(ks[8], (N_HEADS * D_H, D_MODEL), jnp.float32) * s(N_HEADS * D_H)}
    _L1_attn_all = _L1_attn_setup()
    _L1_attn_in = {k: v for k, v in _L1_attn_all.items() if k in ('W_DQ', 'W_UQ', 'W_QR', 'W_DKV', 'W_UK', 'W_UV', 'W_KR', 'W_O')}
    del _L1_attn_all

    def _L1_xattn_setup():
        import jax, jax.numpy as jnp
        import numpy as np
        UNITS = 128
        NUM_HEADS = 8

        def _split_heads(x, n):
            B, S, D = x.shape
            return x.reshape(B, S, n, D // n).transpose(0, 2, 1, 3)
        key = jax.random.key(seed)
        k1, k2, k3 = jax.random.split(key, 3)
        B, S = (8, 128)
        memory = jax.random.normal(k1, (B, S, 2 * UNITS), dtype=jnp.float32)
        query = jax.random.normal(k2, (B, S, UNITS), dtype=jnp.float32)
        seq_mask = jax.random.randint(k3, (B, S), 0, 2, dtype=jnp.int32)
        b = jnp.zeros((1,), dtype=jnp.float32)
        return {'memory': memory, 'query': query, 'seq_mask': seq_mask, 'b': b}
    _L1_xattn_all = _L1_xattn_setup()
    _L1_xattn_in = {k: v for k, v in _L1_xattn_all.items() if k in ('b',)}
    del _L1_xattn_all

    def _L1_ffn_setup():
        import jax, jax.numpy as jnp
        import numpy as np
        D_MODEL = 128
        MLP_DIM = 512
        N_EXPERTS = 8
        B, T = (4, 128)
        key = jax.random.key(seed)
        ks = jax.random.split(key, 7)
        scale_in = (1.0 / D_MODEL) ** 0.5
        scale_out = (1.0 / MLP_DIM) ** 0.5
        bound_g = (1.0 / D_MODEL) ** 0.5
        w_gate = jax.random.uniform(ks[0], (D_MODEL, N_EXPERTS), minval=-bound_g, maxval=bound_g, dtype=jnp.float32)
        b_gate = jax.random.uniform(ks[1], (N_EXPERTS,), minval=-bound_g, maxval=bound_g, dtype=jnp.float32)
        W1 = jax.random.uniform(ks[2], (N_EXPERTS, D_MODEL, MLP_DIM), minval=-scale_in, maxval=scale_in, dtype=jnp.float32)
        b1 = jnp.zeros((N_EXPERTS, MLP_DIM), dtype=jnp.float32)
        W2 = jax.random.uniform(ks[3], (N_EXPERTS, MLP_DIM, D_MODEL), minval=-scale_out, maxval=scale_out, dtype=jnp.float32)
        b2 = jnp.zeros((N_EXPERTS, D_MODEL), dtype=jnp.float32)
        x = jax.random.normal(ks[4], (B, T, D_MODEL), dtype=jnp.float32)
        return {'x': x, 'w_gate': w_gate, 'b_gate': b_gate, 'W1': W1, 'b1': b1, 'W2': W2, 'b2': b2}
    _L1_ffn_all = _L1_ffn_setup()
    _L1_ffn_in = {k: v for k, v in _L1_ffn_all.items() if k in ('w_gate', 'b_gate', 'W1', 'b1', 'W2', 'b2')}
    del _L1_ffn_all
    return {'x': x, 'ctx_2048': ctx_2048, 'mask_BxS2_fk1': mask_BxS2_fk1, 'mask_BxS2_ik0': mask_BxS2_ik0, 'L0_attn_Wq': _L0_attn_in['Wq'], 'L0_attn_Wk': _L0_attn_in['Wk'], 'L0_attn_Wv': _L0_attn_in['Wv'], 'L0_attn_Wg': _L0_attn_in['Wg'], 'L0_attn_Wgk1': _L0_attn_in['Wgk1'], 'L0_attn_Wgk2': _L0_attn_in['Wgk2'], 'L0_attn_bgk2': _L0_attn_in['bgk2'], 'L0_attn_norm_w': _L0_attn_in['norm_w'], 'L0_attn_Wo': _L0_attn_in['Wo'], 'L0_xattn_W_src': _L0_xattn_in['W_src'], 'L0_xattn_b_src': _L0_xattn_in['b_src'], 'L0_xattn_W_tgt': _L0_xattn_in['W_tgt'], 'L0_xattn_b_tgt': _L0_xattn_in['b_tgt'], 'L0_xattn_W_out': _L0_xattn_in['W_out'], 'L0_xattn_b_out': _L0_xattn_in['b_out'], 'L0_ffn_router_w': _L0_ffn_in['router_w'], 'L0_ffn_router_b': _L0_ffn_in['router_b'], 'L0_ffn_w1': _L0_ffn_in['w1'], 'L0_ffn_w2': _L0_ffn_in['w2'], 'L1_attn_W_DQ': _L1_attn_in['W_DQ'], 'L1_attn_W_UQ': _L1_attn_in['W_UQ'], 'L1_attn_W_QR': _L1_attn_in['W_QR'], 'L1_attn_W_DKV': _L1_attn_in['W_DKV'], 'L1_attn_W_UK': _L1_attn_in['W_UK'], 'L1_attn_W_UV': _L1_attn_in['W_UV'], 'L1_attn_W_KR': _L1_attn_in['W_KR'], 'L1_attn_W_O': _L1_attn_in['W_O'], 'L1_xattn_b': _L1_xattn_in['b'], 'L1_ffn_w_gate': _L1_ffn_in['w_gate'], 'L1_ffn_b_gate': _L1_ffn_in['b_gate'], 'L1_ffn_W1': _L1_ffn_in['W1'], 'L1_ffn_b1': _L1_ffn_in['b1'], 'L1_ffn_W2': _L1_ffn_in['W2'], 'L1_ffn_b2': _L1_ffn_in['b2']}

def reference(x, ctx_2048, mask_BxS2_fk1, mask_BxS2_ik0, L0_attn_Wq, L0_attn_Wk, L0_attn_Wv, L0_attn_Wg, L0_attn_Wgk1, L0_attn_Wgk2, L0_attn_bgk2, L0_attn_norm_w, L0_attn_Wo, L0_xattn_W_src, L0_xattn_b_src, L0_xattn_W_tgt, L0_xattn_b_tgt, L0_xattn_W_out, L0_xattn_b_out, L0_ffn_router_w, L0_ffn_router_b, L0_ffn_w1, L0_ffn_w2, L1_attn_W_DQ, L1_attn_W_UQ, L1_attn_W_QR, L1_attn_W_DKV, L1_attn_W_UK, L1_attn_W_UV, L1_attn_W_KR, L1_attn_W_O, L1_xattn_b, L1_ffn_w_gate, L1_ffn_b_gate, L1_ffn_W1, L1_ffn_b1, L1_ffn_W2, L1_ffn_b2):
    import jax
    import jax.numpy as jnp

    def _L0_attn_ref(x, Wq, Wk, Wv, Wg, Wgk1, Wgk2, bgk2, norm_w, Wo):
        import jax, jax.numpy as jnp
        import numpy as np
        H = 8
        CHUNK = 64
        GATE_NORM = 16.0
        EPS = 1e-05
        B, T, D = x.shape
        Dk, Dv = (Wq.shape[1], Wv.shape[1])
        dk, dv = (Dk // H, Dv // H)
        N = T // CHUNK
        scale = dk ** (-0.5)
        q = x @ Wq
        k = x @ Wk
        v = x @ Wv
        g = x @ Wg
        gk = jax.nn.log_sigmoid(x @ Wgk1 @ Wgk2 + bgk2) / GATE_NORM

        def to_chunks(a, d):
            return a.reshape(B, N, CHUNK, H, d).transpose(1, 0, 3, 2, 4)
        qc, kc, vc, gkc = (to_chunks(q, dk), to_chunks(k, dk), to_chunks(v, dv), to_chunks(gk, dk))
        mask = jnp.tril(jnp.ones((CHUNK, CHUNK), x.dtype))

        def step(S, inp):
            qi, ki, vi, gi = inp
            b = jnp.cumsum(gi, axis=2)
            qe = qi * jnp.exp(b) * scale
            ke = ki * jnp.exp(-b)
            A = jnp.einsum('bhik,bhjk->bhij', qe, ke) * mask
            o = A @ vi + jnp.einsum('bhck,bhkv->bhcv', qe, S)
            b_last = b[:, :, -1, :]
            kd = ki * jnp.exp(b_last[:, :, None, :] - b)
            S = S * jnp.exp(b_last)[..., None] + jnp.einsum('bhck,bhcv->bhkv', kd, vi)
            return (S, o)
        S0 = jnp.zeros((B, H, dk, dv), x.dtype)
        _, o = jax.lax.scan(step, S0, (qc, kc, vc, gkc))
        o = o.transpose(1, 0, 3, 2, 4).reshape(B, T, H, dv)
        gg = g.reshape(B, T, H, dv)
        o = o * jax.lax.rsqrt(jnp.mean(o * o, axis=-1, keepdims=True) + EPS) * norm_w
        o = o * (gg * jax.nn.sigmoid(gg))
        return o.reshape(B, T, Dv) @ Wo

    def _L0_xattn_ref(src, tgt, src_mask, tgt_mask, W_src, b_src, W_tgt, b_tgt, W_out, b_out):
        import jax, jax.numpy as jnp
        import numpy as np
        B, S, T = (32, 64, 64)
        SRC_SIZE, TGT_SIZE, OUT_SIZE, NUM_HEAD = (256, 128, 128, 8)
        HEAD_DIM = OUT_SIZE // NUM_HEAD
        b, s, _ = src.shape
        t = tgt.shape[1]
        src_trans = jnp.einsum('bsf,of->bso', src, W_src) + b_src
        tgt_trans = jnp.einsum('btf,of->bto', tgt, W_tgt) + b_tgt
        src_trans = src_trans * src_mask[:, :, None]
        tgt_trans = tgt_trans * tgt_mask[:, :, None]
        src_key, src_val = jnp.split(src_trans, 2, axis=2)
        k = src_key.reshape(b, s, NUM_HEAD, HEAD_DIM)
        v = src_val.reshape(b, s, NUM_HEAD, HEAD_DIM)
        q = tgt_trans.reshape(b, t, NUM_HEAD, HEAD_DIM)
        scores = jnp.einsum('bthd,bshd->bhts', q, k) / np.sqrt(HEAD_DIM)
        scores = jnp.where(src_mask[:, None, None, :] == 0, -jnp.inf, scores)
        attn = jax.nn.softmax(scores, axis=-1)
        tgt_update = jnp.einsum('bhts,bshd->bthd', attn, v).reshape(b, t, OUT_SIZE)
        cat_tgt = jnp.concatenate([tgt, tgt_update], axis=2)
        return jnp.einsum('btf,of->bto', cat_tgt, W_out) + b_out

    def _L0_ffn_ref(hidden_states, router_w, router_b, w1, w2):
        import jax, jax.numpy as jnp
        import numpy as np
        B, S, DIM, FFN, E = (4, 256, 128, 512, 8)
        b, s, d = hidden_states.shape
        x = hidden_states.reshape(-1, d)
        logits = x @ router_w + router_b
        route = jax.nn.softmax(logits, axis=1)
        max_prob = jnp.max(route, axis=1, keepdims=True)
        max_ind = jnp.argmax(route, axis=1)
        out = jnp.zeros_like(x)
        num_experts = w1.shape[0]
        for e in range(num_experts):
            h = x @ w1[e]
            a, g = jnp.split(h, 2, axis=1)
            y = jax.nn.silu(a) * g @ w2[e]
            out = jnp.where((max_ind == e)[:, None], y, out)
        out = out * max_prob
        return out.reshape(b, s, d)

    def _L1_attn_ref(x, W_DQ, W_UQ, W_QR, W_DKV, W_UK, W_UV, W_KR, W_O):
        import jax, jax.numpy as jnp
        import numpy as np
        D_MODEL, N_HEADS = (128, 16)
        D_H = D_MODEL // N_HEADS
        D_HR = D_H // 2
        D_LATENT = 32
        THETA = 10000.0

        def rope(x, theta=THETA):
            S, d = (x.shape[-2], x.shape[-1])
            inv = theta ** (-jnp.arange(0, d, 2, dtype=jnp.float32) / d)
            ang = jnp.arange(S, dtype=jnp.float32)[:, None] * inv
            cos, sin = (jnp.cos(ang), jnp.sin(ang))
            x1, x2 = (x[..., 0::2], x[..., 1::2])
            r1 = x1 * cos - x2 * sin
            r2 = x1 * sin + x2 * cos
            return jnp.stack([r1, r2], axis=-1).reshape(x.shape)
        B, S, _ = x.shape
        d_qk = D_H + D_HR
        c_q = x @ W_DQ
        Qc = (c_q @ W_UQ).reshape(B, S, N_HEADS, D_H).transpose(0, 2, 1, 3)
        Qr = (c_q @ W_QR).reshape(B, S, N_HEADS, D_HR).transpose(0, 2, 1, 3)
        Qr = rope(Qr)
        c_kv = x @ W_DKV
        Kc = (c_kv @ W_UK).reshape(B, S, N_HEADS, D_H).transpose(0, 2, 1, 3)
        Kr = rope((x @ W_KR)[:, None, :, :])
        Kr = jnp.broadcast_to(Kr, (B, N_HEADS, S, D_HR))
        V = (c_kv @ W_UV).reshape(B, S, N_HEADS, D_H).transpose(0, 2, 1, 3)
        Q = jnp.concatenate([Qc, Qr], axis=-1)
        K = jnp.concatenate([Kc, Kr], axis=-1)
        scores = jnp.einsum('bhqd,bhkd->bhqk', Q, K)
        scores = jnp.clip(scores, -80.0, 80.0)
        causal = jnp.tril(jnp.ones((S, S), dtype=bool))
        scores = jnp.where(causal, scores, -jnp.inf)
        weights = jax.nn.softmax(scores / jnp.sqrt(jnp.float32(d_qk)), axis=-1)
        attn = jnp.einsum('bhqk,bhkd->bhqd', weights, V)
        attn = attn.transpose(0, 2, 1, 3).reshape(B, S, N_HEADS * D_H)
        return attn @ W_O

    def _L1_xattn_ref(memory, query, seq_mask, b):
        import jax, jax.numpy as jnp
        import numpy as np
        UNITS = 128
        NUM_HEADS = 8

        def _split_heads(x, n):
            B, S, D = x.shape
            return x.reshape(B, S, n, D // n).transpose(0, 2, 1, 3)
        H = NUM_HEADS
        depth = UNITS // H
        Q = _split_heads(query, H) * depth ** (-0.5)
        k_mem, v_mem = jnp.split(memory, 2, axis=2)
        K = _split_heads(k_mem, H)
        V = _split_heads(v_mem, H)
        logits = jnp.einsum('bhqd,bhkd->bhqk', Q, K) + b[0]
        mask = seq_mask.astype(jnp.float32)[:, None, None, :]
        logits = logits + -1e+30 * (1.0 - mask)
        weights = jax.nn.softmax(logits, axis=-1)
        out = jnp.einsum('bhqk,bhkd->bhqd', weights, V)
        B, _, S, _ = out.shape
        return out.transpose(0, 2, 1, 3).reshape(B, S, UNITS)

    def _L1_ffn_ref(x, w_gate, b_gate, W1, b1, W2, b2):
        import jax, jax.numpy as jnp
        import numpy as np
        D_MODEL = 128
        MLP_DIM = 512
        N_EXPERTS = 8
        B, T = (4, 128)
        b, t, d = x.shape
        x_flat = x.reshape(b * t, d)
        logits = x_flat @ w_gate + b_gate
        probs = jax.nn.softmax(logits, axis=-1)
        route_p = jnp.max(probs, axis=-1)
        route_idx = jnp.argmax(probs, axis=-1)
        h = jnp.einsum('nd,edm->enm', x_flat, W1) + b1[:, None, :]
        h = jax.nn.relu(h)
        y = jnp.einsum('enm,emd->end', h, W2) + b2[:, None, :]
        n = b * t
        out = y[route_idx, jnp.arange(n)] * route_p[:, None]
        return out.reshape(b, t, d)
    x = x + _L0_attn_ref(_layernorm(x, axis=-1), L0_attn_Wq, L0_attn_Wk, L0_attn_Wv, L0_attn_Wg, L0_attn_Wgk1, L0_attn_Wgk2, L0_attn_bgk2, L0_attn_norm_w, L0_attn_Wo)
    x = x + _L0_xattn_ref(ctx_2048, _layernorm(x, axis=-1), mask_BxS2_fk1, mask_BxS2_fk1, L0_xattn_W_src, L0_xattn_b_src, L0_xattn_W_tgt, L0_xattn_b_tgt, L0_xattn_W_out, L0_xattn_b_out)
    x = x + _L0_ffn_ref(_layernorm(x, axis=-1), L0_ffn_router_w, L0_ffn_router_b, L0_ffn_w1, L0_ffn_w2)
    x = x + _L1_attn_ref(_layernorm(x, axis=-1), L1_attn_W_DQ, L1_attn_W_UQ, L1_attn_W_QR, L1_attn_W_DKV, L1_attn_W_UK, L1_attn_W_UV, L1_attn_W_KR, L1_attn_W_O)
    x = x + _L1_xattn_ref(ctx_2048, _layernorm(x, axis=-1), mask_BxS2_ik0, L1_xattn_b)
    x = x + _L1_ffn_ref(_layernorm(x, axis=-1), L1_ffn_w_gate, L1_ffn_b_gate, L1_ffn_W1, L1_ffn_b1, L1_ffn_W2, L1_ffn_b2)
    return x

_drawn_inputs = setup_inputs


def setup_inputs(seed=0):
    import zlib

    import numpy as np

    out = dict(_drawn_inputs(seed))
    spreads = {'L0_attn_bgk2': (0.0, 0.8),
     'L0_attn_norm_w': (1.0, 0.6),
     'L0_xattn_b_src': (0.0, 0.1),
     'L0_xattn_b_tgt': (0.0, 0.597),
     'L0_xattn_b_out': (0.0, 0.1),
     'L0_ffn_router_b': (0.0, 0.8),
     'L1_ffn_b1': (0.0, 2.0),
     'L1_ffn_b2': (0.0, 1.376)}
    factors = {'L0_attn_Wgk1': 8.0,
     'L0_attn_Wgk2': 8.0,
     'L0_ffn_router_w': 8.0,
     'L0_ffn_w1': 8.0,
     'L0_ffn_w2': 8.0,
     'L1_ffn_b_gate': 18.159,
     'L1_attn_W_QR': 2.796,
     'L1_ffn_W1': 4.606}
    for name, (base, spread) in spreads.items():
        noise = np.random.default_rng([zlib.crc32(name.encode()), seed]).standard_normal(out[name].shape)
        drawn = base * np.exp(spread * noise) if base else spread * noise
        out[name] = jnp.asarray(drawn.astype(out[name].dtype))
    for name, factor in factors.items():
        out[name] = (out[name] * factor).astype(out[name].dtype)
    return out
```

```python
import numpy as np
import concourse.bass as bass
from concourse import mybir
from contextlib import ExitStack

FP32 = mybir.dt.float32
I32 = mybir.dt.int32
U32 = mybir.dt.uint32
ALU = mybir.AluOpType
ACT = mybir.ActivationFunctionType
AX = mybir.AxisListType

B, T, D, DC = 8, 256, 128, 256
P = 128
TILES = B * T // P
QT = 4
QN = QT * P
QUADS = TILES // QT
QB = QN // T
CHUNK = 64
GH, DK, DV = 8, 8, 16
XH, XD = 8, 16
XV = XD + 1
STRIP = 32
XG = XH // 4
ROW_BIAS, ROW_MAX = 16, 17
MH, MD, MR, ML = 16, 8, 4, 32
MV = MD + 1
MG = MH // 4
EXP, F = 8, 512
SLOTS = 24
EPS = 1e-5
BIG = 1e30
CLIP = 80.0

CONST_PLAN = [("ident", 128), ("chunk_mask", 128), ("tri", 128), ("ones", 128), ("head_mask", 8),
              ("block_mask", 128), ("reset", 512), ("clip_mask", 128), ("lat_rope", 256),
              ("q_rope", 256), ("sel_q", XG * 128), ("sel_rope", MG * 128), ("iota8", 8),
              ("iota8m", 8), ("slot_iota", SLOTS), ("scan_reset", 128), ("neg_half", 32), ("eps", 32),
              ("tile_starts", TILES), ("mq_a", 1), ("mq_b", 1), ("mk_a", 1),
              ("mk_b", 1), ("is_bias", 1), ("is_max", 1), ("bias_big", 1)]
WEIGHT_PLAN = [("wq", 64), ("wk", 64), ("wv", 128), ("wg", 128), ("wgk1", 16), ("wgk2", 64), ("bgk", 1),
               ("norm_w", 16), ("wo", 128), ("x_q", XG * 128), ("x_k", 2 * XG * 128), ("x_v", 2 * 128),
               ("x_qb", XG), ("x_kb", XG), ("x_vb", 128), ("x_out", 2 * 128), ("x_ob", 128),
               ("r0_w", EXP), ("r0_b", EXP), ("m_lat", 128), ("m_qr", 128), ("m_q", MG * 128),
               ("m_k", MG * 128), ("m_v", 128), ("m_o", 128), ("x1_b", 1), ("r1_w", EXP), ("r1_b", EXP),
               ("b1", EXP * 4), ("b2", EXP * D)]


def columns(plan):
    at, out = 0, {}
    for name, n in plan:
        out[name] = (at, n)
        at += n
    return out, at


CC, CN = columns(CONST_PLAN)
WC, WN = columns(WEIGHT_PLAN)


def build(nc, A):
    ctx = ExitStack()
    with ctx:
        def sb(name, shape, dt=FP32):
            return ctx.enter_context(nc.sbuf_tensor(name, shape, dt))

        sems = {}

        def S(name):
            if name not in sems:
                sems[name] = ctx.enter_context(nc.semaphore(name))
            return sems[name]

        cst = sb("cst", [P, CN])
        wts = sb("wts", [P, WN])

        def C(name, rows=P, r0=0):
            a, n = CC[name]
            return cst[r0:r0 + rows, a:a + n]

        def W(name, rows=P, r0=0):
            a, n = WC[name]
            return wts[r0:r0 + rows, a:a + n]

        x_all = sb("x_all", [P, TILES, D])
        xn_all = sb("xn_all", [P, TILES, D])
        xq = sb("xq", [P, QT, D])
        xn = sb("xn", [P, QT, D])
        xnT = sb("xnT", [P, QN])
        unused = sb("unused", [P, 1])
        stats = sb("stats", [P, QT, 6])
        mv = sb("mv", [P, QT, 2])
        ve = sb("ve", [P, QT])
        rstd = sb("rstd", [P, QT])
        qe = sb("qe", [64, QN])
        kdn = sb("kdn", [P, QT, 64])
        vg = sb("vg", [P, QT, D])
        gate = sb("gate", [P, QT, D])
        qe_bd = sb("qe_bd", [64, 2, GH, P])
        am = sb("am", [P, 2, GH, P])
        st = sb("st", [64, 3, QB, D])
        o_sb = sb("o_sb", [P, QT, D])
        o_sq = sb("o_sq", [P, QT, D])
        ss = sb("ss", [P, QT * GH])
        rs = sb("rs", [P, QT * GH])
        oT = sb("oT", [P, QN])
        ctxT = sb("ctxT", [P, 2, QN])
        mask_row = sb("mask_row", [P, B * T])
        mq = sb("mq", [P, B * T])
        mask_col = sb("mask_col", [P, TILES])
        has = sb("has", [P, B])
        nothas = sb("nothas", [P, B])
        mask_i = mask_row[:, :].bitcast(I32)
        hs = sb("hs", [P, B])
        c1 = sb("c1", [P, 1])
        qa = sb("qa", [P, MG, QN])
        ka = sb("ka", [P, MG, QN])
        vx = sb("vx", [P, QT, XH, XV])
        vm = sb("vm", [P, QT, MH, MV])
        nm = sb("nm", [P, QB, 2, XG, P])
        pT = sb("pT", [P, 3, 1024])
        lr, absz, negz, cum = ka[0:16, 0, :], ka[0:64, 1, :], ka[0:64, 2, :], ka[0:64, 3, :]
        eb, enb, ke, kd = (qa[0:64, g, :] for g in range(MG))
        lat, tq = (t[:, :, :].rearrange("p a b -> p (a b)") for t in (gate, vg))
        cl = am[:, :, :, :].rearrange("p a h i -> p a (h i)")
        rden = sb("rden", [P, 2, MH])
        lg = sb("lg", [P, TILES, EXP])
        lmax = sb("lmax", [P, TILES])
        lex = sb("lex", [P, TILES, EXP])
        lsum = sb("lsum", [P, TILES])
        prob = sb("prob", [P, TILES])
        amin = sb("amin", [P, TILES])
        onehot = sb("onehot", [P, TILES, EXP])
        tie = sb("tie", [P, TILES, EXP])
        cnt = sb("cnt", [P, EXP, TILES])
        incl = sb("incl", [P, EXP, TILES])
        more = sb("more", [P, EXP, TILES])
        ntile = sb("ntile", [P, EXP])
        ends = sb("ends", [P, EXP])
        starts = sb("starts", [P, EXP])
        pos_f = sb("pos_f", [P, TILES])
        pos = sb("pos", [P, TILES], U32)
        slot_ge = sb("slot_ge", [P, SLOTS, EXP])
        slot_f = sb("slot_f", [P, SLOTS])
        slot_e = sb("slot_e", [P, SLOTS], I32)
        zeros = sb("zeros", [P, D])
        w1 = sb("w1", [P, EXP * 2 * F])
        w2 = sb("w2", [P, EXP * 4 * D])
        w1b, w2b = w1[:, 0:EXP * F], w1[:, EXP * F:2 * EXP * F]
        xs = sb("xs", [P, 2, D])
        xsT = sb("xsT", [P, 2, P])
        act_a = am[:, 0, :, :].rearrange("p h i -> p (h i)").rearrange("p (s f) -> p s f", s=2)
        hid = am[:, 1, :, :].rearrange("p h i -> p (h i)").rearrange("p (s f) -> p s f", s=2)
        hidT = sb("hidT", [P, 2, F])
        ys = sb("ys", [P, 2, D])
        ps = ctx.enter_context(nc.psum_tensor("ps", [P, 8, 512], FP32))

        def bank(b, rows=P, r0=0):
            return ps[r0:r0 + rows, b, :]

        ident = C("ident")
        block = ctx.enter_context(nc.Block())

        def tri3(ap, k):
            return ap.rearrange("p (a b) -> p a b", a=k)

        def dve_wait(v, sem, value):
            v.wait_ge(sem, value)
            v.memset(unused[0:1, 0:1], 0.0)

        def dve_ln(v, tag, n):
            for j in range(QT):
                v.bn_stats(stats[:, j, :], xq[:, j, :]).then_inc(S(tag + "stats"), 1)
            dve_wait(v, S(tag + "stats"), (n + 1) * QT)
            for j in range(QT):
                i = v.bn_aggr(mv[:, j, :], stats[:, j, :])
            i.then_inc(S(tag + "mv"), 1)
            v.wait_ge(S(tag + "rstd"), n + 1)
            v.wait_ge(S(tag + "mv"), n + 1)
            for j in range(QT):
                v.tensor_scalar(xn[:, j, :], xq[:, j, :], mv[:, j, 0:1], rstd[:, j:j + 1],
                                ALU.subtract, ALU.mult).then_inc(S(tag + "xn"), 1)

        def pool_ln(g, tag, n):
            g.wait_ge(S(tag + "mv"), n + 1)
            g.tensor_tensor(ve[:, :], mv[:, :, 1], C("eps")[:, 0:QT], ALU.add).then_inc(S(tag + "ve"), 1)
            g.wait_ge(S(tag + "ve"), n + 1)
            g.tensor_tensor(rstd[:, :], ve[:, :], C("neg_half")[:, 0:QT], ALU.pow).then_inc(S(tag + "rstd"), 1)

        def pe_ln(pe, tag, n, b):
            for j in range(QT):
                pe.wait_ge(S(tag + "xn"), n * QT + j + 1)
                i = pe.transpose(bank(b)[:, j * P:(j + 1) * P], xn[:, j, :], ident)
            i.then_inc(S(tag + "xnT_ps"), 1)

        def act_ln(a, tag, n, b):
            a.wait_ge(S(tag + "xnT_ps"), n + 1)
            a.activation(xnT[:, :], bank(b), ACT.Copy).then_inc(S(tag + "xnT"), 1)

        def pe_gla(pe, n):
            pe.wait_ge(S("A_xnT"), n + 1)
            pe.matmul(bank(3, 16), W("wgk1"), xnT[:, :], start=True, stop=True).then_inc(S("lr_ps"), 1)
            pe.matmul(bank(1, 64), W("wq"), xnT[:, :], start=True, stop=True).then_inc(S("q_ps"), 1)
            pe.matmul(bank(2, 64), W("wk"), xnT[:, :], start=True, stop=True).then_inc(S("k_ps"), 1)
            pe.wait_ge(S("lr_sb"), n + 1)
            pe.matmul(bank(4, 64), W("wgk2", 16), lr[:, :], start=True, stop=True).then_inc(S("z_ps"), 1)
            for w, b, s in (("wv", 5, "v_ps"), ("wg", 6, "g_ps")):
                for j in range(QT):
                    i = pe.matmul(bank(b)[:, j * P:(j + 1) * P], xnT[:, j * P:(j + 1) * P], W(w),
                                  start=True, stop=True)
                i.then_inc(S(s), 1)
            pe.wait_ge(S("kd"), n + 1)
            for j in range(QT):
                i = pe.matmul(bank(3)[:, j * 64:(j + 1) * 64], kd[:, j * P:(j + 1) * P], ident[0:64, 0:64],
                              start=True, stop=True)
            i.then_inc(S("kdT_ps"), 1)

            def scores(j):
                pe.wait_ge(S("qe_bd"), n * QT + j + 1)
                if j >= 2:
                    pe.wait_ge(S("am"), n * QT + j - 1)
                for h in range(2):
                    i = pe.matmul(bank(2 * (j % 2) + h), ke[:, j * P:(j + 1) * P],
                                  qe_bd[:, j % 2, 4 * h:4 * h + 4, :], start=True, stop=True)
                i.then_inc(S("sc_ps"), 1)

            def outputs(j):
                if j == 0:
                    pe.wait_ge(S("st"), 2 * (n + 1))
                pe.wait_ge(S("am"), n * QT + j + 1)
                o = bank(5)[:, j * P:(j + 1) * P]
                for h in range(GH):
                    pe.matmul(o[:, h * DV:(h + 1) * DV], am[:, j % 2, h, :], vg[:, j, h * DV:(h + 1) * DV],
                              start=(h == 0), stop=False, skip_group_check=True)
                for c in range(2 * (j % 2), 2 * (j % 2) + 2):
                    if c == 0:
                        continue
                    r = CHUNK * (c % 2)
                    i = pe.matmul(bank(5)[r:r + CHUNK, j * P:(j + 1) * P], qe[:, j * P + r:j * P + r + CHUNK],
                                  st[:, c - 1, j // 2, :], start=False, stop=True, skip_group_check=True)
                i.then_inc(S("o_ps"), 1)

            pe.wait_ge(S("kdn"), n + 1)
            pe.wait_ge(S("v_sb"), n + 1)
            scores(0)
            for c in range(3):
                for b in range(QB):
                    j, r = 2 * b + c // 2, CHUNK * (c % 2)
                    out = bank(4, 64)[:, (c // 2 * QB + b) * D:(c // 2 * QB + b + 1) * D] if c % 2 == 0 \
                        else bank(7, 64)[:, b * D:(b + 1) * D]
                    i = pe.matmul(out, kdn[r:r + CHUNK, j, :], vg[r:r + CHUNK, j, :], start=True, stop=True)
            i.then_inc(S("u_ps"), 1)
            scores(1)
            for j in range(QT):
                outputs(j)
                if j + 2 < QT:
                    scores(j + 2)
            for j in range(QT):
                pe.wait_ge(S("og"), n + 1)
                i = pe.transpose(bank(6)[:, j * P:(j + 1) * P], o_sb[:, j, :], ident)
            i.then_inc(S("goT_ps"), 1)
            pe.wait_ge(S("goT"), n + 1)
            for j in range(QT):
                i = pe.matmul(bank(7)[:, j * P:(j + 1) * P], oT[:, j * P:(j + 1) * P], W("wo"),
                              start=True, stop=True)
            i.then_inc(S("gla_ps"), 1)

        def act_gla(a, n):
            a.wait_ge(S("lr_ps"), n + 1)
            a.activation(lr[:, :], bank(3, 16), ACT.Copy).then_inc(S("lr_sb"), 1)
            a.wait_ge(S("v_ps"), n + 1)
            a.activation(vg[:, :, :], tri3(bank(5), QT), ACT.Copy).then_inc(S("v_sb"), 1)
            a.wait_ge(S("z_ps"), n + 1)
            a.activation(absz[:, :], bank(4, 64), ACT.Abs, bias=W("bgk", 64)).then_inc(S("absz"), 1)
            a.wait_ge(S("absz"), n + 1)
            a.activation(absz[:, :], absz[:, :], ACT.Exp, scale=-1.0).then_inc(S("expz"), 1)
            a.wait_ge(S("expz"), n + 1)
            a.activation(absz[:, :], absz[:, :], ACT.Ln, bias=1.0).then_inc(S("lnz"), 1)
            a.wait_ge(S("cum"), n + 1)
            a.activation(eb[:, :], cum[:, :], ACT.Exp, scale=1.0 / 16).then_inc(S("eb"), 1)
            a.activation(enb[:, :], cum[:, :], ACT.Exp, scale=-1.0 / 16).then_inc(S("enb"), 1)
            a.wait_ge(S("g_ps"), n + 1)
            a.activation(gate[:, :, :], tri3(bank(6), QT), ACT.Silu).then_inc(S("silu"), 1)
            a.wait_ge(S("kdT_ps"), n + 1)
            a.activation(kdn[:, :, :], bank(3)[:, 0:QT * 64].rearrange("p (a b) -> p a b", a=QT),
                         ACT.Copy).then_inc(S("kdn"), 1)
            a.wait_ge(S("o_ps"), n * QT + QT)
            a.activation(o_sq[:, :, :], tri3(bank(5), QT), ACT.Square, scale=float(DV) ** -0.5).then_inc(S("o_sq"), 1)
            a.activation(o_sb[:, :, :], tri3(bank(5), QT), ACT.Copy).then_inc(S("o_sb"), 1)
            a.wait_ge(S("goT_ps"), n + 1)
            a.activation(oT[:, :], bank(6), ACT.Copy).then_inc(S("goT"), 1)

        def dve_gla(v, n):
            v.wait_ge(S("absz"), n + 1)
            v.tensor_scalar(negz[:, :], bank(4, 64), W("bgk", 64), 0.0, ALU.add, ALU.min)\
             .then_inc(S("negz"), 1)
            v.wait_ge(S("lnz"), n + 1)
            v.wait_ge(S("negz"), n + 1)
            v.tensor_tensor(negz[:, :], negz[:, :], absz[:, :], ALU.subtract).then_inc(S("gk"), 1)
            v.wait_ge(S("gk"), n + 1)
            v.tensor_tensor_scan(cum[:, :], C("reset", 64), negz[:, :], 0.0, ALU.mult, ALU.add)\
             .then_inc(S("cum"), 1)
            v.wait_ge(S("eb"), n + 1)
            v.wait_ge(S("q_ps"), n + 1)
            v.scalar_tensor_tensor(qe[:, :], bank(1, 64), float(DK) ** -0.5, eb[:, :], ALU.mult, ALU.mult)\
             .then_inc(S("qe"), 1)
            v.wait_ge(S("enb"), n + 1)
            v.wait_ge(S("k_ps"), n + 1)
            v.tensor_tensor(ke[:, :], bank(2, 64), enb[:, :], ALU.mult).then_inc(S("ke"), 1)
            v.wait_ge(S("ke"), n + 1)
            eb3 = eb[:, :].rearrange("p (c t) -> p c t", t=CHUNK)
            last = eb3[:, :, CHUNK - 1:CHUNK].broadcast_to([64, QN // CHUNK, CHUNK])
            v.tensor_tensor(kd[:, :].rearrange("p (c t) -> p c t", t=CHUNK),
                            ke[:, :].rearrange("p (c t) -> p c t", t=CHUNK), last, ALU.mult)\
             .then_inc(S("kd"), 1)

            def masked(j):
                v.wait_ge(S("sc_ps"), n * QT + j + 1)
                if j >= 2:
                    v.wait_ge(S("o_ps"), n * QT + j - 1)
                r = 2 * (j % 2)
                v.tensor_tensor(am[:, j % 2, :, :],
                                ps[:, r:r + 2, :].rearrange("p b (h i) -> p (b h) i", h=4),
                                C("chunk_mask").unsqueeze(1).broadcast_to([P, GH, P]), ALU.mult)\
                 .then_inc(S("am"), 1)

            masked(0)
            v.wait_ge(S("u_ps"), n + 1)
            bd = C("block_mask", 64).unsqueeze(1).broadcast_to([64, QB, D])
            for c in range(3):
                u = bank(4, 64)[:, c // 2 * QB * D:(c // 2 + 1) * QB * D] if c % 2 == 0 \
                    else bank(7, 64)[:, 0:QB * D]
                v.tensor_tensor(st[:, c, :, :], u.rearrange("p (b d) -> p b d", b=QB), bd, ALU.mult)\
                 .then_inc(S("st_u"), 1)
            v.wait_ge(S("st_u"), 3 * (n + 1))
            for c in range(1, 3):
                if c == 2:
                    v.wait_ge(S("st"), 2 * n + 1)
                for b in range(QB):
                    k = b * (T // CHUNK) + c
                    i = v.scalar_tensor_tensor(st[:, c, b, :], st[:, c - 1, b, :],
                                               eb3[:, k, CHUNK - 1:CHUNK],
                                               st[:, c, b, :], ALU.mult, ALU.add)
                i.then_inc(S("st"), 1)
            for j in range(1, QT):
                masked(j)
            v.wait_ge(S("o_sq"), n + 1)
            v.tensor_reduce(ss[:, :], o_sq[:, :, :].rearrange("p a (h d) -> p (a h) d", d=DV), AX.X, ALU.add)\
             .then_inc(S("ss"), 1)
            v.wait_ge(S("o_sb"), n + 1)
            v.wait_ge(S("rs"), n + 1)
            o3 = o_sb[:, :, :].rearrange("p a (h d) -> p (a h) d", d=DV)
            v.tensor_tensor(o3, o3, rs[:, :].unsqueeze(2).broadcast_to([P, QT * GH, DV]), ALU.mult)\
             .then_inc(S("on"), 1)
            v.wait_ge(S("on"), n + 1)
            v.wait_ge(S("gw"), n + 1)
            v.tensor_tensor(o_sb[:, :, :], o_sb[:, :, :], gate[:, :, :], ALU.mult).then_inc(S("og"), 1)
            v.wait_ge(S("gla_ps"), n + 1)
            v.tensor_tensor(xq[:, :, :], xq[:, :, :], tri3(bank(7), QT), ALU.add).then_inc(S("x1"), 1)
            v.wait_ge(S("x1"), n + 1)

        def pool_gla(g, n):
            g.wait_ge(S("qe"), n + 1)
            for j in range(QT):
                if j >= 2:
                    g.wait_ge(S("sc_ps"), n * QT + j - 1)
                g.tensor_tensor(qe_bd[:, j % 2, :, :],
                                qe[:, j * P:(j + 1) * P].unsqueeze(1).broadcast_to([64, GH, P]),
                                C("head_mask", 64).unsqueeze(2).broadcast_to([64, GH, P]), ALU.mult)\
                 .then_inc(S("qe_bd"), 1)
            g.wait_ge(S("silu"), n + 1)
            g4 = gate[:, :, :].rearrange("p a (h d) -> p (a h) d", d=DV)
            g.tensor_tensor(g4, g4, W("norm_w").unsqueeze(1).broadcast_to([P, QT * GH, DV]), ALU.mult)\
             .then_inc(S("gw"), 1)
            g.wait_ge(S("ss"), n + 1)
            g.tensor_tensor(ss[:, :], ss[:, :], C("eps"), ALU.add).then_inc(S("ss_e"), 1)
            g.wait_ge(S("ss_e"), n + 1)
            g.tensor_tensor(rs[:, :], ss[:, :], C("neg_half"), ALU.pow).then_inc(S("rs"), 1)

        def pair(u):
            return 2 * (u % 3)

        def unit(e):
            b, g, hp = e // 4, e // 2 % 2, e % 2
            return b, g, 2 * hp, 4 * g + 2 * hp

        UB = XH // 2
        UX = QB * UB

        def pe_xattn(pe, n, layer):
            pe.wait_ge(S("B_xnT"), n + 1)
            if layer == 0:
                pe.wait_ge(S("ctx_in"), 16 * (n + 1))
                for g in range(XG):
                    w = W("x_q")[:, g * P:(g + 1) * P]
                    pe.matmul(bank(1 + g), w, xnT[:, :], start=True, stop=True).then_inc(S("xq_ps"), 1)
                for g in range(XG):
                    for half in range(2):
                        w = W("x_k")[:, (half * XG + g) * P:(half * XG + g + 1) * P]
                        i = pe.matmul(bank(3 + g), w, ctxT[:, half, :], start=(half == 0), stop=(half == 1))
                    i.then_inc(S("xk_ps"), 1)
                for j in range(QT):
                    o = bank(5)[:, j * P:(j + 1) * P]
                    for half in range(2):
                        pe.matmul(o, ctxT[:, half, j * P:(j + 1) * P], W("x_v")[:, half * P:(half + 1) * P],
                                  start=(half == 0), stop=False)
                    i = pe.matmul(o, C("ones", 1), W("x_vb", 1), start=False, stop=True)
                i.then_inc(S("xv_ps"), 1)
            else:
                for g in range(XG):
                    w = C("sel_q")[:, g * P:(g + 1) * P]
                    pe.matmul(bank(1 + g), w, xnT[:, :], start=True, stop=True).then_inc(S("xq_ps"), 1)

            def before(u):
                if u == 0:
                    pe.wait_ge(S("xqa"), 2 * (n + 1))
                    pe.wait_ge(S("xka"), n + 1)
                elif u == 2:
                    pe.wait_ge(S("xva"), n + 1)
                if u >= 3 and u - 3 < UX:
                    pe.wait_ge(S("mx_read"), UX * n + u - 2)
                elif u >= 3:
                    pe.wait_ge(S("ex_read"), UX * n + u - UX - 2)

            def max_scores(e):
                b, g, j0, _ = unit(e)
                before(e)
                for jj in range(2):
                    r = STRIP * (j0 + jj)
                    for qt in range(2):
                        q0 = b * T + qt * P
                        i = pe.matmul(bank(pair(e) + jj)[:, qt * T:(qt + 1) * T],
                                      qa[r:r + ROW_MAX, g, q0:q0 + P], ka[r:r + ROW_MAX, g, b * T:(b + 1) * T],
                                      start=True, stop=True)
                i.then_inc(S("mx_ps"), 1)

            def exp_scores(e):
                b, g, j0, _ = unit(e)
                before(UX + e)
                if e % UB == 0:
                    pe.wait_ge(S("q_less_max"), QB * n + b + 1)
                for jj in range(2):
                    r = STRIP * (j0 + jj)
                    for kt in range(2):
                        k0 = b * T + kt * P
                        i = pe.matmul(bank(pair(UX + e) + jj)[:, kt * T:(kt + 1) * T],
                                      ka[r:r + ROW_MAX + 1, g, k0:k0 + P],
                                      qa[r:r + ROW_MAX + 1, g, b * T:(b + 1) * T], start=True, stop=True)
                i.then_inc(S("ex_ps"), 1)

            def values(e):
                b, g, j0, h0 = unit(e)
                if e == UB:
                    pe.wait_ge(S("xo"), QB * n + 1)
                pe.wait_ge(S("ex_read"), UX * n + e + 1)
                for jj in range(2):
                    for qt in range(2):
                        o = bank(6)[:, (qt * XH + h0 + jj) * XV:(qt * XH + h0 + jj + 1) * XV]
                        for kt in range(2):
                            c = jj * 512 + kt * T + qt * P
                            i = pe.matmul(o, pT[:, e % 3, c:c + P], vx[:, 2 * b + kt, h0 + jj, :],
                                          start=(e % UB == 0 and jj == 0 and qt == 0 and kt == 0),
                                          stop=(kt == 1), skip_group_check=True)
                i.then_inc(S("pv"), 1)

            for e in range(UX):
                max_scores(e)
            for b in range(QB):
                pe.wait_ge(S("mx_read"), UX * n + UB * (b + 1))
                if b == 1:
                    pe.wait_ge(S("q_less_max"), QB * n + 1)
                for g in range(XG):
                    for qt in range(2):
                        i = pe.transpose(bank(7)[:, (g * 2 + qt) * P:(g * 2 + qt + 1) * P],
                                         nm[:, b, qt, g, :], ident)
                i.then_inc(S("nm_ps"), 1)
            for e in range(UX + 1):
                if e < UX:
                    exp_scores(e)
                if e >= 1:
                    values(e - 1)
            if layer == 0:
                pe.wait_ge(S("xo"), QB * (n + 1))
                for j in range(QT):
                    i = pe.transpose(bank(7)[:, j * P:(j + 1) * P], o_sb[:, j, :], ident)
                i.then_inc(S("xoT_ps"), 1)
                pe.wait_ge(S("xoT"), n + 1)
                for j in range(QT):
                    o = bank(6)[:, j * P:(j + 1) * P]
                    pe.matmul(o, xnT[:, j * P:(j + 1) * P], W("x_out")[:, 0:P], start=True, stop=False)
                    pe.matmul(o, oT[:, j * P:(j + 1) * P], W("x_out")[:, P:2 * P], start=False, stop=False)
                    i = pe.matmul(o, C("ones", 1), W("x_ob", 1), start=False, stop=True)
                i.then_inc(S("xout_ps"), 1)

        def act_xattn(a, n, q, layer):
            if layer == 1:
                a.wait_ge(S("v_in"), 16 * (q + 1))
                a.activation(vx[:, :, :, 0:XD], ctxT[:, 0, :].rearrange("p (a h d) -> p a h d", a=QT, h=XH),
                             ACT.Copy).then_inc(S("xva"), 1)
            for e in range(UX):
                if e >= 3:
                    a.wait_ge(S("pv"), UX * n + e - 2)
                a.wait_ge(S("ex_ps"), UX * n + e + 1)
                p = pair(UX + e)
                a.activation(pT[:, e % 3, :].rearrange("p (a b) -> p a b", a=2), ps[:, p:p + 2, :],
                             ACT.Exp).then_inc(S("ex_read"), 1)
            if layer == 0:
                a.wait_ge(S("xoT_ps"), n + 1)
                a.activation(oT[:, :], bank(7), ACT.Copy).then_inc(S("xoT"), 1)

        def dve_xattn(v, n, q, layer):
            cols = bass.ds(q * QN, QN)
            for g in range(XG):
                v.wait_ge(S("xq_ps"), XG * n + g + 1)
                if layer == 0:
                    v.scalar_tensor_tensor(qa[:, g, :], bank(1 + g), W("x_qb")[:, g:g + 1], mq[:, cols],
                                           ALU.add, ALU.mult).then_inc(S("xqa"), 1)
                else:
                    for b in range(QB):
                        i = v.tensor_scalar(qa[:, g, b * T:(b + 1) * T], bank(1 + g)[:, b * T:(b + 1) * T],
                                            hs[:, bass.ds(q * QB + b, 1)], C("is_bias"), ALU.mult, ALU.add)
                    i.then_inc(S("xqa"), 1)
            if layer == 0:
                for g in range(XG):
                    v.wait_ge(S("xk_ps"), XG * n + g + 1)
                    i = v.scalar_tensor_tensor(ka[:, g, :], bank(3 + g), W("x_kb")[:, g:g + 1],
                                               mask_row[:, cols], ALU.add, ALU.mult)
                i.then_inc(S("xka"), 1)
                v.wait_ge(S("xv_ps"), n + 1)
                m = mask_col[:, bass.ds(q * QT, QT)].unsqueeze(2).unsqueeze(3).broadcast_to([P, QT, XH, XD])
                v.tensor_tensor(vx[:, :, :, 0:XD], bank(5).rearrange("p (a h d) -> p a h d", a=QT, h=XH), m,
                                ALU.mult).then_inc(S("xva"), 1)
            for e in range(UX):
                b, g, j0, _ = unit(e)
                v.wait_ge(S("mx_ps"), UX * n + e + 1)
                p = pair(e)
                out = nm[:, b, :, g, :].rearrange("p t (j s) -> p j t s", s=STRIP)[:, j0:j0 + 2, :, ROW_MAX]
                v.tensor_reduce(out, ps[:, p:p + 2, :].rearrange("p j (t k) -> p j t k", t=2), AX.X, ALU.max,
                                negate=True).then_inc(S("mx_read"), 1)
            for b in range(QB):
                v.wait_ge(S("nm_ps"), QB * n + b + 1)
                v.wait_ge(S("xqa"), XG * (n + 1))
                qb = qa[:, 0:XG, b * T:(b + 1) * T]
                v.tensor_tensor(qb, qb, bank(7).rearrange("p (g t) -> p g t", g=XG), ALU.add)\
                 .then_inc(S("q_less_max"), 1)
            for b in range(QB):
                v.wait_ge(S("pv"), UX * n + UB * (b + 1))
                o4 = bank(6)[:, 0:2 * XH * XV].rearrange("p (t h d) -> p t h d", t=2, h=XH)
                v.reciprocal(rden[:, :, 0:XH], o4[:, :, :, XD]).then_inc(S("xden"), 1)
                v.wait_ge(S("xden"), QB * n + b + 1)
                v.tensor_tensor(o_sb[:, 2 * b:2 * b + 2, :].rearrange("p t (h d) -> p t h d", h=XH),
                                o4[:, :, :, 0:XD],
                                rden[:, :, 0:XH].unsqueeze(3).broadcast_to([P, 2, XH, XD]), ALU.mult)\
                 .then_inc(S("xo"), 1)
            if layer == 0:
                v.wait_ge(S("xout_ps"), n + 1)
                v.tensor_tensor(xq[:, :, :], xq[:, :, :], tri3(bank(6), QT), ALU.add).then_inc(S("x2"), 1)
            else:
                v.wait_ge(S("xo"), QB * (n + 1))
                v.tensor_tensor(xq[:, :, :], xq[:, :, :], o_sb[:, :, :], ALU.add).then_inc(S("x2"), 1)
            v.wait_ge(S("x2"), n + 1)

        def pool_xattn(g, n, q, layer):
            if layer == 0:
                return
            cols = bass.ds(q * QN, QN)
            g.wait_ge(S("k_in"), 16 * (q + 1))
            kq = ka[:, 0:XG, :]
            g.tensor_tensor(kq, kq, mask_row[:, cols].unsqueeze(1).broadcast_to([P, XG, QN]), ALU.add)\
             .then_inc(S("xka"), 1)

        MU = MH // 2
        MX = QB * MU

        def pe_mla(pe, n):
            pe.wait_ge(S("A_xnT"), n + QUADS + 1)
            pe.matmul(bank(1), W("m_lat"), xnT[:, :], start=True, stop=True).then_inc(S("lat_ps"), 1)
            pe.wait_ge(S("lat"), n + 1)
            pe.matmul(bank(2), W("m_qr", ML), lat[0:ML, :], start=True, stop=True).then_inc(S("qr_ps"), 1)
            kb, qb = (3, 4, 6, 7), (0, 1, 2, 3)
            for g in range(MG):
                pe.matmul(bank(kb[g]), W("m_k")[:, g * P:(g + 1) * P], lat[:, :], start=True, stop=True)\
                  .then_inc(S("mk_ps"), 1)
            for j in range(QT):
                i = pe.matmul(bank(5)[:, j * P:(j + 1) * P], lat[:, j * P:(j + 1) * P], W("m_v"),
                              start=True, stop=True)
            i.then_inc(S("mv_ps"), 1)
            pe.wait_ge(S("tq"), n + 1)
            for g in range(MG):
                if g == MG - 1:
                    pe.wait_ge(S("mka"), MG * n + 1)
                pe.matmul(bank(qb[g]), W("m_q", ML)[:, g * P:(g + 1) * P], lat[0:ML, :], start=True, stop=False)
                pe.matmul(bank(qb[g]), C("sel_rope")[:, g * P:(g + 1) * P], tq[:, :], start=False, stop=True)\
                  .then_inc(S("mq_ps"), 1)

            def scores(u):
                b, hp = u // MU, u % MU
                if u == 0:
                    pe.wait_ge(S("mqa"), MG * (n + 1))
                    pe.wait_ge(S("mka"), MG * (n + 1))
                    pe.wait_ge(S("mva"), n + 1)
                if u >= 3:
                    pe.wait_ge(S("ms_read"), MX * n + u - 2)
                for jj in range(2):
                    r, g = STRIP * (2 * (hp % 2) + jj), hp // 2
                    o = bank(pair(u) + jj)
                    k, qq = ka[r:r + MD + MR, g, :], qa[r:r + MD + MR, g, :]
                    pe.matmul(o[:, 0:T], k[:, b * T:b * T + P], qq[:, b * T:(b + 1) * T], start=True, stop=True)
                    i = pe.matmul(o[:, T:T + P], k[:, b * T + P:(b + 1) * T], qq[:, b * T + P:(b + 1) * T],
                                  start=True, stop=True)
                i.then_inc(S("ms_ps"), 1)

            def values(u):
                b, hp = u // MU, u % MU
                if u == MU:
                    pe.wait_ge(S("mo"), QB * n + 1)
                pe.wait_ge(S("mp"), MX * n + u + 1)
                for jj in range(2):
                    h = 2 * hp + jj
                    for qt, kt, c in ((0, 0, 0), (1, 0, P), (1, 1, 2 * P)):
                        o = bank(6)[:, (qt * MH + h) * MV:(qt * MH + h + 1) * MV]
                        c += jj * 512
                        i = pe.matmul(o, pT[:, u % 3, c:c + P], vm[:, 2 * b + kt, h, :],
                                      start=(u % MU == 0 and jj == 0 and qt == 0), stop=(qt == kt),
                                      skip_group_check=True)
                i.then_inc(S("mpv"), 1)

            for u in range(MX + 2):
                if u < MX:
                    scores(u)
                if u >= 2:
                    values(u - 2)
            pe.wait_ge(S("mo"), QB * (n + 1))
            for j in range(QT):
                i = pe.transpose(bank(7)[:, j * P:(j + 1) * P], o_sb[:, j, :], ident)
            i.then_inc(S("moT_ps"), 1)
            pe.wait_ge(S("moT"), n + 1)
            for j in range(QT):
                i = pe.matmul(bank(6)[:, j * P:(j + 1) * P], oT[:, j * P:(j + 1) * P], W("m_o"),
                              start=True, stop=True)
            i.then_inc(S("mout_ps"), 1)

        def act_mla(a, n):
            kb = (3, 4, 6, 7)
            for g in range(MG):
                a.wait_ge(S("mk_ps"), MG * n + g + 1)
                a.activation(ka[:, g, :], bank(kb[g]), ACT.Copy).then_inc(S("mka"), 1)
            a.wait_ge(S("mv_ps"), n + 1)
            a.activation(vm[:, :, :, 0:MD], bank(5).rearrange("p (a h d) -> p a h d", a=QT, h=MH),
                         ACT.Copy).then_inc(S("mva"), 1)
            for u in range(MX):
                if u >= 3:
                    a.wait_ge(S("mpv"), MX * n + u - 2)
                a.wait_ge(S("ms_read"), MX * n + u + 1)
                view = [t.rearrange("p (a b) -> p a b", a=2)[:, :, 0:3 * P] for t in (pT[:, u % 3, :], cl[:, u % 2, :])]
                a.activation(view[0], view[1], ACT.Exp, scale=float(MD + MR) ** -0.5).then_inc(S("mp"), 1)
            a.wait_ge(S("moT_ps"), n + 1)
            a.activation(oT[:, :], bank(7), ACT.Copy).then_inc(S("moT"), 1)

        def dve_mla(v, n):
            v.wait_ge(S("lat_ps"), n + 1)

            def rope(name):
                return C(name).unsqueeze(1).broadcast_to([P, QB, T])

            v.tensor_tensor(tri3(lat[:, :], QB), tri3(bank(1), QB), rope("lat_rope"), ALU.mult)\
             .then_inc(S("lat"), 1)
            v.wait_ge(S("qr_ps"), n + 1)
            v.tensor_tensor(tri3(tq[:, :], QB), tri3(bank(2), QB), rope("q_rope"), ALU.mult)\
             .then_inc(S("tq"), 1)
            for g in range(MG):
                v.wait_ge(S("mq_ps"), MG * n + g + 1)
                v.tensor_copy(qa[:, g, :], bank((0, 1, 2, 3)[g])).then_inc(S("mqa"), 1)

            def normalise(b):
                v.wait_ge(S("mpv"), MX * n + MU * (b + 1))
                o4 = bank(6)[:, 0:2 * MH * MV].rearrange("p (t h d) -> p t h d", t=2, h=MH)
                v.reciprocal(rden[:, :, :], o4[:, :, :, MD]).then_inc(S("mden"), 1)
                v.wait_ge(S("mden"), QB * n + b + 1)
                v.tensor_tensor(o_sb[:, 2 * b:2 * b + 2, :].rearrange("p t (h d) -> p t h d", h=MH),
                                o4[:, :, :, 0:MD],
                                rden[:, :, :].unsqueeze(3).broadcast_to([P, 2, MH, MD]), ALU.mult)\
                 .then_inc(S("mo"), 1)

            for u in range(MX):
                if u >= 2:
                    v.wait_ge(S("mp"), MX * n + u - 1)
                v.wait_ge(S("ms_ps"), MX * n + u + 1)
                p = pair(u)
                blocks = ps[:, p:p + 2, :].rearrange("p a (b c) -> p (a b) c", c=P)
                out = cl[:, u % 2, :].rearrange("p (a c) -> p a c", c=P)
                v.scalar_tensor_tensor(out[:, 0:8:2, :], blocks[:, 0:8:2, :], -CLIP,
                                       C("clip_mask").unsqueeze(1).broadcast_to([P, 4, P]), ALU.max, ALU.min)
                v.tensor_scalar(out[:, 1:8:4, :], blocks[:, 1:8:4, :], -CLIP, CLIP, ALU.max, ALU.min)\
                 .then_inc(S("ms_read"), 1)
                if u == MU + 2:
                    normalise(0)
            normalise(1)
            v.wait_ge(S("mout_ps"), n + 1)
            v.tensor_tensor(xq[:, :, :], xq[:, :, :], tri3(bank(6), QT), ALU.add).then_inc(S("x3"), 1)
            v.wait_ge(S("x3"), n + 1)

        def pe_router(pe, n, layer):
            pe.wait_ge(S("C_xnT"), n + 1)
            for j in range(QT):
                i = pe.matmul(bank(1)[:, j * EXP:(j + 1) * EXP], xnT[:, j * P:(j + 1) * P],
                              W("r%d_w" % layer), start=True, stop=True)
            i.then_inc(S("lg_ps"), 1)

        def dve_router(v, n, q, layer):
            tiles = bass.ds(q * QT, QT)
            v.wait_ge(S("lg_ps"), n + 1)
            v.tensor_tensor(lg[:, tiles, :], bank(1)[:, 0:QT * EXP].rearrange("p (a e) -> p a e", a=QT),
                            W("r%d_b" % layer).unsqueeze(1).broadcast_to([P, QT, EXP]), ALU.add)\
             .then_inc(S("lg"), 1)
            v.tensor_copy(x_all[:, tiles, :], xq[:, :, :]).then_inc(S("x_saved"), 1)
            v.wait_ge(S("xn_saved"), n + 1)

        def act_router(a, n, q):
            a.wait_ge(S("C_xn"), QT * (n + 1))
            a.activation(xn_all[:, bass.ds(q * QT, QT), :], xn[:, :, :], ACT.Copy).then_inc(S("xn_saved"), 1)

        def pe_sort(pe, layer):
            pe.wait_ge(S("onehot"), layer + 1)
            oh = onehot[:, :, :].rearrange("p t e -> p (t e)")
            pe.matmul(bank(0)[:, 0:P], C("tri"), oh, start=True, stop=True)
            pe.matmul(bank(1)[:, 0:P], C("ones"), oh, start=True, stop=True).then_inc(S("rank_ps"), 1)

        def act_sort(a, layer):
            a.wait_ge(S("lless"), layer + 1)
            a.activation(lex[:, :, :], lg[:, :, :], ACT.Exp).then_inc(S("lex"), 1)

        def dve_sort(v, layer):
            step = [0]

            def done(i):
                step[0] += 1
                i.then_inc(S("sort%d" % layer), 1)
                v.wait_ge(S("sort%d" % layer), step[0])

            def over(ap, shape, axis):
                return ap.unsqueeze(axis).broadcast_to(shape)

            te = [P, TILES, EXP]
            v.wait_ge(S("lg"), QUADS * (layer + 1))
            done(v.tensor_reduce(lmax[:, :], lg[:, :, :], AX.X, ALU.max))
            v.tensor_tensor(lg[:, :, :], lg[:, :, :], over(lmax[:, :], te, 2), ALU.subtract)\
             .then_inc(S("lless"), 1)
            v.wait_ge(S("lless"), layer + 1)
            done(v.scalar_tensor_tensor(tie[:, :, :],
                                        lg[:, :, :], 0.0, over(C("iota8m"), te, 1), ALU.is_equal, ALU.mult))
            done(v.tensor_reduce(amin[:, :], tie[:, :, :],
                                 AX.X, ALU.min))
            v.tensor_tensor(onehot[:, :, :], over(C("iota8m"), te, 1), over(amin[:, :], te, 2), ALU.is_equal)\
             .then_inc(S("onehot"), 1)
            v.wait_ge(S("lex"), layer + 1)
            done(v.tensor_reduce(lsum[:, :], lex[:, :, :], AX.X, ALU.add))
            done(v.reciprocal(prob[:, :], lsum[:, :]))
            v.wait_ge(S("rank_ps"), layer + 1)
            done(v.tensor_copy(cnt[:, :, :], bank(1)[:, 0:P].rearrange("p (t e) -> p e t", e=EXP)))
            flat = [t[:, :, :].rearrange("p e t -> p (e t)") for t in (incl, cnt)]
            done(v.tensor_tensor_scan(flat[0], C("scan_reset"), flat[1], 0.0, ALU.mult, ALU.add))
            total = incl[:, :, TILES - 1]
            et = [P, EXP, TILES]
            done(v.tensor_tensor(more[:, :, :], over(total, et, 2), over(C("tile_starts"), et, 1), ALU.is_gt))
            done(v.tensor_reduce(ntile[:, :], more[:, :, :], AX.X, ALU.add))
            done(v.tensor_tensor_scan(ends[:, :], C("ones")[:, 0:EXP], ntile[:, :], 0.0, ALU.mult, ALU.add))
            done(v.tensor_tensor(starts[:, :], ends[:, :], ntile[:, :], ALU.subtract))
            done(v.tensor_tensor(incl[:, :, :], incl[:, :, :], cnt[:, :, :], ALU.subtract))
            done(v.scalar_tensor_tensor(incl[:, :, :], over(starts[:, :], et, 2), float(P), incl[:, :, :],
                                        ALU.mult, ALU.add))
            et_t = incl[:, :, :].rearrange("p e t -> p t e")
            done(v.tensor_tensor(lex[:, :, :], bank(0)[:, 0:P].rearrange("p (t e) -> p t e", e=EXP), et_t, ALU.add))
            done(v.tensor_tensor(lex[:, :, :], lex[:, :, :], onehot[:, :, :], ALU.mult))
            done(v.tensor_reduce(pos_f[:, :], lex[:, :, :], AX.X, ALU.add))
            v.tensor_copy(pos[:, :], pos_f[:, :]).then_inc(S("pos"), 1)
            if layer == 0:
                v.memset(slot_f[:, :], 0.0).then_inc(S("ys"), 2)
                v.wait_ge(S("ys"), 2)
            se = [P, SLOTS, EXP]
            done(v.tensor_tensor(slot_ge[:, :, :], over(C("slot_iota"), se, 2), over(ends[:, :], se, 1), ALU.is_ge))
            done(v.tensor_reduce(slot_f[:, :], slot_ge[:, :, :], AX.X, ALU.add))
            if layer == 0:
                for s in range(2):
                    v.memset(ys[:, s, :], 0.0).then_inc(S("y_out%d" % s), 16)
            v.tensor_scalar(slot_e[:, :], slot_f[:, :], float(EXP - 1), None, ALU.min).then_inc(S("slots"), 1)

        TURNS = SLOTS // 2

        def pool_scatter(g, layer):
            g.wait_ge(S("pos"), layer + 1)
            g.wait_ge(S("xn_saved"), QUADS * (layer + 1))
            g.wait_ge(S("zeroed"), 16)
            for t in range(TILES):
                g.indirect_dma_start(A["sorted_x"], bass.IndirectOffsetOnAxis(ap=pos[:, t:t + 1], axis=0),
                                     xn_all[:, t, :], None).then_inc(S("scattered"), 16)

        def pool_gather(g, layer):
            for s in range(2):
                g.wait_ge(S("y_out%d" % s), 16 * ((layer + 1) * TURNS + 1))
            for t in range(TILES):
                g.indirect_dma_start(xn_all[:, t, :], None, A["sorted_y"],
                                     bass.IndirectOffsetOnAxis(ap=pos[:, t:t + 1], axis=0))\
                 .then_inc(S("gathered"), 16)

        def sp_experts(sp, layer):
            sp.wait_ge(S("scattered"), 16 * TILES * (layer + 1))
            for s in range(2):
                sp.dma_start(xs[:, s, :], A["sorted_x"][s * P:(s + 1) * P, :]).then_inc(S("xs_in%d" % s), 16)
            with sp.Fori(0, TURNS - 1) as i:
                n = i + layer * TURNS
                for s in range(2):
                    sp.wait_ge(S("xsT_ps"), 2 * n + s + 1)
                    sp.dma_start(xs[:, s, :], A["sorted_x"][bass.ds((i * 2 + 2 + s) * P, P), :])\
                      .then_inc(S("xs_in%d" % s), 16)
                for s in range(2):
                    sp.wait_ge(S("ys"), 2 * n + s + 3)
                    sp.dma_start(A["sorted_y"][bass.ds((i * 2 + s) * P, P), :], ys[:, s, :])\
                      .then_inc(S("y_out%d" % s), 16)
            for s in range(2):
                sp.wait_ge(S("ys"), 2 * TURNS * (layer + 1) + 1 + s)
                sp.dma_start(A["sorted_y"][(SLOTS - 2 + s) * P:(SLOTS - 1 + s) * P, :], ys[:, s, :])\
                  .then_inc(S("y_out%d" % s), 16)

        def pe_experts(pe, layer):
            pe.wait_ge(S("slots"), layer + 1)
            pe.wait_ge(S("w_in"), 32 * (layer + 1))
            with pe.Fori(0, TURNS) as i:
                n = i + layer * TURNS
                es = [pe.value_load(slot_e[0:1, bass.ds(i * 2 + s, 1)], min_val=0, max_val=EXP - 1)
                      for s in range(2)]
                for s in range(2):
                    pe.wait_ge(S("ys"), 2 * n + s + 1)
                    pe.wait_ge(S("xs_in%d" % s), 16 * (n + 1))
                    pe.transpose(bank(4 * s)[:, 0:P], xs[:, s, :], ident).then_inc(S("xsT_ps"), 1)
                for s in range(2):
                    pe.wait_ge(S("xsT"), 2 * n + s + 1)
                    if layer == 0:
                        for half in range(2):
                            k = pe.matmul(bank(4 * s + 1 + half), xsT[:, s, :],
                                          w1[:, bass.ds(es[s] * (2 * F) + half * F, F)], start=True, stop=True)
                    else:
                        k = pe.matmul(bank(4 * s + 1), xsT[:, s, :], w1b[:, bass.ds(es[s] * F, F)],
                                      start=True, stop=True)
                    k.then_inc(S("h_ps"), 1)
                for s in range(2):
                    pe.wait_ge(S("hid"), 2 * n + s + 1)
                    for j in range(4):
                        k = pe.transpose(bank(4 * s + 3)[:, j * P:(j + 1) * P], hid[:, s, j * P:(j + 1) * P], ident)
                    k.then_inc(S("hT_ps"), 1)
                for s in range(2):
                    pe.wait_ge(S("hidT"), 2 * n + s + 1)
                    wsrc = w2 if layer == 0 else w2b
                    for j in range(4):
                        k = pe.matmul(bank(4 * s)[:, 0:D], hidT[:, s, j * P:(j + 1) * P],
                                      wsrc[:, bass.ds(es[s] * (4 * D) + j * D, D)], start=(j == 0), stop=(j == 3))
                    k.then_inc(S("y_ps"), 1)

        def act_experts(a, layer):
            a.wait_ge(S("slots"), layer + 1)
            with a.Fori(0, TURNS) as i:
                n = i + layer * TURNS
                if layer == 1:
                    es = [a.value_load(slot_e[0:1, bass.ds(i * 2 + s, 1)], min_val=0, max_val=EXP - 1)
                          for s in range(2)]
                for s in range(2):
                    a.wait_ge(S("xsT_ps"), 2 * n + s + 1)
                    a.activation(xsT[:, s, :], bank(4 * s)[:, 0:P], ACT.Copy).then_inc(S("xsT"), 1)
                for s in range(2):
                    a.wait_ge(S("h_ps"), 2 * n + s + 1)
                    if layer == 0:
                        a.activation(act_a[:, s, :], bank(4 * s + 1), ACT.Silu).then_inc(S("silu_a"), 1)
                    else:
                        a.activation(hid[:, s, :], bank(4 * s + 1), ACT.Copy).then_inc(S("hid"), 1)
                for s in range(2):
                    a.wait_ge(S("hT_ps"), 2 * n + s + 1)
                    if layer == 0:
                        a.activation(hidT[:, s, :], bank(4 * s + 3), ACT.Copy).then_inc(S("hidT"), 1)
                    else:
                        for j in range(4):
                            k = a.activation(hidT[:, s, j * P:(j + 1) * P], bank(4 * s + 3)[:, j * P:(j + 1) * P],
                                             ACT.Relu, bias=W("b1")[:, bass.ds(es[s] * 4 + j, 1)])
                        k.then_inc(S("hidT"), 1)

        def dve_experts(v, layer):
            v.wait_ge(S("slots"), layer + 1)
            with v.Fori(0, TURNS) as i:
                n = i + layer * TURNS
                if layer == 1:
                    es = [v.value_load(slot_e[0:1, bass.ds(i * 2 + s, 1)], min_val=0, max_val=EXP - 1)
                          for s in range(2)]
                if layer == 0:
                    for s in range(2):
                        v.wait_ge(S("silu_a"), 2 * n + s + 1)
                        v.tensor_tensor(hid[:, s, :], bank(4 * s + 2), act_a[:, s, :], ALU.mult)\
                         .then_inc(S("hid"), 1)
                for s in range(2):
                    v.wait_ge(S("y_ps"), 2 * n + s + 1)
                    v.wait_ge(S("y_out%d" % s), 16 * (n + 1))
                    if layer == 0:
                        v.tensor_copy(ys[:, s, :], bank(4 * s)[:, 0:D]).then_inc(S("ys"), 1)
                    else:
                        v.tensor_tensor(ys[:, s, :], bank(4 * s)[:, 0:D], W("b2")[:, bass.ds(es[s] * D, D)],
                                        ALU.add).then_inc(S("ys"), 1)

        def dve_combine(v, q, layer):
            tiles = bass.ds(q * QT, QT)
            y = xn_all[:, tiles, :]
            p = prob[:, tiles].unsqueeze(2).broadcast_to([P, QT, D])
            v.wait_ge(S("gathered"), 16 * TILES * (layer + 1))
            if layer == 0:
                v.wait_ge(S("x_saved"), QUADS + q)
            v.tensor_tensor(y, y, p, ALU.mult).then_inc(S("yp"), 1)
            v.wait_ge(S("yp"), q + layer * QUADS + 1)
            out = xq[:, :, :] if layer == 0 else x_all[:, tiles, :]
            v.tensor_tensor(out, y, x_all[:, tiles, :], ALU.add).then_inc(S("x_next"), 1)

        @block.sync
        def _(sp):
            sp.dma_start(cst[:, :], A["consts"]).then_inc(S("consts_in"), 16)
            sp.dma_start(wts[:, :], A["weights"]).then_inc(S("weights_in"), 16)
            sp.dma_start(xq[:, :, :], A["x"][:, 0:QT, :]).then_inc(S("x_in"), 16)
            sp.dma_start(mask_row[:, :], A["mask"].broadcast_to([P, B * T])).then_inc(S("mask_in"), 16)
            sp.dma_start(mask_col[:, :], A["mask_col"]).then_inc(S("mask_in"), 16)
            sp.dma_start(ctxT[:, :, :], A["ctxT"][:, :, 0:QN]).then_inc(S("ctx_in"), 16)
            sp.wait_ge(S("zeros"), 1)
            sp.dma_start(A["sorted_x"].rearrange("(s p) d -> p s d", p=P),
                         zeros[:, :].unsqueeze(1).broadcast_to([P, SLOTS, D])).then_inc(S("zeroed"), 16)
            sp.dma_start(w1[:, :], A["w1_0"]).then_inc(S("w_in"), 16)
            sp.dma_start(w2[:, :], A["w2_0"]).then_inc(S("w_in"), 16)
            with sp.Fori(0, QUADS - 1) as q:
                sp.wait_ge(S("xv_ps"), q + 1)
                sp.dma_start(ctxT[:, :, :], A["ctxT"][:, :, bass.ds((q + 1) * QN, QN)]).then_inc(S("ctx_in"), 16)
                sp.wait_ge(S("x_saved"), q + 1)
                sp.dma_start(xq[:, :, :], A["x"][:, bass.ds((q + 1) * QT, QT), :]).then_inc(S("x_in"), 16)
            sp.wait_ge(S("x_saved"), QUADS)
            sp.dma_start(mask_i[:, :],
                         A["mask_i"].broadcast_to([P, B * T])).then_inc(S("mask_in"), 16)
            sp_experts(sp, 0)
            sp.wait_ge(S("y_ps"), SLOTS)
            sp.dma_start(w1b, A["w1_1"]).then_inc(S("w_in"), 16)
            sp.dma_start(w2b, A["w2_1"]).then_inc(S("w_in"), 16)
            with sp.Fori(0, QUADS) as q:
                sp.wait_ge(S("xva"), QUADS + q)
                sp.dma_start(ctxT[:, 0, :].rearrange("p (a d) -> p a d", a=QT),
                             A["ctxv"][:, bass.ds(q * QT, QT), :]).then_inc(S("v_in"), 16)
                sp.wait_ge(S("ms_ps"), MX * (q + 1))
                sp.dma_start(ka[:, 0:XG, :], A["kpad"][:, :, bass.ds(q * QN, QN)]).then_inc(S("k_in"), 16)
            sp_experts(sp, 1)
            with sp.Fori(0, QUADS) as q:
                sp.wait_ge(S("x_next"), QUADS + q + 1)
                sp.dma_start(A["out"][:, bass.ds(q * QT, QT), :], x_all[:, bass.ds(q * QT, QT), :]).then_inc(S("out_written"), 16)
            sp.wait_ge(S("out_written"), 16 * QUADS)

        @block.gpsimd
        def _(g):
            g.memset(zeros[:, :], 0.0).then_inc(S("zeros"), 1)
            g.memset(nm[:, :, :, :, :], 0.0).then_inc(S("filled"), 1)
            g.memset(vx[:, :, :, :], 1.0).then_inc(S("filled"), 1)
            g.memset(vm[:, :, :, :], 1.0).then_inc(S("filled"), 1)
            g.wait_ge(S("consts_in"), 16)
            g.wait_ge(S("weights_in"), 16)
            with g.Fori(0, QUADS) as q:
                pool_ln(g, "A_", q)
                pool_gla(g, q)
                pool_ln(g, "B_", q)
                pool_ln(g, "C_", q)
            pool_scatter(g, 0)
            pool_gather(g, 0)
            g.wait_ge(S("mask1"), 6)
            with g.Fori(0, QUADS) as q:
                n = q + QUADS
                pool_ln(g, "A_", n)
                pool_xattn(g, n, q, 1)
                pool_ln(g, "B_", n)
                pool_ln(g, "C_", n)
            pool_scatter(g, 1)
            pool_gather(g, 1)

        @block.scalar
        def _(a):
            a.wait_ge(S("consts_in"), 16)
            a.wait_ge(S("weights_in"), 16)
            with a.Fori(0, QUADS) as q:
                act_ln(a, "A_", q, 0)
                act_gla(a, q)
                act_ln(a, "B_", q, 0)
                act_xattn(a, q, q, 0)
                act_ln(a, "C_", q, 0)
                act_router(a, q, q)
            act_sort(a, 0)
            act_experts(a, 0)
            with a.Fori(0, QUADS) as q:
                n = q + QUADS
                act_ln(a, "A_", n, 0)
                act_mla(a, q)
                act_ln(a, "B_", n, 0)
                act_xattn(a, n, q, 1)
                act_ln(a, "C_", n, 0)
                act_router(a, n, q)
            act_sort(a, 1)
            act_experts(a, 1)

        @block.tensor
        def _(pe):
            pe.wait_ge(S("consts_in"), 16)
            pe.wait_ge(S("weights_in"), 16)
            with pe.Fori(0, QUADS) as q:
                pe_ln(pe, "A_", q, 0)
                pe_gla(pe, q)
                pe_ln(pe, "B_", q, 0)
                pe_xattn(pe, q, 0)
                pe_ln(pe, "C_", q, 0)
                pe_router(pe, q, 0)
            pe_sort(pe, 0)
            pe_experts(pe, 0)
            with pe.Fori(0, QUADS) as q:
                n = q + QUADS
                pe_ln(pe, "A_", n, 0)
                pe_mla(pe, q)
                pe_ln(pe, "B_", n, 0)
                pe_xattn(pe, n, 1)
                pe_ln(pe, "C_", n, 0)
                pe_router(pe, n, 1)
            pe_sort(pe, 1)
            pe_experts(pe, 1)

        @block.vector
        def _(v):
            v.wait_ge(S("filled"), 3)
            v.wait_ge(S("consts_in"), 16)
            v.wait_ge(S("weights_in"), 16)
            v.wait_ge(S("mask_in"), 32)
            v.tensor_scalar(mq[:, :], mask_row[:, :], C("mq_a"), C("mq_b"), ALU.mult, ALU.add)
            v.tensor_scalar(mask_row[:, :], mask_row[:, :], C("mk_a"), C("mk_b"), ALU.mult, ALU.add)\
             .then_inc(S("factors"), 1)
            v.wait_ge(S("factors"), 1)
            with v.Fori(0, QUADS) as q:
                v.wait_ge(S("x_in"), (q + 1) * 16)
                dve_ln(v, "A_", q)
                dve_gla(v, q)
                dve_ln(v, "B_", q)
                dve_xattn(v, q, q, 0)
                dve_ln(v, "C_", q)
                dve_router(v, q, q, 0)
            dve_sort(v, 0)
            v.wait_ge(S("mask_in"), 48)
            v.tensor_copy(mq[:, :], mask_i[:, :]).then_inc(S("mask1"), 1)
            v.wait_ge(S("mask1"), 1)
            m3 = mq[:, :].rearrange("p (b t) -> p b t", b=B)
            v.tensor_reduce(has[:, :], m3, AX.X, ALU.max).then_inc(S("mask1"), 1)
            v.tensor_scalar(c1[:, :], W("x1_b"), C("is_bias"), C("is_max"), ALU.mult, ALU.add)
            v.wait_ge(S("mask1"), 2)
            v.tensor_scalar(nothas[:, :], has[:, :], -1.0, 1.0, ALU.mult, ALU.add)
            v.tensor_scalar(hs[:, :], has[:, :], float(XD) ** -0.5, None, ALU.mult).then_inc(S("mask1"), 1)
            v.wait_ge(S("mask1"), 3)
            v.tensor_tensor(m3, m3, nothas[:, :].unsqueeze(2).broadcast_to([P, B, T]), ALU.max)\
             .then_inc(S("mask1"), 1)
            v.wait_ge(S("mask1"), 4)
            v.tensor_scalar(mq[:, :], mq[:, :], 1.0, C("bias_big"), ALU.subtract, ALU.mult)\
             .then_inc(S("mask1"), 1)
            v.wait_ge(S("mask1"), 5)
            v.tensor_scalar(mask_row[:, :], mq[:, :], c1[:, 0:1], None, ALU.add).then_inc(S("mask1"), 1)
            dve_experts(v, 0)
            with v.Fori(0, QUADS) as q:
                n = q + QUADS
                dve_combine(v, q, 0)
                v.wait_ge(S("x_next"), q + 1)
                dve_ln(v, "A_", n)
                dve_mla(v, q)
                dve_ln(v, "B_", n)
                dve_xattn(v, n, q, 1)
                dve_ln(v, "C_", n)
                dve_router(v, n, q, 1)
            dve_sort(v, 1)
            dve_experts(v, 1)
            with v.Fori(0, QUADS) as q:
                dve_combine(v, q, 1)


def constants():
    c = np.zeros((P, CN), np.float32)

    def put(name, a, r0=0):
        at, n = CC[name]
        a = np.asarray(a, np.float32)
        c[r0:r0 + a.shape[0], at:at + n] = a.reshape(a.shape[0], n)

    p = np.arange(P)
    put("ident", np.eye(P))
    put("chunk_mask", (p[:, None] <= p[None]) & (p[:, None] // CHUNK == p[None] // CHUNK))
    put("tri", p[:, None] < p[None])
    put("ones", np.ones((P, P)))
    k = np.arange(64)
    put("head_mask", k[:, None] // DK == np.arange(GH)[None])
    put("block_mask", k[:, None] // DK == (p // DV)[None])
    put("reset", np.broadcast_to(np.arange(QN) % CHUNK != 0, (64, QN)))
    lim = np.where(p[:, None] <= p[None], CLIP, -BIG)
    put("clip_mask", lim)
    inv = (np.float32(10000.0) ** (-np.arange(0, MR, 2, dtype=np.float32) / MR)).astype(np.float32)
    ang = np.arange(T, dtype=np.float32)[None] * inv[:, None]
    cos, sin = np.cos(ang).astype(np.float32), np.sin(ang).astype(np.float32)
    r = np.arange(MR)
    cos4, sin4 = cos[r // 2], sin[r // 2] * np.where(r % 2 == 0, -1.0, 1.0)[:, None]
    lat = np.zeros((P, T), np.float32)
    lat[0:64] = 1.0
    lat[64:64 + MR], lat[96:96 + MR] = cos4, sin4
    put("lat_rope", lat)
    put("q_rope", np.concatenate([np.tile(cos4, (MH, 1)), np.tile(sin4, (MH, 1))]))
    sel = np.zeros((P, XG, P), np.float32)
    for h in range(XH):
        for d in range(XD):
            sel[h * XD + d, h // 4, STRIP * (h % 4) + d] = 1.0
    put("sel_q", sel)
    sel = np.zeros((P, MG, P), np.float32)
    for h in range(MH):
        for d in range(MR):
            for half in range(2):
                sel[64 * half + h * MR + d, h // 4, STRIP * (h % 4) + MD + d] = 1.0
    put("sel_rope", sel)
    e = np.arange(EXP)
    put("iota8", np.broadcast_to(e, (P, EXP)))
    put("iota8m", np.broadcast_to(e - EXP, (P, EXP)))
    put("slot_iota", np.broadcast_to(np.arange(SLOTS), (P, SLOTS)))
    put("scan_reset", np.broadcast_to(np.arange(P) % TILES != 0, (P, P)))
    put("neg_half", np.full((P, 32), -0.5))
    put("eps", np.full((P, 32), EPS))
    row = (p % STRIP)[:, None]
    real, bias, most = row < XD, row == ROW_BIAS, row == ROW_MAX
    put("mq_a", XD ** -0.5 * real)
    put("mq_b", bias)
    put("mk_a", real | bias)
    put("mk_b", 1.0 * most - bias)
    put("tile_starts", np.broadcast_to(P * np.arange(TILES), (P, TILES)))
    put("is_bias", row == ROW_BIAS)
    put("is_max", row == ROW_MAX)
    put("bias_big", BIG * (row == ROW_BIAS))
    return c


def weights(I):
    w = np.zeros((P, WN), np.float32)

    def put(name, a):
        at, n = WC[name]
        w[0:a.shape[0], at:at + n] = a.reshape(a.shape[0], n)

    def strips(m, heads, size, rows=P, r0=0):
        out = np.zeros((rows, heads // 4, 4, STRIP), np.float32)
        out[r0:r0 + m.shape[0], :, :, 0:size] = m.reshape(m.shape[0], heads // 4, 4, size)
        return out.reshape(rows, heads // 4, P)

    def strip_col(v, heads, size, bias, most):
        out = np.zeros((4, STRIP, heads // 4), np.float32)
        out[:, ROW_BIAS], out[:, ROW_MAX] = bias, most
        out[:, 0:size] = v.reshape(heads // 4, 4, size).transpose(1, 2, 0)
        return out.reshape(P, heads // 4)

    swap = np.arange(MR) ^ 1
    put("wq", I["L0_attn_Wq"])
    put("wk", I["L0_attn_Wk"])
    put("wv", I["L0_attn_Wv"])
    put("wg", I["L0_attn_Wg"])
    put("wgk1", I["L0_attn_Wgk1"])
    put("wgk2", I["L0_attn_Wgk2"])
    put("bgk", I["L0_attn_bgk2"][:, None])
    put("norm_w", np.broadcast_to(I["L0_attn_norm_w"], (P, DV)))
    put("wo", I["L0_attn_Wo"])
    put("x_q", strips(I["L0_xattn_W_tgt"].T, XH, XD))
    src = I["L0_xattn_W_src"]
    kt = src[0:D].T
    put("x_k", np.stack([strips(kt[0:P], XH, XD), strips(kt[P:], XH, XD)], 1))
    put("x_v", np.stack([src[D:].T[0:P], src[D:].T[P:]], 1))
    put("x_qb", strip_col(I["L0_xattn_b_tgt"], XH, XD, 1.0, 0.0))
    put("x_kb", strip_col(I["L0_xattn_b_src"][0:D], XH, XD, BIG, 1.0))
    put("x_vb", I["L0_xattn_b_src"][None, D:])
    wo = I["L0_xattn_W_out"].T
    put("x_out", np.stack([wo[0:P], wo[P:]], 1))
    put("x_ob", I["L0_xattn_b_out"][None])
    put("r0_w", I["L0_ffn_router_w"])
    put("r0_b", np.broadcast_to(I["L0_ffn_router_b"], (P, EXP)))
    m = np.zeros((P, P), np.float32)
    m[:, 0:ML], m[:, ML:2 * ML] = I["L1_attn_W_DQ"], I["L1_attn_W_DKV"]
    m[:, 64:64 + MR], m[:, 96:96 + MR] = I["L1_attn_W_KR"], I["L1_attn_W_KR"][:, swap]
    put("m_lat", m)
    qr = I["L1_attn_W_QR"].reshape(ML, MH, MR)
    put("m_qr", np.concatenate([qr.reshape(ML, -1), qr[:, :, swap].reshape(ML, -1)], 1))
    put("m_q", strips(I["L1_attn_W_UQ"], MH, MD))
    mk = strips(I["L1_attn_W_UK"], MH, MD, r0=ML).reshape(P, MG, 4, STRIP)
    for d in range(MR):
        mk[64 + d, :, :, MD + d] = 1.0
        mk[96 + d, :, :, MD + d] = 1.0
    put("m_k", mk)
    m = np.zeros((P, P), np.float32)
    m[ML:2 * ML] = I["L1_attn_W_UV"]
    put("m_v", m)
    put("m_o", I["L1_attn_W_O"])
    put("x1_b", np.broadcast_to(I["L1_xattn_b"], (P, 1)))
    put("r1_w", I["L1_ffn_w_gate"])
    put("r1_b", np.broadcast_to(I["L1_ffn_b_gate"], (P, EXP)))
    put("b1", I["L1_ffn_b1"].reshape(EXP, 4, P).transpose(2, 0, 1))
    put("b2", np.broadcast_to(I["L1_ffn_b2"].reshape(1, -1), (P, EXP * D)))
    return w


def kernel(**inputs):
    import numpy as np
    import concourse.bacc as bacc
    from concourse import mybir
    from concourse.bass_utils import run_bass_kernel_spmd

    I = {k: np.asarray(v) for k, v in inputs.items()}
    ctx = I["ctx_2048"].reshape(TILES, P, DC)
    ctxT = I["ctx_2048"].reshape(B * T, 2, P).transpose(2, 1, 0)
    kpad = np.zeros((4, STRIP, XG, B * T), np.float32)
    kpad[:, 0:XD] = I["ctx_2048"][:, :, 0:D].reshape(B * T, XG, 4, XD).transpose(2, 3, 1, 0)
    arrays = {
        "x": I["x"].reshape(TILES, P, D).transpose(1, 0, 2),
        "ctxT": ctxT,
        "kpad": kpad.reshape(P, XG, B * T),
        "ctxv": ctx[:, :, D:].transpose(1, 0, 2),
        "mask": I["mask_BxS2_fk1"].reshape(1, B * T),
        "mask_col": I["mask_BxS2_fk1"].reshape(TILES, P).T,
        "mask_i": I["mask_BxS2_ik0"].reshape(1, B * T),
        "w1_0": I["L0_ffn_w1"].transpose(1, 0, 2).reshape(P, -1),
        "w2_0": I["L0_ffn_w2"].reshape(EXP, 4, P, D).transpose(2, 0, 1, 3).reshape(P, -1),
        "w1_1": I["L1_ffn_W1"].transpose(1, 0, 2).reshape(P, -1),
        "w2_1": I["L1_ffn_W2"].reshape(EXP, 4, P, D).transpose(2, 0, 1, 3).reshape(P, -1),
        "consts": constants(),
        "weights": weights(I),
    }
    nc = bacc.Bacc("TRN2", target_bir_lowering=False, num_devices=1)
    feed, A = {}, {}
    for name, a in arrays.items():
        a = np.ascontiguousarray(a)
        feed["in_" + name] = a
        A[name] = nc.dram_tensor("in_" + name, a.shape, mybir.dt.from_np(a.dtype), kind="ExternalInput").ap()
    for name in ("sorted_x", "sorted_y"):
        A[name] = nc.dram_tensor(name, (SLOTS * P, D), mybir.dt.float32, kind="Internal").ap()
    A["out"] = nc.dram_tensor("out_x", (P, TILES, D), mybir.dt.float32, kind="ExternalOutput").ap()
    build(nc, A)
    r = run_bass_kernel_spmd(nc, [feed], core_ids=[0])
    out = r.results[0]["out_x"]
    return out.transpose(1, 0, 2).reshape(B, T, D)
```

```python
import numpy as np
import concourse.bass as bass
from concourse import mybir
from contextlib import ExitStack

FP32 = mybir.dt.float32
BF16 = mybir.dt.bfloat16
I32 = mybir.dt.int32
U32 = mybir.dt.uint32
ALU = mybir.AluOpType
ACT = mybir.ActivationFunctionType
AX = mybir.AxisListType

B, T, D, DC = 8, 256, 128, 256
P = 128
TILES = B * T // P
QT = 4
QN = QT * P
QUADS = TILES // QT
QB = QN // T
CHUNK = 64
GH, DK, DV = 8, 8, 16
XH, XD = 8, 16
STRIP = 32
XG = XH // 4
Q_PARTS = (0, 0, 0, None, 1, 1, 2)
K_PARTS = (0, 1, 2, None, 0, 1, 0)
SLOT_ROWS = len(Q_PARTS) * XD
ROW_BIAS = 3 * XD
ROW_MAX = ROW_BIAS + 1
MH, MD, MR, ML = 16, 8, 4, 32
MG = MH // 4
EXP, F = 8, 512
SLOTS = 24
EPS = 1e-5
BIG = 1e30
CLIP = 80.0

CONST_PLAN = [("ident", 128), ("chunk_mask", 128), ("tri", 128), ("ones", 128), ("head_mask", 8),
              ("block_mask", 128), ("reset", 512), ("clip_mask", 128), ("lat_rope", 256),
              ("q_rope", 256), ("sel_out", XG * 128), ("sel_den", 128), ("sel_rope", MG * 128), ("iota8", 8),
              ("iota8m", 8), ("slot_iota", SLOTS), ("scan_reset", 128), ("neg_half", 32), ("eps", 32),
              ("tile_starts", TILES), ("q_one", 1), ("k_ones", 1)]
WEIGHT_PLAN = [("wq", 64), ("wk", 64), ("wv", 128), ("wg", 128), ("wgk1", 16), ("wgk2", 64), ("bgk", 1),
               ("norm_w", 16), ("wo", 128), ("x_q", 128), ("x_k", 2 * 128), ("x_v", 2 * 128),
               ("x_qb", 1), ("x_kb", 1), ("x_vb", 128), ("x_out", (1 + XG) * 128), ("x_ob", 128),
               ("r0_w", EXP), ("r0_b", EXP), ("m_lat", 128), ("m_qr", 128), ("m_q", MG * 128),
               ("m_k", MG * 128), ("m_v", 128), ("m_o", MG * 128), ("x1_b", 1), ("r1_w", EXP), ("r1_b", EXP),
               ("b1", EXP * 4), ("b2", EXP * D)]


def columns(plan):
    at, out = 0, {}
    for name, n in plan:
        out[name] = (at, n)
        at += n
    return out, at


CC, CN = columns(CONST_PLAN)
WC, WN = columns(WEIGHT_PLAN)


def build(nc, A):
    ctx = ExitStack()
    with ctx:
        def sb(name, shape, dt=FP32):
            return ctx.enter_context(nc.sbuf_tensor(name, shape, dt))

        sems = {}

        def S(name):
            if name not in sems:
                sems[name] = ctx.enter_context(nc.semaphore(name))
            return sems[name]

        cst = sb("cst", [P, CN])
        wts = sb("wts", [P, WN])

        def C(name, rows=P, r0=0):
            a, n = CC[name]
            return cst[r0:r0 + rows, a:a + n]

        def W(name, rows=P, r0=0):
            a, n = WC[name]
            return wts[r0:r0 + rows, a:a + n]

        x_all = sb("x_all", [P, TILES, D])
        xn_all = sb("xn_all", [P, TILES, D])
        xq = sb("xq", [P, QT, D])
        xn = sb("xn", [P, QT, D])
        xnT = sb("xnT", [P, QN])
        unused = sb("unused", [P, 1])
        stats = sb("stats", [P, QT, 6])
        mv = sb("mv", [P, QT, 2])
        ve = sb("ve", [P, QT])
        rstd = sb("rstd", [P, QT])
        qe = sb("qe", [64, QN])
        kdn = sb("kdn", [P, QT, 64])
        vg = sb("vg", [P, QT, D])
        gate = sb("gate", [P, QT, D])
        qe_bd = sb("qe_bd", [64, 2, GH, P])
        am = sb("am", [P, 2, GH, P])
        st = sb("st", [64, 3, QB, D])
        o_sb = sb("o_sb", [P, QT, D])
        o_sq = sb("o_sq", [P, QT, D])
        ss = sb("ss", [P, QT * GH])
        rs = sb("rs", [P, QT * GH])
        oT = sb("oT", [P, QN])
        ctxT = sb("ctxT", [P, 2, QN])
        mask_row = sb("mask_row", [P, B * T])
        mask_bias = sb("mask_bias", [1, B * T], BF16)
        mask_col = sb("mask_col", [P, TILES])
        has = sb("has", [P, B])
        nothas = sb("nothas", [P, B])
        mask_i = mask_row[:, :].bitcast(I32)
        qa = sb("qa", [P, MG, QN])
        ka = sb("ka", [P, MG, QN])
        vm = sb("vm", [P, QT, MH, STRIP])
        vx = vm[:, :, 0:XH, :]
        pT = sb("pT", [P, 3, 1024])
        ident_b = sb("ident_b", [P, P], BF16)
        sel_qp = sb("sel_qp", [P, XH, P], BF16)
        sel_kp = sb("sel_kp", [P, 3, XH, P], BF16)
        q_parts = sb("q_parts", [P, 3, QN], BF16)
        k_parts = sb("k_parts", [P, 3, QN], BF16)
        qs, ks = (t[:, :, :].rearrange("p g t -> p (g t)").bitcast(BF16).rearrange("p (h t) -> p h t", h=XH)
                  for t in (qa, ka))
        neg_max = sb("neg_max", [P, QT, XH])
        nm_rest = sb("nm_rest", [P, QT, XH])
        nm_parts = sb("nm_parts", [P, QT, 3, XH], BF16)
        nm_rows = sb("nm_rows", [3 * XH, QN], BF16)
        lr, absz, negz, cum = ka[0:16, 0, :], ka[0:64, 1, :], ka[0:64, 2, :], ka[0:64, 3, :]
        eb, enb, ke, kd = (qa[0:64, g, :] for g in range(MG))
        lat, tq, xo0, xo1 = (t[:, :, :].rearrange("p a b -> p (a b)") for t in (gate, vg, o_sb, o_sq))
        rec, on = (lat, tq), (xo0, xo1)
        kf, qf = xo0, xo1
        rest = {"k": lat, "q": tq}
        cl = am[:, :, :, :].rearrange("p a h i -> p a (h i)")
        lg = sb("lg", [P, TILES, EXP])
        lmax = sb("lmax", [P, TILES])
        lex = sb("lex", [P, TILES, EXP])
        lsum = sb("lsum", [P, TILES])
        prob = sb("prob", [P, TILES])
        amin = sb("amin", [P, TILES])
        onehot = sb("onehot", [P, TILES, EXP])
        tie = sb("tie", [P, TILES, EXP])
        cnt = sb("cnt", [P, EXP, TILES])
        incl = sb("incl", [P, EXP, TILES])
        more = sb("more", [P, EXP, TILES])
        ntile = sb("ntile", [P, EXP])
        ends = sb("ends", [P, EXP])
        starts = sb("starts", [P, EXP])
        pos_f = sb("pos_f", [P, TILES])
        pos = sb("pos", [P, TILES], U32)
        slot_ge = sb("slot_ge", [P, SLOTS, EXP])
        slot_f = sb("slot_f", [P, SLOTS])
        slot_e = sb("slot_e", [P, SLOTS], I32)
        zeros = sb("zeros", [P, D])
        w1 = sb("w1", [P, EXP * 2 * F])
        w2 = sb("w2", [P, EXP * 4 * D])
        w1b, w2b = w1[:, 0:EXP * F], w1[:, EXP * F:2 * EXP * F]
        hidT = pT[:, 0, :].rearrange("p (s f) -> p s f", s=2)
        xs, xsT, ys = (pT[:, 1, k * 256:(k + 1) * 256].rearrange("p (s d) -> p s d", s=2) for k in range(3))
        act_a = am[:, 0, :, :].rearrange("p h i -> p (h i)").rearrange("p (s f) -> p s f", s=2)
        hid = am[:, 1, :, :].rearrange("p h i -> p (h i)").rearrange("p (s f) -> p s f", s=2)
        ps = ctx.enter_context(nc.psum_tensor("ps", [P, 8, 512], FP32))

        def bank(b, rows=P, r0=0):
            return ps[r0:r0 + rows, b, :]

        ident = C("ident")
        block = ctx.enter_context(nc.Block())

        def tri3(ap, k):
            return ap.rearrange("p (a b) -> p a b", a=k)

        def dve_wait(v, sem, value):
            v.wait_ge(sem, value)
            v.memset(unused[0:1, 0:1], 0.0)

        def dve_ln(v, n):
            for j in range(QT):
                v.bn_stats(stats[:, j, :], xq[:, j, :]).then_inc(S("ln_stats"), 1)
            dve_wait(v, S("ln_stats"), (n + 1) * QT)
            for j in range(QT):
                i = v.bn_aggr(mv[:, j, :], stats[:, j, :])
            i.then_inc(S("ln_mv"), 1)
            v.wait_ge(S("ln_rstd"), n + 1)
            v.wait_ge(S("ln_mv"), n + 1)
            for j in range(QT):
                v.tensor_scalar(xn[:, j, :], xq[:, j, :], mv[:, j, 0:1], rstd[:, j:j + 1],
                                ALU.subtract, ALU.mult).then_inc(S("ln_xn"), 1)

        def pool_ln(g, n):
            g.wait_ge(S("ln_mv"), n + 1)
            g.tensor_tensor(ve[:, :], mv[:, :, 1], C("eps")[:, 0:QT], ALU.add).then_inc(S("ln_ve"), 1)
            g.wait_ge(S("ln_ve"), n + 1)
            g.tensor_tensor(rstd[:, :], ve[:, :], C("neg_half")[:, 0:QT], ALU.pow).then_inc(S("ln_rstd"), 1)

        def pe_ln(pe, n, b):
            for j in range(QT):
                pe.wait_ge(S("ln_xn"), n * QT + j + 1)
                i = pe.transpose(bank(b)[:, j * P:(j + 1) * P], xn[:, j, :], ident)
            i.then_inc(S("ln_xnT_ps"), 1)

        def act_ln(a, n, b):
            a.wait_ge(S("ln_xnT_ps"), n + 1)
            a.activation(xnT[:, :], bank(b), ACT.Copy).then_inc(S("ln_xnT"), 1)

        def pe_gla(pe, n):
            pe.wait_ge(S("ln_xnT"), 3 * n + 1)
            pe.matmul(bank(3, 16), W("wgk1"), xnT[:, :], start=True, stop=True).then_inc(S("lr_ps"), 1)
            pe.matmul(bank(1, 64), W("wq"), xnT[:, :], start=True, stop=True).then_inc(S("q_ps"), 1)
            pe.matmul(bank(2, 64), W("wk"), xnT[:, :], start=True, stop=True).then_inc(S("k_ps"), 1)
            pe.wait_ge(S("lr_sb"), n + 1)
            pe.matmul(bank(4, 64), W("wgk2", 16), lr[:, :], start=True, stop=True).then_inc(S("z_ps"), 1)
            for w, b, s in (("wv", 5, "v_ps"), ("wg", 6, "g_ps")):
                for j in range(QT):
                    i = pe.matmul(bank(b)[:, j * P:(j + 1) * P], xnT[:, j * P:(j + 1) * P], W(w),
                                  start=True, stop=True)
                i.then_inc(S(s), 1)
            pe.wait_ge(S("kd"), n + 1)
            for j in range(QT):
                i = pe.matmul(bank(3)[:, j * 64:(j + 1) * 64], kd[:, j * P:(j + 1) * P], ident[0:64, 0:64],
                              start=True, stop=True)
            i.then_inc(S("kdT_ps"), 1)

            def scores(j):
                pe.wait_ge(S("qe_bd"), n * QT + j + 1)
                if j >= 2:
                    pe.wait_ge(S("am"), n * QT + j - 1)
                for h in range(2):
                    i = pe.matmul(bank(2 * (j % 2) + h), ke[:, j * P:(j + 1) * P],
                                  qe_bd[:, j % 2, 4 * h:4 * h + 4, :], start=True, stop=True)
                i.then_inc(S("sc_ps"), 1)

            def outputs(j):
                if j == 0:
                    pe.wait_ge(S("st"), 2 * (n + 1))
                pe.wait_ge(S("am"), n * QT + j + 1)
                o = bank(5)[:, j * P:(j + 1) * P]
                for h in range(GH):
                    pe.matmul(o[:, h * DV:(h + 1) * DV], am[:, j % 2, h, :], vg[:, j, h * DV:(h + 1) * DV],
                              start=(h == 0), stop=False, skip_group_check=True)
                for c in range(2 * (j % 2), 2 * (j % 2) + 2):
                    if c == 0:
                        continue
                    r = CHUNK * (c % 2)
                    i = pe.matmul(bank(5)[r:r + CHUNK, j * P:(j + 1) * P], qe[:, j * P + r:j * P + r + CHUNK],
                                  st[:, c - 1, j // 2, :], start=False, stop=True, skip_group_check=True)
                i.then_inc(S("o_ps"), 1)

            pe.wait_ge(S("kdn"), n + 1)
            pe.wait_ge(S("v_sb"), n + 1)
            scores(0)
            for c in range(3):
                for b in range(QB):
                    j, r = 2 * b + c // 2, CHUNK * (c % 2)
                    out = bank(4, 64)[:, (c // 2 * QB + b) * D:(c // 2 * QB + b + 1) * D] if c % 2 == 0 \
                        else bank(7, 64)[:, b * D:(b + 1) * D]
                    i = pe.matmul(out, kdn[r:r + CHUNK, j, :], vg[r:r + CHUNK, j, :], start=True, stop=True)
            i.then_inc(S("u_ps"), 1)
            scores(1)
            for j in range(QT):
                outputs(j)
                if j + 2 < QT:
                    scores(j + 2)
            for j in range(QT):
                pe.wait_ge(S("og"), n + 1)
                i = pe.transpose(bank(6)[:, j * P:(j + 1) * P], o_sb[:, j, :], ident)
            i.then_inc(S("goT_ps"), 1)
            pe.wait_ge(S("goT"), n + 1)
            for j in range(QT):
                i = pe.matmul(bank(7)[:, j * P:(j + 1) * P], oT[:, j * P:(j + 1) * P], W("wo"),
                              start=True, stop=True)
            i.then_inc(S("gla_ps"), 1)

        def act_gla(a, n):
            a.wait_ge(S("lr_ps"), n + 1)
            a.activation(lr[:, :], bank(3, 16), ACT.Copy).then_inc(S("lr_sb"), 1)
            a.wait_ge(S("v_ps"), n + 1)
            a.activation(vg[:, :, :], tri3(bank(5), QT), ACT.Copy).then_inc(S("v_sb"), 1)
            a.wait_ge(S("z_ps"), n + 1)
            a.activation(absz[:, :], bank(4, 64), ACT.Abs, bias=W("bgk", 64)).then_inc(S("absz"), 1)
            a.wait_ge(S("absz"), n + 1)
            a.activation(absz[:, :], absz[:, :], ACT.Exp, scale=-1.0).then_inc(S("expz"), 1)
            a.wait_ge(S("expz"), n + 1)
            a.activation(absz[:, :], absz[:, :], ACT.Ln, bias=1.0).then_inc(S("lnz"), 1)
            a.wait_ge(S("cum"), n + 1)
            a.activation(eb[:, :], cum[:, :], ACT.Exp, scale=1.0 / 16).then_inc(S("eb"), 1)
            a.activation(enb[:, :], cum[:, :], ACT.Exp, scale=-1.0 / 16).then_inc(S("enb"), 1)
            a.wait_ge(S("g_ps"), n + 1)
            a.activation(gate[:, :, :], tri3(bank(6), QT), ACT.Silu).then_inc(S("silu"), 1)
            a.wait_ge(S("kdT_ps"), n + 1)
            a.activation(kdn[:, :, :], bank(3)[:, 0:QT * 64].rearrange("p (a b) -> p a b", a=QT),
                         ACT.Copy).then_inc(S("kdn"), 1)
            a.wait_ge(S("o_ps"), n * QT + QT)
            a.activation(o_sq[:, :, :], tri3(bank(5), QT), ACT.Square, scale=float(DV) ** -0.5).then_inc(S("o_sq"), 1)
            a.activation(o_sb[:, :, :], tri3(bank(5), QT), ACT.Copy).then_inc(S("o_sb"), 1)
            a.wait_ge(S("goT_ps"), n + 1)
            a.activation(oT[:, :], bank(6), ACT.Copy).then_inc(S("goT"), 1)

        def dve_gla(v, n):
            v.wait_ge(S("absz"), n + 1)
            v.tensor_scalar(negz[:, :], bank(4, 64), W("bgk", 64), 0.0, ALU.add, ALU.min)\
             .then_inc(S("negz"), 1)
            v.wait_ge(S("lnz"), n + 1)
            v.wait_ge(S("negz"), n + 1)
            v.tensor_tensor(negz[:, :], negz[:, :], absz[:, :], ALU.subtract).then_inc(S("gk"), 1)
            v.wait_ge(S("gk"), n + 1)
            v.tensor_tensor_scan(cum[:, :], C("reset", 64), negz[:, :], 0.0, ALU.mult, ALU.add)\
             .then_inc(S("cum"), 1)
            v.wait_ge(S("eb"), n + 1)
            v.wait_ge(S("q_ps"), n + 1)
            v.scalar_tensor_tensor(qe[:, :], bank(1, 64), float(DK) ** -0.5, eb[:, :], ALU.mult, ALU.mult)\
             .then_inc(S("qe"), 1)
            v.wait_ge(S("enb"), n + 1)
            v.wait_ge(S("k_ps"), n + 1)
            v.tensor_tensor(ke[:, :], bank(2, 64), enb[:, :], ALU.mult).then_inc(S("ke"), 1)
            v.wait_ge(S("ke"), n + 1)
            eb3 = eb[:, :].rearrange("p (c t) -> p c t", t=CHUNK)
            last = eb3[:, :, CHUNK - 1:CHUNK].broadcast_to([64, QN // CHUNK, CHUNK])
            v.tensor_tensor(kd[:, :].rearrange("p (c t) -> p c t", t=CHUNK),
                            ke[:, :].rearrange("p (c t) -> p c t", t=CHUNK), last, ALU.mult)\
             .then_inc(S("kd"), 1)

            def masked(j):
                v.wait_ge(S("sc_ps"), n * QT + j + 1)
                if j >= 2:
                    v.wait_ge(S("o_ps"), n * QT + j - 1)
                r = 2 * (j % 2)
                v.tensor_tensor(am[:, j % 2, :, :],
                                ps[:, r:r + 2, :].rearrange("p b (h i) -> p (b h) i", h=4),
                                C("chunk_mask").unsqueeze(1).broadcast_to([P, GH, P]), ALU.mult)\
                 .then_inc(S("am"), 1)

            masked(0)
            v.wait_ge(S("u_ps"), n + 1)
            bd = C("block_mask", 64).unsqueeze(1).broadcast_to([64, QB, D])
            for c in range(3):
                u = bank(4, 64)[:, c // 2 * QB * D:(c // 2 + 1) * QB * D] if c % 2 == 0 \
                    else bank(7, 64)[:, 0:QB * D]
                v.tensor_tensor(st[:, c, :, :], u.rearrange("p (b d) -> p b d", b=QB), bd, ALU.mult)\
                 .then_inc(S("st_u"), 1)
            v.wait_ge(S("st_u"), 3 * (n + 1))
            for c in range(1, 3):
                if c == 2:
                    v.wait_ge(S("st"), 2 * n + 1)
                for b in range(QB):
                    k = b * (T // CHUNK) + c
                    i = v.scalar_tensor_tensor(st[:, c, b, :], st[:, c - 1, b, :],
                                               eb3[:, k, CHUNK - 1:CHUNK],
                                               st[:, c, b, :], ALU.mult, ALU.add)
                i.then_inc(S("st"), 1)
            for j in range(1, QT):
                masked(j)
            v.wait_ge(S("o_sq"), n + 1)
            v.tensor_reduce(ss[:, :], o_sq[:, :, :].rearrange("p a (h d) -> p (a h) d", d=DV), AX.X, ALU.add)\
             .then_inc(S("ss"), 1)
            v.wait_ge(S("o_sb"), n + 1)
            v.wait_ge(S("rs"), n + 1)
            o3 = o_sb[:, :, :].rearrange("p a (h d) -> p (a h) d", d=DV)
            v.tensor_tensor(o3, o3, rs[:, :].unsqueeze(2).broadcast_to([P, QT * GH, DV]), ALU.mult)\
             .then_inc(S("on"), 1)
            v.wait_ge(S("on"), n + 1)
            v.wait_ge(S("gw"), n + 1)
            v.tensor_tensor(o_sb[:, :, :], o_sb[:, :, :], gate[:, :, :], ALU.mult).then_inc(S("og"), 1)
            v.wait_ge(S("gla_ps"), n + 1)
            v.tensor_tensor(xq[:, :, :], xq[:, :, :], tri3(bank(7), QT), ALU.add).then_inc(S("x1"), 1)
            v.wait_ge(S("x1"), n + 1)

        def pool_gla(g, n):
            g.wait_ge(S("qe"), n + 1)
            for j in range(QT):
                if j >= 2:
                    g.wait_ge(S("sc_ps"), n * QT + j - 1)
                g.tensor_tensor(qe_bd[:, j % 2, :, :],
                                qe[:, j * P:(j + 1) * P].unsqueeze(1).broadcast_to([64, GH, P]),
                                C("head_mask", 64).unsqueeze(2).broadcast_to([64, GH, P]), ALU.mult)\
                 .then_inc(S("qe_bd"), 1)
            g.wait_ge(S("silu"), n + 1)
            g4 = gate[:, :, :].rearrange("p a (h d) -> p (a h) d", d=DV)
            g.tensor_tensor(g4, g4, W("norm_w").unsqueeze(1).broadcast_to([P, QT * GH, DV]), ALU.mult)\
             .then_inc(S("gw"), 1)
            g.wait_ge(S("ss"), n + 1)
            g.tensor_tensor(ss[:, :], ss[:, :], C("eps"), ALU.add).then_inc(S("ss_e"), 1)
            g.wait_ge(S("ss_e"), n + 1)
            g.tensor_tensor(rs[:, :], ss[:, :], C("neg_half"), ALU.pow).then_inc(S("rs"), 1)

        UB = XH // 2
        UX = QB * UB

        def unit(e):
            return e // UB, 2 * (e % UB)

        ORDER = [("M", 0), ("M", 1), ("M", 2), ("M", 3), ("N", 0), ("M", 4), ("M", 5), ("E", 0), ("M", 6),
                 ("E", 1), ("M", 7), ("E", 2), ("N", 1), ("E", 3), ("E", 4), ("E", 5), ("E", 6), ("E", 7)]
        SCORES = [k for k in ORDER if k[0] != "N"]

        def pair(kind, e):
            return 2 * (SCORES.index((kind, e)) % 3)

        PACK_BANKS = (2, 4, 6, 7)

        def pe_project(pe, n):
            pe.matmul(bank(1), W("x_q"), xnT[:, :], start=True, stop=True).then_inc(S("xq_ps"), 1)
            pe.wait_ge(S("ctx_in"), 16 * (n + 1))
            for half in range(2):
                i = pe.matmul(bank(3), W("x_k")[:, half * P:(half + 1) * P], ctxT[:, half, :],
                              start=(half == 0), stop=(half == 1))
            i.then_inc(S("xk_ps"), 1)
            for j in range(QT):
                o = bank(5)[:, j * P:(j + 1) * P]
                for half in range(2):
                    pe.matmul(o, ctxT[:, half, j * P:(j + 1) * P], W("x_v")[:, half * P:(half + 1) * P],
                              start=(half == 0), stop=False)
                i = pe.matmul(o, C("ones", 1), W("x_vb", 1), start=False, stop=True)
            i.then_inc(S("xv_ps"), 1)

        def pe_pack(pe, side, n):
            pe.wait_ge(S(side + "_part2"), n + 1)
            for h in range(XH):
                if h >= 4:
                    pe.wait_ge(S(side + "_slots%d" % (h % 2)), UB * n + (h - 4) // 2 + 1)
                elif side == "q":
                    pe.wait_ge(S("k_slots%d" % (h % 2)), UB * n + (h + 4) // 2 + 1)
                o = PACK_BANKS[h % 4]
                if side == "q":
                    for part, (lo, rows) in enumerate(((0, 64), (64, 32), (96, 16))):
                        i = pe.matmul(bank(o, rows, lo), sel_qp[:, h, lo:lo + rows], q_parts[:, part, :],
                                      start=True, stop=True)
                else:
                    for part in range(3):
                        i = pe.matmul(bank(o), sel_kp[:, part, h, :], k_parts[:, part, :],
                                      start=(part == 0), stop=(part == 2))
                i.then_inc(S(side + "_slots_ps"), 1)

        def pe_xattn(pe, n, layer):
            pe.wait_ge(S("ln_xnT"), 3 * n + 2)
            if layer == 0:
                pe_project(pe, n)
            pe_pack(pe, "k", n)
            pe_pack(pe, "q", n)

            def before(k):
                at = SCORES.index(k)
                if at == 0:
                    for side in "qk":
                        for r in range(2):
                            pe.wait_ge(S(side + "_slots%d" % r), UB * (n + 1))
                    pe.wait_ge(S("mask_row_in"), 16 * (n + 1))
                elif at == 2:
                    pe.wait_ge(S("xva"), n + 1)
                if at >= 3:
                    kind, e = SCORES[at - 3]
                    pe.wait_ge(S("mx_read" if kind == "M" else "ex_read"), UX * n + e + 1)

            def max_scores(e):
                b, h0 = unit(e)
                before(("M", e))
                for jj in range(2):
                    for qt in range(2):
                        q0 = b * T + qt * P
                        i = pe.matmul(bank(pair("M", e) + jj)[:, qt * T:(qt + 1) * T],
                                      qs[0:SLOT_ROWS, h0 + jj, q0:q0 + P],
                                      ks[0:SLOT_ROWS, h0 + jj, b * T:(b + 1) * T], start=True, stop=True)
                i.then_inc(S("mx_ps"), 1)

            def exp_scores(e):
                b, h0 = unit(e)
                before(("E", e))
                if e % UB == 0:
                    pe.wait_ge(S("max_in"), 48 * (QB * n + b + 1))
                for jj in range(2):
                    for kt in range(2):
                        k0 = b * T + kt * P
                        i = pe.matmul(bank(pair("E", e) + jj)[:, kt * T:(kt + 1) * T],
                                      ks[0:SLOT_ROWS, h0 + jj, k0:k0 + P],
                                      qs[0:SLOT_ROWS, h0 + jj, b * T:(b + 1) * T], start=True, stop=True)
                i.then_inc(S("ex_ps"), 1)

            def max_rows(b):
                pe.wait_ge(S("nm_parts"), QB * n + b + 1)
                for t in range(2):
                    i = pe.matmul(bank(6 + b, 3 * XH)[:, t * P:(t + 1) * P],
                                  nm_parts[:, 2 * b + t, :, :].rearrange("p l h -> p (l h)"), ident_b[:, :],
                                  start=True, stop=True)
                i.then_inc(S("nm_ps"), 1)

            def values(e):
                b, h0 = unit(e)
                if e % UB == 0:
                    pe.wait_ge(S("nm_rows"), QB * n + b + 1)
                pe.wait_ge(S("ex_read"), UX * n + e + 1)
                for jj in range(2):
                    g, r = (h0 + jj) // 4, STRIP * ((h0 + jj) % 4)
                    for kt in range(2):
                        i = pe.matmul(bank(6 + b, STRIP, r)[:, g * T:(g + 1) * T],
                                      vx[:, 2 * b + kt, h0 + jj, :],
                                      pT[:, e % 3, jj * 512 + kt * T:jj * 512 + (kt + 1) * T],
                                      start=(kt == 0), stop=(kt == 1), skip_group_check=True)
                i.then_inc(S("pv"), 1)

            def denominators(b):
                pe.wait_ge(S("xrec"), QB * n + b + 1)
                pe.matmul(bank(2 + b), C("sel_den"), rec[b], start=True, stop=True).then_inc(S("xbc_ps"), 1)

            for kind, e in ORDER:
                if kind == "M":
                    max_scores(e)
                elif kind == "N":
                    max_rows(e)
                else:
                    exp_scores(e)
                    if e >= 1:
                        values(e - 1)
            denominators(0)
            values(UX - 1)
            denominators(1)
            for b in range(QB):
                pe.wait_ge(S("xon"), QB * n + b + 1)
                for t in range(2):
                    o, j = bank(4 + b)[:, t * P:(t + 1) * P], 2 * b + t
                    if layer == 0:
                        pe.matmul(o, xnT[:, j * P:(j + 1) * P], W("x_out")[:, 0:P], start=True, stop=False)
                        pe.matmul(o, C("ones", 1), W("x_ob", 1), start=False, stop=False)
                    w = W("x_out")[:, P:] if layer == 0 else C("sel_out")
                    for g in range(XG):
                        i = pe.matmul(o, on[b][:, g * T + t * P:g * T + (t + 1) * P], w[:, g * P:(g + 1) * P],
                                      start=(layer == 1 and g == 0), stop=(g == XG - 1))
                i.then_inc(S("xout_ps"), 1)

        def act_parts(a, side, n, src, scale, ready, count):
            parts = q_parts if side == "q" else k_parts
            a.wait_ge(S(ready), count)
            a.activation(parts[:, 0, :], src, ACT.Copy, scale=scale).then_inc(S(side + "_part0"), 1)
            a.wait_ge(S(side + "_rest"), n + 1)
            a.activation(parts[:, 1, :], rest[side], ACT.Copy).then_inc(S(side + "_part1"), 1)

        def dve_parts(v, side, n, src, scale):
            parts = q_parts if side == "q" else k_parts
            v.wait_ge(S(side + "_part0"), n + 1)
            v.scalar_tensor_tensor(rest[side], src, scale, parts[:, 0, :], ALU.mult, ALU.subtract)\
             .then_inc(S(side + "_rest"), 1)
            v.wait_ge(S(side + "_rest"), n + 1)
            v.wait_ge(S(side + "_part1"), n + 1)
            v.tensor_tensor(parts[:, 2, :], rest[side], parts[:, 1, :], ALU.subtract)\
             .then_inc(S(side + "_part2"), 1)

        def act_slots(a, side, n):
            out, ones = (qs, "q_one") if side == "q" else (ks, "k_ones")
            for h in range(0, XH, 2):
                a.wait_ge(S(side + "_slots_ps"), XH * n + h + 1)
                a.activation(out[0:SLOT_ROWS, h, :], bank(PACK_BANKS[h % 4], SLOT_ROWS), ACT.Identity,
                             bias=C(ones, SLOT_ROWS)).then_inc(S(side + "_slots0"), 1)

        def dve_slots(v, side, n):
            out, ones = (qs, "q_one") if side == "q" else (ks, "k_ones")
            for h in range(1, XH, 2):
                v.wait_ge(S(side + "_slots_ps"), XH * n + h + 1)
                v.tensor_scalar(out[0:SLOT_ROWS, h, :], bank(PACK_BANKS[h % 4], SLOT_ROWS),
                                C(ones, SLOT_ROWS), None, ALU.add).then_inc(S(side + "_slots1"), 1)

        def act_xattn(a, n, q, layer):
            MX = QB * MH // 2
            if layer == 0:
                act_parts(a, "k", n, kf, 1.0, "kf", n + 1)
            else:
                act_parts(a, "k", n, ctxT[:, 0, :], 1.0, "k_in", 16 * (q + 1))
                a.wait_ge(S("v_in"), 16 * (q + 1))
                a.wait_ge(S("mpv"), MX * (q + 1))
                a.activation(vx[:, :, :, 0:XD], ctxT[:, 1, :].rearrange("p (a h d) -> p a h d", a=QT, h=XH),
                             ACT.Copy).then_inc(S("xva"), 1)
            act_parts(a, "q", n, qf, float(XD) ** -0.5, "qf", n + 1)

            def copy_values(b):
                a.wait_ge(S("pv"), UX * n + UB * (b + 1))
                a.activation(on[b], bank(6 + b), ACT.Copy).then_inc(S("xo"), 1)

            act_slots(a, "k", n)
            act_slots(a, "q", n)
            for kind, e in ORDER:
                if kind == "N":
                    a.wait_ge(S("nm_ps"), QB * n + e + 1)
                    a.activation(nm_rows[:, e * T:(e + 1) * T], bank(6 + e, 3 * XH)[:, 0:T], ACT.Copy)\
                     .then_inc(S("nm_rows"), 1)
                elif kind == "E":
                    if e >= 3:
                        a.wait_ge(S("pv"), UX * n + e - 2)
                    a.wait_ge(S("ex_ps"), UX * n + e + 1)
                    p = pair("E", e)
                    out, scores = pT[:, e % 3, :].rearrange("p (a b) -> p a b", a=2), ps[:, p:p + 2, :]
                    if layer == 0:
                        i = a.activation(out, scores, ACT.Exp)
                    else:
                        i = a.activation(out, scores, ACT.Exp, bias=W("x1_b"))
                    i.then_inc(S("ex_read"), 1)
                    if e == UB + 1:
                        copy_values(0)
            copy_values(1)

        def dve_xattn(v, n, q, layer):
            cols = bass.ds(q * QN, QN)
            if layer == 0:
                v.wait_ge(S("xk_ps"), n + 1)
                v.scalar_tensor_tensor(kf, bank(3), W("x_kb"), mask_row[:, cols], ALU.add, ALU.mult)\
                 .then_inc(S("kf"), 1)
                v.wait_ge(S("xq_ps"), n + 1)
                v.scalar_tensor_tensor(qf, bank(1), W("x_qb"), mask_row[:, cols], ALU.add, ALU.mult)\
                 .then_inc(S("qf"), 1)
                v.wait_ge(S("kf"), n + 1)
                dve_parts(v, "k", n, kf, 1.0)
                v.wait_ge(S("qf"), n + 1)
                dve_parts(v, "q", n, qf, float(XD) ** -0.5)
                v.wait_ge(S("xv_ps"), n + 1)
                m = mask_col[:, bass.ds(q * QT, QT)].unsqueeze(2).unsqueeze(3).broadcast_to([P, QT, XH, XD])
                v.tensor_tensor(vx[:, :, :, 0:XD], bank(5).rearrange("p (a h d) -> p a h d", a=QT, h=XH), m,
                                ALU.mult).then_inc(S("xva"), 1)
            else:
                v.wait_ge(S("ln_xnT"), 3 * n + 2)
                hb = has[:, bass.ds(q * QB, QB)].unsqueeze(2).broadcast_to([P, QB, T])
                v.tensor_tensor(tri3(qf, QB), tri3(xnT[:, :], QB), hb, ALU.mult).then_inc(S("qf"), 1)
                v.wait_ge(S("k_in"), 16 * (q + 1))
                dve_parts(v, "k", n, ctxT[:, 0, :], 1.0)
                v.wait_ge(S("qf"), n + 1)
                dve_parts(v, "q", n, qf, float(XD) ** -0.5)
            dve_slots(v, "k", n)
            dve_slots(v, "q", n)
            STEPS = 4 + layer

            def minus_max(b):
                step = [STEPS * (QB * q + b)]

                def done(i):
                    step[0] += 1
                    i.then_inc(S("nm_step%d" % layer), 1)
                    v.wait_ge(S("nm_step%d" % layer), step[0])

                t = slice(2 * b, 2 * b + 2)
                m, r, parts = neg_max[:, t, :], nm_rest[:, t, :], nm_parts[:, t, :, :]
                v.wait_ge(S("mx_read"), UX * n + UB * (b + 1))
                if layer == 1:
                    done(v.tensor_scalar(m, m, W("x1_b"), None, ALU.subtract))
                done(v.tensor_copy(parts[:, :, 0, :], m))
                done(v.tensor_tensor(r, m, parts[:, :, 0, :], ALU.subtract))
                done(v.tensor_copy(parts[:, :, 1, :], r))
                v.tensor_tensor(parts[:, :, 2, :], r, parts[:, :, 1, :], ALU.subtract)\
                 .then_inc(S("nm_parts"), 1)
                done(v.memset(unused[0:1, 0:1], 0.0))

            for b in range(QB):
                for e in range(UB * b, UB * (b + 1)):
                    _, h0 = unit(e)
                    v.wait_ge(S("mx_ps"), UX * n + e + 1)
                    p = pair("M", e)
                    v.tensor_reduce(neg_max[:, 2 * b:2 * b + 2, h0:h0 + 2].rearrange("p t j -> p j t"),
                                    ps[:, p:p + 2, :].rearrange("p j (t k) -> p j t k", t=2), AX.X, ALU.max,
                                    negate=True).then_inc(S("mx_read"), 1)
                minus_max(b)
            for b in range(QB):
                v.wait_ge(S("xo"), QB * n + b + 1)
                v.reciprocal(rec[b], on[b]).then_inc(S("xrec"), 1)
            for b in range(QB):
                v.wait_ge(S("xbc_ps"), QB * n + b + 1)
                v.tensor_tensor(on[b], on[b], bank(2 + b), ALU.mult).then_inc(S("xon"), 1)
            for b in range(QB):
                v.wait_ge(S("xout_ps"), QB * n + b + 1)
                xb = xq[:, 2 * b:2 * b + 2, :]
                v.tensor_tensor(xb, xb, bank(4 + b)[:, 0:T].rearrange("p (a d) -> p a d", a=2), ALU.add)\
                 .then_inc(S("x2"), 1)
            v.wait_ge(S("x2"), QB * (n + 1))

        def sp_xattn(sp, n, q):
            for r in range(2):
                sp.wait_ge(S("k_slots%d" % r), UB * (n + 1))
            sp.dma_start(ks[ROW_BIAS:ROW_BIAS + 1, :, :],
                         mask_bias[:, bass.ds(q * QN, QN)].unsqueeze(1).broadcast_to([1, XH, QN]))\
              .then_inc(S("mask_row_in"), 16)
            for b in range(QB):
                sp.wait_ge(S("nm_rows"), QB * n + b + 1)
                for part in range(3):
                    sp.dma_start(qs[ROW_MAX + part:ROW_MAX + part + 1, :, b * T:(b + 1) * T],
                                 nm_rows[part * XH:(part + 1) * XH, b * T:(b + 1) * T]).then_inc(S("max_in"), 16)

        MU = MH // 2
        MX = QB * MU
        p_part = [pT[:, c // 2, c % 2 * 512:(c % 2 + 1) * 512] for c in range(4)]
        m_rec = [lat, tq] + p_part[2:]
        m_on = [xo0, xo1] + p_part[:2]

        def m_pair(u):
            return 2 * (u % 2)

        def m_bank(b, g):
            return 4 + 2 * b + g // 2

        def pe_mla(pe, n):
            pe.wait_ge(S("ln_xnT"), 3 * (n + QUADS) + 1)
            pe.matmul(bank(1), W("m_lat"), xnT[:, :], start=True, stop=True).then_inc(S("lat_ps"), 1)
            pe.wait_ge(S("lat"), n + 1)
            pe.matmul(bank(2), W("m_qr", ML), lat[0:ML, :], start=True, stop=True).then_inc(S("qr_ps"), 1)
            kb, qb = (3, 4, 6, 7), (0, 1, 2, 3)
            for g in range(MG):
                pe.matmul(bank(kb[g]), W("m_k")[:, g * P:(g + 1) * P], lat[:, :], start=True, stop=True)\
                  .then_inc(S("mk_ps"), 1)
            for j in range(QT):
                i = pe.matmul(bank(5)[:, j * P:(j + 1) * P], lat[:, j * P:(j + 1) * P], W("m_v"),
                              start=True, stop=True)
            i.then_inc(S("mv_ps"), 1)
            pe.wait_ge(S("tq"), n + 1)
            for g in range(MG):
                if g == MG - 1:
                    pe.wait_ge(S("mka"), MG * n + 1)
                pe.matmul(bank(qb[g]), W("m_q", ML)[:, g * P:(g + 1) * P], lat[0:ML, :], start=True, stop=False)
                pe.matmul(bank(qb[g]), C("sel_rope")[:, g * P:(g + 1) * P], tq[:, :], start=False, stop=True)\
                  .then_inc(S("mq_ps"), 1)

            def scores(u):
                b, hp = u // MU, u % MU
                if u == 0:
                    pe.wait_ge(S("mqa"), MG * (n + 1))
                    pe.wait_ge(S("mka"), MG * (n + 1))
                    pe.wait_ge(S("mva"), n + 1)
                if u >= 2:
                    pe.wait_ge(S("ms_read"), MX * n + u - 1)
                for jj in range(2):
                    r, g = STRIP * (2 * (hp % 2) + jj), hp // 2
                    o = bank(m_pair(u) + jj)
                    k, qq = ka[r:r + MD + MR, g, :], qa[r:r + MD + MR, g, :]
                    pe.matmul(o[:, 0:T], k[:, b * T:b * T + P], qq[:, b * T:(b + 1) * T], start=True, stop=True)
                    i = pe.matmul(o[:, T:T + P], k[:, b * T + P:(b + 1) * T], qq[:, b * T + P:(b + 1) * T],
                                  start=True, stop=True)
                i.then_inc(S("ms_ps"), 1)

            def values(u):
                b, hp = u // MU, u % MU
                pe.wait_ge(S("mp"), MX * n + u + 1)
                for jj in range(2):
                    r, g = STRIP * (2 * (hp % 2) + jj), hp // 2
                    o = bank(m_bank(b, g), STRIP, r)[:, g % 2 * T:(g % 2 + 1) * T]
                    p = pT[:, u % 3, jj * 512:jj * 512 + 3 * P]
                    pe.matmul(o, vm[:, 2 * b, 2 * hp + jj, :], p[:, 0:T], start=True, stop=False,
                              skip_group_check=True)
                    i = pe.matmul(o[:, P:T], vm[:, 2 * b + 1, 2 * hp + jj, :], p[:, T:T + P], start=False,
                                  stop=True, skip_group_check=True)
                i.then_inc(S("mpv"), 1)

            for u in range(MX + 2):
                if u < MX:
                    scores(u)
                if u >= 2:
                    values(u - 2)
            for c in range(2 * QB):
                pe.wait_ge(S("mrec"), 2 * QB * n + c + 1)
                pe.matmul(bank(c), C("sel_den"), m_rec[c], start=True, stop=True).then_inc(S("mbc_ps"), 1)
            for b in range(QB):
                pe.wait_ge(S("mon"), 2 * (QB * n + b + 1))
                for t in range(2):
                    for g in range(MG):
                        i = pe.matmul(bank(4 + b)[:, t * P:(t + 1) * P],
                                      m_on[2 * b + g // 2][:, g % 2 * T + t * P:g % 2 * T + (t + 1) * P],
                                      W("m_o")[:, g * P:(g + 1) * P], start=(g == 0), stop=(g == MG - 1))
                i.then_inc(S("mout_ps"), 1)

        def act_mla(a, n):
            kb = (3, 4, 6, 7)
            for g in range(MG):
                a.wait_ge(S("mk_ps"), MG * n + g + 1)
                a.activation(ka[:, g, :], bank(kb[g]), ACT.Copy).then_inc(S("mka"), 1)
            a.wait_ge(S("mv_ps"), n + 1)
            a.activation(vm[:, :, :, 0:MD], bank(5).rearrange("p (a h d) -> p a h d", a=QT, h=MH),
                         ACT.Copy).then_inc(S("mva"), 1)

            def copy_values(b):
                a.wait_ge(S("mpv"), MX * n + MU * (b + 1))
                for c in range(2 * b, 2 * b + 2):
                    a.activation(m_on[c], bank(4 + c), ACT.Copy).then_inc(S("mo"), 1)

            for u in range(MX):
                if u >= 3:
                    a.wait_ge(S("mpv"), MX * n + u - 2)
                a.wait_ge(S("ms_read"), MX * n + u + 1)
                view = [t.rearrange("p (a b) -> p a b", a=2)[:, :, 0:3 * P] for t in (pT[:, u % 3, :], cl[:, u % 2, :])]
                a.activation(view[0], view[1], ACT.Exp, scale=float(MD + MR) ** -0.5).then_inc(S("mp"), 1)
                if u == MU + 2:
                    copy_values(0)
            copy_values(1)

        def dve_mla(v, n):
            v.wait_ge(S("lat_ps"), n + 1)

            def rope(name):
                return C(name).unsqueeze(1).broadcast_to([P, QB, T])

            v.tensor_tensor(tri3(lat[:, :], QB), tri3(bank(1), QB), rope("lat_rope"), ALU.mult)\
             .then_inc(S("lat"), 1)
            v.wait_ge(S("qr_ps"), n + 1)
            v.tensor_tensor(tri3(tq[:, :], QB), tri3(bank(2), QB), rope("q_rope"), ALU.mult)\
             .then_inc(S("tq"), 1)
            for g in range(MG):
                v.wait_ge(S("mq_ps"), MG * n + g + 1)
                v.tensor_copy(qa[:, g, :], bank((0, 1, 2, 3)[g])).then_inc(S("mqa"), 1)

            def denominators(b):
                for c in range(2 * b, 2 * b + 2):
                    v.wait_ge(S("mo"), 2 * QB * n + c + 1)
                    v.reciprocal(m_rec[c], m_on[c]).then_inc(S("mrec"), 1)

            for u in range(MX):
                if u >= 2:
                    v.wait_ge(S("mp"), MX * n + u - 1)
                v.wait_ge(S("ms_ps"), MX * n + u + 1)
                p = m_pair(u)
                blocks = ps[:, p:p + 2, :].rearrange("p a (b c) -> p (a b) c", c=P)
                out = cl[:, u % 2, :].rearrange("p (a c) -> p a c", c=P)
                v.scalar_tensor_tensor(out[:, 0:8:2, :], blocks[:, 0:8:2, :], -CLIP,
                                       C("clip_mask").unsqueeze(1).broadcast_to([P, 4, P]), ALU.max, ALU.min)
                v.tensor_scalar(out[:, 1:8:4, :], blocks[:, 1:8:4, :], -CLIP, CLIP, ALU.max, ALU.min)\
                 .then_inc(S("ms_read"), 1)
                if u == MU + 3:
                    denominators(0)
            denominators(1)
            for c in range(2 * QB):
                v.wait_ge(S("mbc_ps"), 2 * QB * n + c + 1)
                v.tensor_tensor(m_on[c], m_on[c], bank(c), ALU.mult).then_inc(S("mon"), 1)
            for b in range(QB):
                v.wait_ge(S("mout_ps"), QB * n + b + 1)
                xb = xq[:, 2 * b:2 * b + 2, :]
                v.tensor_tensor(xb, xb, bank(4 + b)[:, 0:T].rearrange("p (a d) -> p a d", a=2), ALU.add)\
                 .then_inc(S("x3"), 1)
            v.wait_ge(S("x3"), QB * (n + 1))

        def pe_router(pe, n, layer):
            pe.wait_ge(S("ln_xnT"), 3 * n + 3)
            for j in range(QT):
                i = pe.matmul(bank(1)[:, j * EXP:(j + 1) * EXP], xnT[:, j * P:(j + 1) * P],
                              W("r%d_w" % layer), start=True, stop=True)
            i.then_inc(S("lg_ps"), 1)

        def dve_router(v, n, q, layer):
            tiles = bass.ds(q * QT, QT)
            v.wait_ge(S("lg_ps"), n + 1)
            v.tensor_tensor(lg[:, tiles, :], bank(1)[:, 0:QT * EXP].rearrange("p (a e) -> p a e", a=QT),
                            W("r%d_b" % layer).unsqueeze(1).broadcast_to([P, QT, EXP]), ALU.add)\
             .then_inc(S("lg"), 1)
            v.tensor_copy(x_all[:, tiles, :], xq[:, :, :]).then_inc(S("x_saved"), 1)
            v.wait_ge(S("xn_saved"), n + 1)

        def act_router(a, n, q):
            a.wait_ge(S("ln_xn"), QT * 3 * (n + 1))
            a.activation(xn_all[:, bass.ds(q * QT, QT), :], xn[:, :, :], ACT.Copy).then_inc(S("xn_saved"), 1)

        def pe_sort(pe, layer):
            pe.wait_ge(S("onehot"), layer + 1)
            oh = onehot[:, :, :].rearrange("p t e -> p (t e)")
            pe.matmul(bank(0)[:, 0:P], C("tri"), oh, start=True, stop=True)
            pe.matmul(bank(1)[:, 0:P], C("ones"), oh, start=True, stop=True).then_inc(S("rank_ps"), 1)

        def act_sort(a, layer):
            a.wait_ge(S("lless"), layer + 1)
            a.activation(lex[:, :, :], lg[:, :, :], ACT.Exp).then_inc(S("lex"), 1)

        def dve_sort(v, layer):
            step = [0]

            def done(i):
                step[0] += 1
                i.then_inc(S("sort%d" % layer), 1)
                v.wait_ge(S("sort%d" % layer), step[0])

            def over(ap, shape, axis):
                return ap.unsqueeze(axis).broadcast_to(shape)

            te = [P, TILES, EXP]
            v.wait_ge(S("lg"), QUADS * (layer + 1))
            done(v.tensor_reduce(lmax[:, :], lg[:, :, :], AX.X, ALU.max))
            v.tensor_tensor(lg[:, :, :], lg[:, :, :], over(lmax[:, :], te, 2), ALU.subtract)\
             .then_inc(S("lless"), 1)
            v.wait_ge(S("lless"), layer + 1)
            done(v.scalar_tensor_tensor(tie[:, :, :],
                                        lg[:, :, :], 0.0, over(C("iota8m"), te, 1), ALU.is_equal, ALU.mult))
            done(v.tensor_reduce(amin[:, :], tie[:, :, :],
                                 AX.X, ALU.min))
            v.tensor_tensor(onehot[:, :, :], over(C("iota8m"), te, 1), over(amin[:, :], te, 2), ALU.is_equal)\
             .then_inc(S("onehot"), 1)
            v.wait_ge(S("lex"), layer + 1)
            done(v.tensor_reduce(lsum[:, :], lex[:, :, :], AX.X, ALU.add))
            done(v.reciprocal(prob[:, :], lsum[:, :]))
            v.wait_ge(S("rank_ps"), layer + 1)
            done(v.tensor_copy(cnt[:, :, :], bank(1)[:, 0:P].rearrange("p (t e) -> p e t", e=EXP)))
            flat = [t[:, :, :].rearrange("p e t -> p (e t)") for t in (incl, cnt)]
            done(v.tensor_tensor_scan(flat[0], C("scan_reset"), flat[1], 0.0, ALU.mult, ALU.add))
            total = incl[:, :, TILES - 1]
            et = [P, EXP, TILES]
            done(v.tensor_tensor(more[:, :, :], over(total, et, 2), over(C("tile_starts"), et, 1), ALU.is_gt))
            done(v.tensor_reduce(ntile[:, :], more[:, :, :], AX.X, ALU.add))
            done(v.tensor_tensor_scan(ends[:, :], C("ones")[:, 0:EXP], ntile[:, :], 0.0, ALU.mult, ALU.add))
            done(v.tensor_tensor(starts[:, :], ends[:, :], ntile[:, :], ALU.subtract))
            done(v.tensor_tensor(incl[:, :, :], incl[:, :, :], cnt[:, :, :], ALU.subtract))
            done(v.scalar_tensor_tensor(incl[:, :, :], over(starts[:, :], et, 2), float(P), incl[:, :, :],
                                        ALU.mult, ALU.add))
            et_t = incl[:, :, :].rearrange("p e t -> p t e")
            done(v.tensor_tensor(lex[:, :, :], bank(0)[:, 0:P].rearrange("p (t e) -> p t e", e=EXP), et_t, ALU.add))
            done(v.tensor_tensor(lex[:, :, :], lex[:, :, :], onehot[:, :, :], ALU.mult))
            done(v.tensor_reduce(pos_f[:, :], lex[:, :, :], AX.X, ALU.add))
            v.tensor_copy(pos[:, :], pos_f[:, :]).then_inc(S("pos"), 1)
            if layer == 0:
                v.memset(slot_f[:, :], 0.0).then_inc(S("ys"), 2)
                v.wait_ge(S("ys"), 2)
            se = [P, SLOTS, EXP]
            done(v.tensor_tensor(slot_ge[:, :, :], over(C("slot_iota"), se, 2), over(ends[:, :], se, 1), ALU.is_ge))
            done(v.tensor_reduce(slot_f[:, :], slot_ge[:, :, :], AX.X, ALU.add))
            if layer == 0:
                for s in range(2):
                    v.memset(ys[:, s, :], 0.0).then_inc(S("y_out%d" % s), 16)
            v.tensor_scalar(slot_e[:, :], slot_f[:, :], float(EXP - 1), None, ALU.min).then_inc(S("slots"), 1)

        TURNS = SLOTS // 2

        def pool_scatter(g, layer):
            g.wait_ge(S("pos"), layer + 1)
            g.wait_ge(S("xn_saved"), QUADS * (layer + 1))
            g.wait_ge(S("zeroed"), 16)
            for t in range(TILES):
                g.indirect_dma_start(A["sorted_x"], bass.IndirectOffsetOnAxis(ap=pos[:, t:t + 1], axis=0),
                                     xn_all[:, t, :], None).then_inc(S("scattered"), 16)

        def pool_gather(g, layer):
            for s in range(2):
                g.wait_ge(S("y_out%d" % s), 16 * ((layer + 1) * TURNS + 1))
            for t in range(TILES):
                g.indirect_dma_start(xn_all[:, t, :], None, A["sorted_y"],
                                     bass.IndirectOffsetOnAxis(ap=pos[:, t:t + 1], axis=0))\
                 .then_inc(S("gathered"), 16)

        def sp_experts(sp, layer):
            sp.wait_ge(S("scattered"), 16 * TILES * (layer + 1))
            for s in range(2):
                sp.dma_start(xs[:, s, :], A["sorted_x"][s * P:(s + 1) * P, :]).then_inc(S("xs_in%d" % s), 16)
            with sp.Fori(0, TURNS - 1) as i:
                n = i + layer * TURNS
                for s in range(2):
                    sp.wait_ge(S("xsT_ps"), 2 * n + s + 1)
                    sp.dma_start(xs[:, s, :], A["sorted_x"][bass.ds((i * 2 + 2 + s) * P, P), :])\
                      .then_inc(S("xs_in%d" % s), 16)
                for s in range(2):
                    sp.wait_ge(S("ys"), 2 * n + s + 3)
                    sp.dma_start(A["sorted_y"][bass.ds((i * 2 + s) * P, P), :], ys[:, s, :])\
                      .then_inc(S("y_out%d" % s), 16)
            for s in range(2):
                sp.wait_ge(S("ys"), 2 * TURNS * (layer + 1) + 1 + s)
                sp.dma_start(A["sorted_y"][(SLOTS - 2 + s) * P:(SLOTS - 1 + s) * P, :], ys[:, s, :])\
                  .then_inc(S("y_out%d" % s), 16)

        def pe_experts(pe, layer):
            pe.wait_ge(S("slots"), layer + 1)
            pe.wait_ge(S("w_in"), 32 * (layer + 1))
            with pe.Fori(0, TURNS) as i:
                n = i + layer * TURNS
                es = [pe.value_load(slot_e[0:1, bass.ds(i * 2 + s, 1)], min_val=0, max_val=EXP - 1)
                      for s in range(2)]
                for s in range(2):
                    pe.wait_ge(S("ys"), 2 * n + s + 1)
                    pe.wait_ge(S("xs_in%d" % s), 16 * (n + 1))
                    pe.transpose(bank(4 * s)[:, 0:P], xs[:, s, :], ident).then_inc(S("xsT_ps"), 1)
                for s in range(2):
                    pe.wait_ge(S("xsT"), 2 * n + s + 1)
                    if layer == 0:
                        for half in range(2):
                            k = pe.matmul(bank(4 * s + 1 + half), xsT[:, s, :],
                                          w1[:, bass.ds(es[s] * (2 * F) + half * F, F)], start=True, stop=True)
                    else:
                        k = pe.matmul(bank(4 * s + 1), xsT[:, s, :], w1b[:, bass.ds(es[s] * F, F)],
                                      start=True, stop=True)
                    k.then_inc(S("h_ps"), 1)
                for s in range(2):
                    pe.wait_ge(S("hid"), 2 * n + s + 1)
                    for j in range(4):
                        k = pe.transpose(bank(4 * s + 3)[:, j * P:(j + 1) * P], hid[:, s, j * P:(j + 1) * P], ident)
                    k.then_inc(S("hT_ps"), 1)
                for s in range(2):
                    pe.wait_ge(S("hidT"), 2 * n + s + 1)
                    wsrc = w2 if layer == 0 else w2b
                    for j in range(4):
                        k = pe.matmul(bank(4 * s)[:, 0:D], hidT[:, s, j * P:(j + 1) * P],
                                      wsrc[:, bass.ds(es[s] * (4 * D) + j * D, D)], start=(j == 0), stop=(j == 3))
                    k.then_inc(S("y_ps"), 1)

        def act_experts(a, layer):
            a.wait_ge(S("slots"), layer + 1)
            with a.Fori(0, TURNS) as i:
                n = i + layer * TURNS
                if layer == 1:
                    es = [a.value_load(slot_e[0:1, bass.ds(i * 2 + s, 1)], min_val=0, max_val=EXP - 1)
                          for s in range(2)]
                for s in range(2):
                    a.wait_ge(S("xsT_ps"), 2 * n + s + 1)
                    a.activation(xsT[:, s, :], bank(4 * s)[:, 0:P], ACT.Copy).then_inc(S("xsT"), 1)
                for s in range(2):
                    a.wait_ge(S("h_ps"), 2 * n + s + 1)
                    if layer == 0:
                        a.activation(act_a[:, s, :], bank(4 * s + 1), ACT.Silu).then_inc(S("silu_a"), 1)
                    else:
                        a.activation(hid[:, s, :], bank(4 * s + 1), ACT.Copy).then_inc(S("hid"), 1)
                for s in range(2):
                    a.wait_ge(S("hT_ps"), 2 * n + s + 1)
                    if layer == 0:
                        a.activation(hidT[:, s, :], bank(4 * s + 3), ACT.Copy).then_inc(S("hidT"), 1)
                    else:
                        for j in range(4):
                            k = a.activation(hidT[:, s, j * P:(j + 1) * P], bank(4 * s + 3)[:, j * P:(j + 1) * P],
                                             ACT.Relu, bias=W("b1")[:, bass.ds(es[s] * 4 + j, 1)])
                        k.then_inc(S("hidT"), 1)

        def dve_experts(v, layer):
            v.wait_ge(S("slots"), layer + 1)
            with v.Fori(0, TURNS) as i:
                n = i + layer * TURNS
                if layer == 1:
                    es = [v.value_load(slot_e[0:1, bass.ds(i * 2 + s, 1)], min_val=0, max_val=EXP - 1)
                          for s in range(2)]
                if layer == 0:
                    for s in range(2):
                        v.wait_ge(S("silu_a"), 2 * n + s + 1)
                        v.tensor_tensor(hid[:, s, :], bank(4 * s + 2), act_a[:, s, :], ALU.mult)\
                         .then_inc(S("hid"), 1)
                for s in range(2):
                    v.wait_ge(S("y_ps"), 2 * n + s + 1)
                    v.wait_ge(S("y_out%d" % s), 16 * (n + 1))
                    if layer == 0:
                        v.tensor_copy(ys[:, s, :], bank(4 * s)[:, 0:D]).then_inc(S("ys"), 1)
                    else:
                        v.tensor_tensor(ys[:, s, :], bank(4 * s)[:, 0:D], W("b2")[:, bass.ds(es[s] * D, D)],
                                        ALU.add).then_inc(S("ys"), 1)

        def dve_combine(v, q, layer):
            tiles = bass.ds(q * QT, QT)
            y = xn_all[:, tiles, :]
            p = prob[:, tiles].unsqueeze(2).broadcast_to([P, QT, D])
            v.wait_ge(S("gathered"), 16 * TILES * (layer + 1))
            if layer == 0:
                v.wait_ge(S("x_saved"), QUADS + q)
            v.tensor_tensor(y, y, p, ALU.mult).then_inc(S("yp"), 1)
            v.wait_ge(S("yp"), q + layer * QUADS + 1)
            out = xq[:, :, :] if layer == 0 else x_all[:, tiles, :]
            v.tensor_tensor(out, y, x_all[:, tiles, :], ALU.add).then_inc(S("x_next"), 1)

        @block.sync
        def _(sp):
            sp.dma_start(cst[:, :], A["consts"]).then_inc(S("consts_in"), 16)
            sp.dma_start(wts[:, :], A["weights"]).then_inc(S("weights_in"), 16)
            sp.dma_start(xq[:, :, :], A["x"][:, 0:QT, :]).then_inc(S("x_in"), 16)
            sp.dma_start(mask_row[:, :], A["mask"].broadcast_to([P, B * T])).then_inc(S("mask_in"), 16)
            sp.dma_start(mask_col[:, :], A["mask_col"]).then_inc(S("mask_in"), 16)
            sp.dma_start(ctxT[:, :, :], A["ctxT"][:, :, 0:QN]).then_inc(S("ctx_in"), 16)
            sp.wait_ge(S("zeros"), 1)
            sp.dma_start(A["sorted_x"].rearrange("(s p) d -> p s d", p=P),
                         zeros[:, :].unsqueeze(1).broadcast_to([P, SLOTS, D])).then_inc(S("zeroed"), 16)
            sp.dma_start(w1[:, :], A["w1_0"]).then_inc(S("w_in"), 16)
            sp.dma_start(w2[:, :], A["w2_0"]).then_inc(S("w_in"), 16)
            with sp.Fori(0, QUADS - 1) as q:
                sp.wait_ge(S("xv_ps"), q + 1)
                sp.dma_start(ctxT[:, :, :], A["ctxT"][:, :, bass.ds((q + 1) * QN, QN)]).then_inc(S("ctx_in"), 16)
                sp_xattn(sp, q, q)
                sp.wait_ge(S("x_saved"), q + 1)
                sp.dma_start(xq[:, :, :], A["x"][:, bass.ds((q + 1) * QT, QT), :]).then_inc(S("x_in"), 16)
            sp_xattn(sp, QUADS - 1, QUADS - 1)
            sp.wait_ge(S("x_saved"), QUADS)
            sp.dma_start(mask_i[:, :],
                         A["mask_i"].broadcast_to([P, B * T])).then_inc(S("mask_in"), 16)
            sp_experts(sp, 0)
            sp.wait_ge(S("y_ps"), SLOTS)
            sp.dma_start(w1b, A["w1_1"]).then_inc(S("w_in"), 16)
            sp.dma_start(w2b, A["w2_1"]).then_inc(S("w_in"), 16)
            with sp.Fori(0, QUADS) as q:
                sp.wait_ge(S("k_part2"), QUADS + q)
                sp.dma_start(ctxT[:, 0, :], A["ctxT"][:, 0, bass.ds(q * QN, QN)]).then_inc(S("k_in"), 16)
                sp.wait_ge(S("xva"), QUADS + q)
                sp.dma_start(ctxT[:, 1, :].rearrange("p (a d) -> p a d", a=QT),
                             A["ctxv"][:, bass.ds(q * QT, QT), :]).then_inc(S("v_in"), 16)
                sp_xattn(sp, q + QUADS, q)
            sp_experts(sp, 1)
            with sp.Fori(0, QUADS) as q:
                sp.wait_ge(S("x_next"), QUADS + q + 1)
                sp.dma_start(A["out"][:, bass.ds(q * QT, QT), :], x_all[:, bass.ds(q * QT, QT), :]).then_inc(S("out_written"), 16)
            sp.wait_ge(S("out_written"), 16 * QUADS)

        @block.gpsimd
        def _(g):
            g.memset(zeros[:, :], 0.0).then_inc(S("zeros"), 1)
            g.memset(sel_kp[:, :, :, :], 0.0).then_inc(S("cleared"), 1)
            g.memset(sel_qp[:, :, :], 0.0).then_inc(S("cleared"), 1)
            g.memset(vm[:, :, :, :], 1.0).then_inc(S("filled"), 1)
            g.wait_ge(S("consts_in"), 16)
            g.wait_ge(S("weights_in"), 16)
            with g.Fori(0, QUADS) as q:
                pool_ln(g, 3 * q + 0)
                pool_gla(g, q)
                pool_ln(g, 3 * q + 1)
                pool_ln(g, 3 * q + 2)
            pool_scatter(g, 0)
            pool_gather(g, 0)
            with g.Fori(0, QUADS) as q:
                n = q + QUADS
                pool_ln(g, 3 * n + 0)
                pool_ln(g, 3 * n + 1)
                pool_ln(g, 3 * n + 2)
            pool_scatter(g, 1)
            pool_gather(g, 1)

        @block.scalar
        def _(a):
            a.wait_ge(S("consts_in"), 16)
            a.wait_ge(S("weights_in"), 16)
            with a.Fori(0, QUADS) as q:
                act_ln(a, 3 * q + 0, 0)
                act_gla(a, q)
                act_ln(a, 3 * q + 1, 0)
                act_xattn(a, q, q, 0)
                act_ln(a, 3 * q + 2, 0)
                act_router(a, q, q)
            act_sort(a, 0)
            act_experts(a, 0)
            with a.Fori(0, QUADS) as q:
                n = q + QUADS
                act_ln(a, 3 * n + 0, 0)
                act_mla(a, q)
                act_ln(a, 3 * n + 1, 0)
                act_xattn(a, n, q, 1)
                act_ln(a, 3 * n + 2, 0)
                act_router(a, n, q)
            act_sort(a, 1)
            act_experts(a, 1)

        @block.tensor
        def _(pe):
            pe.wait_ge(S("consts_in"), 16)
            pe.wait_ge(S("weights_in"), 16)
            pe.wait_ge(S("selections"), 8)
            with pe.Fori(0, QUADS) as q:
                pe_ln(pe, 3 * q + 0, 0)
                pe_gla(pe, q)
                pe_ln(pe, 3 * q + 1, 0)
                pe_xattn(pe, q, 0)
                pe_ln(pe, 3 * q + 2, 0)
                pe_router(pe, q, 0)
            pe_sort(pe, 0)
            pe_experts(pe, 0)
            with pe.Fori(0, QUADS) as q:
                n = q + QUADS
                pe_ln(pe, 3 * n + 0, 0)
                pe_mla(pe, q)
                pe_ln(pe, 3 * n + 1, 0)
                pe_xattn(pe, n, 1)
                pe_ln(pe, 3 * n + 2, 0)
                pe_router(pe, n, 1)
            pe_sort(pe, 1)
            pe_experts(pe, 1)

        @block.vector
        def _(v):
            v.wait_ge(S("filled"), 1)
            v.wait_ge(S("consts_in"), 16)
            v.wait_ge(S("weights_in"), 16)
            v.wait_ge(S("cleared"), 2)
            v.tensor_copy(ident_b[:, :], ident).then_inc(S("selections"), 1)
            dims = ident.rearrange("p (h d) -> p h d", h=XH)
            for slot, (qp, kp) in enumerate(zip(Q_PARTS, K_PARTS)):
                if qp is not None:
                    at = slice(slot * XD, (slot + 1) * XD)
                    v.tensor_copy(sel_qp[:, :, at], dims)
                    v.tensor_copy(sel_kp[:, kp, :, at], dims).then_inc(S("selections"), 1)
            v.wait_ge(S("mask_in"), 32)
            v.tensor_scalar(mask_bias[:, :], mask_row[0:1, :], 1.0, BIG, ALU.subtract, ALU.mult)\
             .then_inc(S("selections"), 1)
            with v.Fori(0, QUADS) as q:
                v.wait_ge(S("x_in"), (q + 1) * 16)
                dve_ln(v, 3 * q + 0)
                dve_gla(v, q)
                dve_ln(v, 3 * q + 1)
                dve_xattn(v, q, q, 0)
                dve_ln(v, 3 * q + 2)
                dve_router(v, q, q, 0)
            dve_sort(v, 0)
            v.wait_ge(S("mask_in"), 48)
            v.tensor_copy(mask_row[:, :], mask_i[:, :]).then_inc(S("mask1"), 1)
            v.wait_ge(S("mask1"), 1)
            m3 = mask_row[:, :].rearrange("p (b t) -> p b t", b=B)
            v.tensor_reduce(has[:, :], m3, AX.X, ALU.max).then_inc(S("mask1"), 1)
            v.wait_ge(S("mask1"), 2)
            v.tensor_scalar(nothas[:, :], has[:, :], -1.0, 1.0, ALU.mult, ALU.add).then_inc(S("mask1"), 1)
            v.wait_ge(S("mask1"), 3)
            v.tensor_tensor(m3[0:1], m3[0:1], nothas[0:1, :].unsqueeze(2).broadcast_to([1, B, T]), ALU.max)\
             .then_inc(S("mask1"), 1)
            v.wait_ge(S("mask1"), 4)
            v.tensor_scalar(mask_bias[:, :], mask_row[0:1, :], 1.0, BIG, ALU.subtract, ALU.mult)\
             .then_inc(S("mask1"), 1)
            dve_experts(v, 0)
            with v.Fori(0, QUADS) as q:
                n = q + QUADS
                dve_combine(v, q, 0)
                v.wait_ge(S("x_next"), q + 1)
                dve_ln(v, 3 * n + 0)
                dve_mla(v, q)
                dve_ln(v, 3 * n + 1)
                dve_xattn(v, n, q, 1)
                dve_ln(v, 3 * n + 2)
                dve_router(v, n, q, 1)
            dve_sort(v, 1)
            dve_experts(v, 1)
            with v.Fori(0, QUADS) as q:
                dve_combine(v, q, 1)


def constants():
    c = np.zeros((P, CN), np.float32)

    def put(name, a, r0=0):
        at, n = CC[name]
        a = np.asarray(a, np.float32)
        c[r0:r0 + a.shape[0], at:at + n] = a.reshape(a.shape[0], n)

    p = np.arange(P)
    put("ident", np.eye(P))
    put("chunk_mask", (p[:, None] <= p[None]) & (p[:, None] // CHUNK == p[None] // CHUNK))
    put("tri", p[:, None] < p[None])
    put("ones", np.ones((P, P)))
    k = np.arange(64)
    put("head_mask", k[:, None] // DK == np.arange(GH)[None])
    put("block_mask", k[:, None] // DK == (p // DV)[None])
    put("reset", np.broadcast_to(np.arange(QN) % CHUNK != 0, (64, QN)))
    lim = np.where(p[:, None] <= p[None], CLIP, -BIG)
    put("clip_mask", lim)
    inv = (np.float32(10000.0) ** (-np.arange(0, MR, 2, dtype=np.float32) / MR)).astype(np.float32)
    ang = np.arange(T, dtype=np.float32)[None] * inv[:, None]
    cos, sin = np.cos(ang).astype(np.float32), np.sin(ang).astype(np.float32)
    r = np.arange(MR)
    cos4, sin4 = cos[r // 2], sin[r // 2] * np.where(r % 2 == 0, -1.0, 1.0)[:, None]
    lat = np.zeros((P, T), np.float32)
    lat[0:64] = 1.0
    lat[64:64 + MR], lat[96:96 + MR] = cos4, sin4
    put("lat_rope", lat)
    put("q_rope", np.concatenate([np.tile(cos4, (MH, 1)), np.tile(sin4, (MH, 1))]))
    sel = np.zeros((P, XG, P), np.float32)
    for h in range(XH):
        for d in range(XD):
            sel[STRIP * (h % 4) + d, h // 4, h * XD + d] = 1.0
    put("sel_out", sel)
    sel = np.zeros((P, P), np.float32)
    for s in range(4):
        sel[STRIP * s + XD, STRIP * s:STRIP * s + XD] = 1.0
    put("sel_den", sel)
    sel = np.zeros((P, MG, P), np.float32)
    for h in range(MH):
        for d in range(MR):
            for half in range(2):
                sel[64 * half + h * MR + d, h // 4, STRIP * (h % 4) + MD + d] = 1.0
    put("sel_rope", sel)
    e = np.arange(EXP)
    put("iota8", np.broadcast_to(e, (P, EXP)))
    put("iota8m", np.broadcast_to(e - EXP, (P, EXP)))
    put("slot_iota", np.broadcast_to(np.arange(SLOTS), (P, SLOTS)))
    put("scan_reset", np.broadcast_to(np.arange(P) % TILES != 0, (P, P)))
    put("neg_half", np.full((P, 32), -0.5))
    put("eps", np.full((P, 32), EPS))
    put("tile_starts", np.broadcast_to(P * np.arange(TILES), (P, TILES)))
    put("q_one", p[:, None] == ROW_BIAS)
    put("k_ones", (p[:, None] >= ROW_MAX) & (p[:, None] < ROW_MAX + 3))
    return c


def weights(I):
    w = np.zeros((P, WN), np.float32)

    def put(name, a):
        at, n = WC[name]
        w[0:a.shape[0], at:at + n] = a.reshape(a.shape[0], n)

    def strips(m, heads, size, rows=P, r0=0):
        out = np.zeros((rows, heads // 4, 4, STRIP), np.float32)
        out[r0:r0 + m.shape[0], :, :, 0:size] = m.reshape(m.shape[0], heads // 4, 4, size)
        return out.reshape(rows, heads // 4, P)

    def strip_rows(m, heads, size):
        out = np.zeros((4, STRIP, heads // 4, m.shape[1]), np.float32)
        out[:, 0:size] = m.reshape(heads // 4, 4, size, -1).transpose(1, 2, 0, 3)
        return out.reshape(P, heads // 4, -1)

    swap = np.arange(MR) ^ 1
    put("wq", I["L0_attn_Wq"])
    put("wk", I["L0_attn_Wk"])
    put("wv", I["L0_attn_Wv"])
    put("wg", I["L0_attn_Wg"])
    put("wgk1", I["L0_attn_Wgk1"])
    put("wgk2", I["L0_attn_Wgk2"])
    put("bgk", I["L0_attn_bgk2"][:, None])
    put("norm_w", np.broadcast_to(I["L0_attn_norm_w"], (P, DV)))
    put("wo", I["L0_attn_Wo"])
    put("x_q", I["L0_xattn_W_tgt"].T)
    src = I["L0_xattn_W_src"]
    kt = src[0:D].T
    put("x_k", np.stack([kt[0:P], kt[P:]], 1))
    put("x_v", np.stack([src[D:].T[0:P], src[D:].T[P:]], 1))
    put("x_qb", I["L0_xattn_b_tgt"][:, None])
    put("x_kb", I["L0_xattn_b_src"][0:D, None])
    put("x_vb", I["L0_xattn_b_src"][None, D:])
    wo = I["L0_xattn_W_out"].T
    put("x_out", np.concatenate([wo[0:P, None], strip_rows(wo[P:], XH, XD)], 1))
    put("x_ob", I["L0_xattn_b_out"][None])
    put("r0_w", I["L0_ffn_router_w"])
    put("r0_b", np.broadcast_to(I["L0_ffn_router_b"], (P, EXP)))
    m = np.zeros((P, P), np.float32)
    m[:, 0:ML], m[:, ML:2 * ML] = I["L1_attn_W_DQ"], I["L1_attn_W_DKV"]
    m[:, 64:64 + MR], m[:, 96:96 + MR] = I["L1_attn_W_KR"], I["L1_attn_W_KR"][:, swap]
    put("m_lat", m)
    qr = I["L1_attn_W_QR"].reshape(ML, MH, MR)
    put("m_qr", np.concatenate([qr.reshape(ML, -1), qr[:, :, swap].reshape(ML, -1)], 1))
    put("m_q", strips(I["L1_attn_W_UQ"], MH, MD))
    mk = strips(I["L1_attn_W_UK"], MH, MD, r0=ML).reshape(P, MG, 4, STRIP)
    for d in range(MR):
        mk[64 + d, :, :, MD + d] = 1.0
        mk[96 + d, :, :, MD + d] = 1.0
    put("m_k", mk)
    m = np.zeros((P, P), np.float32)
    m[ML:2 * ML] = I["L1_attn_W_UV"]
    put("m_v", m)
    put("m_o", strip_rows(I["L1_attn_W_O"], MH, MD))
    put("x1_b", np.broadcast_to(I["L1_xattn_b"], (P, 1)))
    put("r1_w", I["L1_ffn_w_gate"])
    put("r1_b", np.broadcast_to(I["L1_ffn_b_gate"], (P, EXP)))
    put("b1", I["L1_ffn_b1"].reshape(EXP, 4, P).transpose(2, 0, 1))
    put("b2", np.broadcast_to(I["L1_ffn_b2"].reshape(1, -1), (P, EXP * D)))
    return w


def kernel(**inputs):
    import numpy as np
    import concourse.bacc as bacc
    from concourse import mybir
    from concourse.bass_utils import run_bass_kernel_spmd

    I = {k: np.asarray(v) for k, v in inputs.items()}
    ctx = I["ctx_2048"].reshape(TILES, P, DC)
    ctxT = I["ctx_2048"].reshape(B * T, 2, P).transpose(2, 1, 0)
    arrays = {
        "x": I["x"].reshape(TILES, P, D).transpose(1, 0, 2),
        "ctxT": ctxT,
        "ctxv": ctx[:, :, D:].transpose(1, 0, 2),
        "mask": I["mask_BxS2_fk1"].reshape(1, B * T),
        "mask_col": I["mask_BxS2_fk1"].reshape(TILES, P).T,
        "mask_i": I["mask_BxS2_ik0"].reshape(1, B * T),
        "w1_0": I["L0_ffn_w1"].transpose(1, 0, 2).reshape(P, -1),
        "w2_0": I["L0_ffn_w2"].reshape(EXP, 4, P, D).transpose(2, 0, 1, 3).reshape(P, -1),
        "w1_1": I["L1_ffn_W1"].transpose(1, 0, 2).reshape(P, -1),
        "w2_1": I["L1_ffn_W2"].reshape(EXP, 4, P, D).transpose(2, 0, 1, 3).reshape(P, -1),
        "consts": constants(),
        "weights": weights(I),
    }
    nc = bacc.Bacc("TRN2", target_bir_lowering=False, num_devices=1)
    feed, A = {}, {}
    for name, a in arrays.items():
        a = np.ascontiguousarray(a)
        feed["in_" + name] = a
        A[name] = nc.dram_tensor("in_" + name, a.shape, mybir.dt.from_np(a.dtype), kind="ExternalInput").ap()
    for name in ("sorted_x", "sorted_y"):
        A[name] = nc.dram_tensor(name, (SLOTS * P, D), mybir.dt.float32, kind="Internal").ap()
    A["out"] = nc.dram_tensor("out_x", (P, TILES, D), mybir.dt.float32, kind="ExternalOutput").ap()
    build(nc, A)
    r = run_bass_kernel_spmd(nc, [feed], core_ids=[0])
    out = r.results[0]["out_x"]
    return out.transpose(1, 0, 2).reshape(B, T, D)
```

```python
import numpy as np
import concourse.bass as bass
from concourse import mybir
from contextlib import ExitStack

FP32 = mybir.dt.float32
BF16 = mybir.dt.bfloat16
I32 = mybir.dt.int32
U32 = mybir.dt.uint32
ALU = mybir.AluOpType
ACT = mybir.ActivationFunctionType
AX = mybir.AxisListType

B, T, D, DC = 8, 256, 128, 256
P = 128
TILES = B * T // P
QT = 4
QN = QT * P
QUADS = TILES // QT
QB = QN // T
CHUNK = 64
GH, DK, DV = 8, 8, 16
XH, XD = 8, 16
STRIP = 32
XG = XH // 4
Q_PARTS = (0, 0, 0, None, 1, 1, 2)
K_PARTS = (0, 1, 2, None, 0, 1, 0)
SLOT_ROWS = len(Q_PARTS) * XD
ROW_BIAS = 3 * XD
ROW_MAX = ROW_BIAS + 1
MH, MD, MR, ML = 16, 8, 4, 32
MG = MH // 4
EXP, F = 8, 512
SLOTS = 24
EPS = 1e-5
LN_EXP, SILU, SQRT = "natural_log_exp_and_others", "silu_and_others", "sqrt_and_others"
BIG = 1e30
CLIP = 80.0

X_COLS, M_COLS = D + XH, D + MH


CONST_PLAN = [("ident", 128), ("chunk_mask", 128), ("tri", 128), ("ones", 128), ("head_mask", 8),
              ("block_mask", 128), ("reset", 512), ("x_sel", XG * X_COLS), ("iota8", 8),
              ("iota8m", 8), ("slot_iota", SLOTS), ("scan_reset", 128), ("neg_half", 32), ("eps", 32),
              ("tile_starts", TILES), ("q_one", 1), ("k_ones", 1),
              ("clip_mask", 128), ("lat_rope", 256), ("q_rope", 256), ("m_sel", MG * M_COLS), ("sel_rope", MG * 128)]
WEIGHT_PLAN = [("wq", 128), ("wk", 128), ("wv", 128), ("wg", 128), ("wgk1", 128), ("wgk2", 128), ("bgk", 1),
               ("norm_w", 16), ("wo", 128), ("x_q", 128), ("x_k", 2 * 128), ("x_v", 2 * 128),
               ("x_qb", 1), ("x_kb", 1), ("x_vb", 128), ("x_out", 2 * 128), ("x_ob", 128),
               ("r0_w", EXP), ("r0_b", EXP), ("m_lat", 128), ("m_qr", 128), ("m_q", MG * 128),
               ("m_k", MG * 128), ("m_v", 128), ("m_o", 128), ("x1_b", 1), ("r1_w", EXP), ("r1_b", EXP),
               ("b1", EXP * 4), ("b2", EXP * D)]


def columns(plan):
    at, out = 0, {}
    for name, n in plan:
        out[name] = (at, n)
        at += n
    return out, at


CC, CN = columns(CONST_PLAN)
WC, WN = columns(WEIGHT_PLAN)
C_LATE, W_LATE = CC["clip_mask"][0], WC["m_lat"][0]


def build(nc, A):
    ctx = ExitStack()
    with ctx:
        def sb(name, shape, dt=FP32):
            return ctx.enter_context(nc.sbuf_tensor(name, shape, dt))

        sems = {}

        def S(name):
            if name not in sems:
                sems[name] = ctx.enter_context(nc.semaphore(name))
            return sems[name]

        cst = sb("cst", [P, CN])
        wts = sb("wts", [P, WN])

        def C(name, rows=P, r0=0):
            a, n = CC[name]
            return cst[r0:r0 + rows, a:a + n]

        def W(name, rows=P, r0=0):
            a, n = WC[name]
            return wts[r0:r0 + rows, a:a + n]

        x_all = sb("x_all", [P, TILES, D])
        xn_all = sb("xn_all", [P, TILES, D])
        xq = sb("xq", [P, QT, D])
        xn = sb("xn", [P, QT, D])
        xnT = sb("xnT", [P, QN])
        unused = sb("unused", [P, 1])
        stats = sb("stats", [P, QT, 6])
        mv = sb("mv", [P, QT, 2])
        ve = sb("ve", [P, QT])
        rstd = sb("rstd", [P, QT])
        qe = sb("qe", [P, QT, CHUNK])
        ke_bd = sb("ke_bd", [P, QT, P])
        kdn = sb("kdn", [P, QT, P])
        vg = sb("vg", [P, QT, D])
        gate = sb("gate", [P, QT, D])
        qe_bd = sb("qe_bd", [P, 2, GH, CHUNK])
        am = sb("am", [P, 2, GH, P])
        st = sb("st", [P, 3, QB, D])
        o_sb = sb("o_sb", [P, QT, D])
        o_sq = sb("o_sq", [P, QT, D])
        ss = sb("ss", [P, QT * GH])
        rs = sb("rs", [P, QT * GH])
        oT = sb("oT", [P, QN])
        ctxT = sb("ctxT", [P, 2, QN])
        mask_row = sb("mask_row", [P, B * T])
        mask_bias = sb("mask_bias", [1, B * T], BF16)
        mask_col = sb("mask_col", [P, TILES])
        has = sb("has", [P, B])
        nothas = sb("nothas", [P, B])
        mask_i = mask_row[:, :].bitcast(I32)
        qa = sb("qa", [P, MG, QN])
        ka = sb("ka", [P, MG, QN])
        vm = sb("vm", [P, QT, MH, STRIP])
        vx = vm[:, :, 0:XH, :]
        xv = (vm[:, :, XH:2 * XH, :], vx)
        pT = sb("pT", [P, 3, 1024])
        ident_b = sb("ident_b", [P, P], BF16)
        sel_qp = sb("sel_qp", [P, XH, P], BF16)
        sel_kp = sb("sel_kp", [P, 3, XH, P], BF16)
        q_parts = sb("q_parts", [P, 3, QN], BF16)
        k_parts = sb("k_parts", [P, 3, QN], BF16)
        qs, ks0 = (t[:, :, :].rearrange("p g t -> p (g t)").bitcast(BF16).rearrange("p (h t) -> p h t", h=XH)
                   for t in (qa, ka))
        neg_max = sb("neg_max", [P, QT, XH])
        nm_rest = sb("nm_rest", [P, QT, XH])
        nm_parts = sb("nm_parts", [P, QT, 3, XH], BF16)
        nm_rows = sb("nm_rows", [3 * XH, QN], BF16)
        lr, absz, negz, cum = (
            pT[0:rows, c // 2, c % 2 * QN:(c % 2 + 1) * QN] for c, rows in enumerate((P, P, P, P)))
        eb, enb, ke, kd = (qa[:, g, :] for g in range(MG))
        lat, tq, xo0, xo1 = (t[:, :, :].rearrange("p a b -> p (a b)") for t in (gate, vg, o_sb, o_sq))
        rden = sb("rden", [P, QT, MH])
        on = (xo0, xo1)
        kf, qf = xo0, xo1
        rest = {"k": lat, "q": tq}
        cl = am[:, :, :, :].rearrange("p a h i -> p a (h i)")
        lg = sb("lg", [P, TILES, EXP])
        lmax = sb("lmax", [P, TILES])
        lex = sb("lex", [P, TILES, EXP])
        lsum = sb("lsum", [P, TILES])
        prob = sb("prob", [P, TILES])
        amin = sb("amin", [P, TILES])
        onehot = sb("onehot", [P, TILES, EXP])
        tie = sb("tie", [P, TILES, EXP])
        cnt = sb("cnt", [P, EXP, TILES])
        incl = sb("incl", [P, EXP, TILES])
        more = sb("more", [P, EXP, TILES])
        ntile = sb("ntile", [P, EXP])
        ends = sb("ends", [P, EXP])
        starts = sb("starts", [P, EXP])
        pos_f = sb("pos_f", [P, TILES])
        pos = sb("pos", [P, TILES], U32)
        slot_ge = sb("slot_ge", [P, SLOTS, EXP])
        slot_f = sb("slot_f", [P, SLOTS])
        slot_e = sb("slot_e", [P, SLOTS])
        turn_e = sb("turn_e", [P, SLOTS // 4], I32)
        zeros = sb("zeros", [P, D])
        w1 = sb("w1", [P, EXP * 2 * F])
        w2 = sb("w2", [P, EXP * 4 * D])
        ks1 = w2[:, 4 * QN:8 * QN].bitcast(BF16).rearrange("p (h t) -> p h t", h=XH)
        ks = (ks0, ks1)
        w1b, w2b = w1[:, 0:EXP * F], w1[:, EXP * F:2 * EXP * F]
        hidT = pT[:, 0, :].rearrange("p (s f) -> p s f", s=2)
        xs, xsT, ys = (pT[:, 1 + k // 2, k % 2 * 512:(k % 2 + 1) * 512].rearrange("p (s d) -> p s d", s=4)
                       for k in range(3))
        act_a = am[:, 0, :, :].rearrange("p h i -> p (h i)").rearrange("p (s f) -> p s f", s=2)
        hid = am[:, 1, :, :].rearrange("p h i -> p (h i)").rearrange("p (s f) -> p s f", s=2)
        ps = ctx.enter_context(nc.psum_tensor("ps", [P, 8, 512], FP32))

        def bank(b, rows=P, r0=0):
            return ps[r0:r0 + rows, b, :]

        ident = C("ident")
        block = ctx.enter_context(nc.Block())

        def tri3(ap, k):
            return ap.rearrange("p (a b) -> p a b", a=k)

        def dve_wait(v, sem, value):
            v.wait_ge(sem, value)
            v.memset(unused[0:1, 0:1], 0.0)

        def dve_ln(v, n, meanwhile=None):
            for j in range(QT):
                v.bn_stats(stats[:, j, :], xq[:, j, :]).then_inc(S("ln_stats"), 1)
            dve_wait(v, S("ln_stats"), (n + 1) * QT)
            for j in range(QT):
                i = v.bn_aggr(mv[:, j, :], stats[:, j, :])
            i.then_inc(S("ln_mv"), 1)
            if meanwhile:
                meanwhile()
            v.wait_ge(S("ln_rstd"), n + 1)
            v.wait_ge(S("ln_mv"), n + 1)
            for j in range(QT):
                v.tensor_scalar(xn[:, j, :], xq[:, j, :], mv[:, j, 0:1], rstd[:, j:j + 1],
                                ALU.subtract, ALU.mult).then_inc(S("ln_xn"), 1)

        def pool_ln(g, n):
            g.wait_ge(S("ln_mv"), n + 1)
            g.tensor_tensor(ve[:, :], mv[:, :, 1], C("eps")[:, 0:QT], ALU.add).then_inc(S("ln_ve"), 1)
            g.wait_ge(S("ln_ve"), n + 1)
            g.tensor_tensor(rstd[:, :], ve[:, :], C("neg_half")[:, 0:QT], ALU.pow).then_inc(S("ln_rstd"), 1)

        def pe_ln(pe, n, b):
            for j in range(QT):
                pe.wait_ge(S("ln_xn"), n * QT + j + 1)
                i = pe.transpose(bank(b)[:, j * P:(j + 1) * P], xn[:, j, :], ident)
            i.then_inc(S("ln_xnT_ps"), 1)

        def act_ln(a, n, b):
            a.wait_ge(S("ln_xnT_ps"), n + 1)
            a.activation(xnT[:, :], bank(b), ACT.Copy).then_inc(S("ln_xnT"), 1)

        def pe_gla(pe, n):
            pe.wait_ge(S("ln_xnT"), 3 * n + 1)
            pe.matmul(bank(3), W("wgk1"), xnT[:, :], start=True, stop=True).then_inc(S("lr_ps"), 1)
            pe.matmul(bank(1), W("wq"), xnT[:, :], start=True, stop=True).then_inc(S("q_ps"), 1)
            pe.wait_ge(S("lr_sb"), n + 1)
            pe.matmul(bank(4), W("wgk2"), lr[:, :], start=True, stop=True).then_inc(S("z_ps"), 1)
            pe.matmul(bank(2), W("wk"), xnT[:, :], start=True, stop=True).then_inc(S("k_ps"), 1)
            pe.wait_ge(S("xva"), n + 1)
            for w, b, s in (("wv", 5, "v_ps"), ("wg", 6, "g_ps")):
                for j in range(QT):
                    i = pe.matmul(bank(b)[:, j * P:(j + 1) * P], xnT[:, j * P:(j + 1) * P], W(w),
                                  start=True, stop=True)
                i.then_inc(S(s), 1)
            pe.wait_ge(S("kd"), n + 1)
            for j in range(QT):
                i = pe.transpose(bank(3)[:, j * P:(j + 1) * P], kd[:, j * P:(j + 1) * P], ident)
            i.then_inc(S("kdT_ps"), 1)

            def scores(j):
                pe.wait_ge(S("qe_bd"), n * QT + j + 1)
                if j == 3:
                    pe.wait_ge(S("kdn"), n + 1)
                pe.matmul(bank(j), ke_bd[:, j, :], qe_bd[:, j % 2, :, :], start=True, stop=True)\
                  .then_inc(S("sc_ps"), 1)

            def outputs(j):
                b, t = j // 2, j % 2
                pe.wait_ge(S("am"), 2 * (n * QT + j + 1))
                if j == 2:
                    pe.wait_ge(S("silu"), n + 1)
                for h in range(GH):
                    i = pe.matmul(bank(5 + b, STRIP, STRIP * (h % 4))[:, h // 4 * T + t * P:h // 4 * T + (t + 1) * P],
                                  vx[:, j, h, :], am[:, j % 2, h, :], start=True, stop=True, skip_group_check=True)
                i.then_inc(S("o_ps"), 1)

            def to_tokens(b):
                pe.wait_ge(S("go"), QB * n + b + 1)
                if b == 0:
                    pe.wait_ge(S("st"), 2 * (n + 1))
                for t in range(2):
                    cols = slice(t * P, (t + 1) * P)
                    for g in range(2):
                        pe.matmul(bank(4 + 3 * b)[:, cols], go[b][:, g * T + t * P:g * T + (t + 1) * P],
                                  C("x_sel")[:, g * X_COLS:g * X_COLS + D], start=(g == 0), stop=False,
                                  skip_group_check=True)
                    for c in range(max(2 * t, 1), 2 * t + 2):
                        r = CHUNK * (c % 2)
                        i = pe.matmul(bank(4 + 3 * b)[r:r + CHUNK, cols], qe[r:r + CHUNK, 2 * b + t, :],
                                      st[r:r + CHUNK, c - 1, b, :], start=False, stop=True, skip_group_check=True)
                i.then_inc(S("o_tokens"), 1)

            pe.wait_ge(S("ke_bd"), n + 1)
            scores(0)
            pe.wait_ge(S("kdn"), n + 1)
            pe.wait_ge(S("v_sb"), n + 1)
            for c in range(3):
                for b in range(QB):
                    j, r = 2 * b + c // 2, CHUNK * (c % 2)
                    out = bank(4)[:, (c // 2 * QB + b) * D:(c // 2 * QB + b + 1) * D] if c % 2 == 0 \
                        else bank(7)[:, b * D:(b + 1) * D]
                    i = pe.matmul(out, kdn[r:r + CHUNK, j, :], vx[r:r + CHUNK, j, :, 0:DV], start=True, stop=True)
            i.then_inc(S("u_ps"), 1)
            scores(1)
            for j in range(QT):
                outputs(j)
                if j + 2 < QT:
                    scores(j + 2)
                if j == 2:
                    to_tokens(0)
            to_tokens(1)
            for b in range(QB):
                pe.wait_ge(S("og"), QB * n + b + 1)
                for t in range(2):
                    i = pe.transpose(bank(b)[:, t * P:(t + 1) * P], o_sb[:, 2 * b + t, :], ident)
                i.then_inc(S("goT_ps"), 1)
                pe.wait_ge(S("goT"), QB * n + b + 1)
                for t in range(2):
                    j = 2 * b + t
                    i = pe.matmul(bank(2 + b)[:, t * P:(t + 1) * P], oT[:, j * P:(j + 1) * P], W("wo"),
                                  start=True, stop=True)
                i.then_inc(S("gla_ps"), 1)

        go = (tq, xo1)

        def chunks(ap, odd):
            return ap.rearrange("p (j c t) -> p j c t", c=2, t=CHUNK)[:, :, odd, :]

        def act_gla(a, n):
            a.wait_ge(S("lr_ps"), n + 1)
            a.activation(lr[:, :], bank(3), ACT.Copy).then_inc(S("lr_sb"), 1)
            a.wait_ge(S("z_ps"), n + 1)
            a.activation(absz, bank(4), ACT.Abs, bias=W("bgk")).then_inc(S("absz"), 1)
            a.wait_ge(S("absz"), n + 1)
            a.activation(absz, absz, ACT.Exp, scale=-1.0).then_inc(S("expz"), 1)
            a.wait_ge(S("expz"), n + 1)
            a.activation(absz, absz, ACT.Ln, bias=1.0).then_inc(S("lnz"), 1)
            a.wait_ge(S("v_ps"), n + 1)
            a.activation(vx[:, :, :, 0:DV], bank(5).rearrange("p (a h d) -> p a h d", a=QT, h=GH),
                         ACT.Copy).then_inc(S("v_sb"), 1)
            a.wait_ge(S("cum"), n + 1)
            a.activation(eb, cum, ACT.Exp, scale=1.0 / 16).then_inc(S("eb"), 1)
            a.activation(enb, cum, ACT.Exp, scale=-1.0 / 16).then_inc(S("enb"), 1)
            a.wait_ge(S("ke"), n + 1)
            for odd in range(2):
                r = odd * CHUNK
                i = a.activation(ke_bd[r:r + CHUNK, :, r:r + CHUNK], chunks(ke[r:r + CHUNK, :], odd), ACT.Copy)
            i.then_inc(S("ke_bd"), 1)
            a.wait_ge(S("kdT_ps"), n + 1)
            a.activation(kdn[:, :, :], tri3(bank(3), QT), ACT.Copy).then_inc(S("kdn"), 1)
            a.wait_ge(S("g_ps"), n + 1)
            a.activation(gate[:, :, :], tri3(bank(6), QT), ACT.Silu).then_inc(S("silu"), 1)
            a.preload_act_table_set(SQRT)
            for b in range(QB):
                a.wait_ge(S("o_ps"), n * QT + 2 * b + 2)
                a.activation(go[b], bank(5 + b), ACT.Copy).then_inc(S("go"), 1)
            for b in range(QB):
                t = slice(2 * b, 2 * b + 2)
                a.wait_ge(S("o_tokens"), QB * n + b + 1)
                a.activation(sq[:, t, :], bank(4 + 3 * b)[:, 0:T].rearrange("p (a d) -> p a d", a=2), ACT.Square,
                             scale=float(DV) ** -0.5).then_inc(S("o_sq"), 1)
            for b in range(QB):
                hs = slice(2 * b * GH, 2 * (b + 1) * GH)
                a.wait_ge(S("ss"), QB * n + b + 1)
                a.activation(ss[:, hs], ss[:, hs], ACT.Sqrt, bias=C("eps")[:, 0:1]).then_inc(S("rms"), 1)
            for b in range(QB):
                a.wait_ge(S("goT_ps"), QB * n + b + 1)
                a.activation(oT[:, b * T:(b + 1) * T], bank(b)[:, 0:T], ACT.Copy).then_inc(S("goT"), 1)
            a.preload_act_table_set(LN_EXP)

        sq = kd.rearrange("p (a d) -> p a d", a=QT)

        def dve_gla(v, n):
            v.wait_ge(S("absz"), n + 1)
            v.tensor_scalar(negz, bank(4), W("bgk"), 0.0, ALU.add, ALU.min).then_inc(S("negz"), 1)
            v.wait_ge(S("lnz"), n + 1)
            v.wait_ge(S("negz"), n + 1)
            v.tensor_tensor(negz, negz, absz, ALU.subtract).then_inc(S("gk"), 1)
            v.wait_ge(S("gk"), n + 1)
            v.tensor_tensor_scan(cum, C("reset"), negz, 0.0, ALU.mult, ALU.add).then_inc(S("cum"), 1)
            v.wait_ge(S("eb"), n + 1)
            v.wait_ge(S("q_ps"), n + 1)
            for odd in range(2):
                r = odd * CHUNK
                i = v.scalar_tensor_tensor(qe[r:r + CHUNK, :, :], chunks(bank(1, CHUNK, r), odd), float(DK) ** -0.5,
                                           chunks(eb[r:r + CHUNK, :], odd), ALU.mult, ALU.mult)
            i.then_inc(S("qe"), 1)
            v.wait_ge(S("enb"), n + 1)
            v.wait_ge(S("k_ps"), n + 1)
            v.tensor_tensor(ke, bank(2), enb, ALU.mult).then_inc(S("ke"), 1)
            v.wait_ge(S("ke"), n + 1)
            eb3 = eb.rearrange("p (c t) -> p c t", t=CHUNK)
            last = eb3[:, :, CHUNK - 1:CHUNK].broadcast_to([P, QN // CHUNK, CHUNK])
            v.tensor_tensor(kd.rearrange("p (c t) -> p c t", t=CHUNK),
                            ke.rearrange("p (c t) -> p c t", t=CHUNK), last, ALU.mult).then_inc(S("kd"), 1)

            def masked(j):
                v.wait_ge(S("sc_ps"), n * QT + j + 1)
                if j >= 2:
                    v.wait_ge(S("o_ps"), n * QT + j - 1)
                for r in (0, CHUNK):
                    v.tensor_tensor(am[r:r + CHUNK, j % 2, :, r:r + CHUNK],
                                    bank(j, CHUNK, r).rearrange("p (h i) -> p h i", h=GH),
                                    C("chunk_mask", CHUNK, r)[:, r:r + CHUNK].unsqueeze(1)
                                    .broadcast_to([CHUNK, GH, CHUNK]), ALU.mult).then_inc(S("am"), 1)

            masked(0)
            v.wait_ge(S("u_ps"), n + 1)
            bd = C("block_mask").unsqueeze(1).broadcast_to([P, QB, D])
            for c in range(3):
                u = bank(4)[:, c // 2 * QB * D:(c // 2 + 1) * QB * D] if c % 2 == 0 else bank(7)[:, 0:QB * D]
                v.tensor_tensor(st[:, c, :, :], u.rearrange("p (b d) -> p b d", b=QB), bd, ALU.mult)\
                 .then_inc(S("st_u"), 1)
            v.wait_ge(S("st_u"), 3 * (n + 1))
            for c in range(1, 3):
                if c == 2:
                    v.wait_ge(S("st"), 2 * n + 1)
                for b in range(QB):
                    k = b * (T // CHUNK) + c
                    i = v.scalar_tensor_tensor(st[:, c, b, :], st[:, c - 1, b, :],
                                               eb3[:, k, CHUNK - 1:CHUNK],
                                               st[:, c, b, :], ALU.mult, ALU.add)
                i.then_inc(S("st"), 1)
            for j in range(1, QT):
                masked(j)
            for b in range(QB):
                t, hs = slice(2 * b, 2 * b + 2), slice(2 * b * GH, 2 * (b + 1) * GH)
                v.wait_ge(S("o_sq"), QB * n + b + 1)
                v.tensor_reduce(ss[:, hs], sq[:, t, :].rearrange("p a (h d) -> p (a h) d", d=DV), AX.X, ALU.add)\
                 .then_inc(S("ss"), 1)
            for b in range(QB):
                t, hs = slice(2 * b, 2 * b + 2), slice(2 * b * GH, 2 * (b + 1) * GH)
                v.wait_ge(S("rms"), QB * n + b + 1)
                v.reciprocal(rs[:, hs], ss[:, hs]).then_inc(S("rs"), 1)
                v.wait_ge(S("rs"), QB * n + b + 1)
                v.tensor_tensor(o_sb[:, t, :].rearrange("p a (h d) -> p (a h) d", d=DV),
                                bank(4 + 3 * b)[:, 0:T].rearrange("p (k d) -> p k d", d=DV),
                                rs[:, hs].unsqueeze(2).broadcast_to([P, 2 * GH, DV]), ALU.mult)\
                 .then_inc(S("on"), 1)
                v.wait_ge(S("on"), QB * n + b + 1)
                v.wait_ge(S("gw"), n + 1)
                v.tensor_tensor(o_sb[:, t, :], o_sb[:, t, :], gate[:, t, :], ALU.mult).then_inc(S("og"), 1)
            for b in range(QB):
                xb = xq[:, 2 * b:2 * b + 2, :]
                v.wait_ge(S("gla_ps"), QB * n + b + 1)
                v.tensor_tensor(xb, xb, bank(2 + b)[:, 0:T].rearrange("p (a d) -> p a d", a=2), ALU.add)\
                 .then_inc(S("x1"), 1)
            v.wait_ge(S("x1"), QB * (n + 1))

        def pool_gla(g, n):
            g.wait_ge(S("qe"), n + 1)
            for j in range(QT):
                if j >= 2:
                    g.wait_ge(S("sc_ps"), n * QT + j - 1)
                g.tensor_tensor(qe_bd[:, j % 2, :, :],
                                qe[:, j, :].unsqueeze(1).broadcast_to([P, GH, CHUNK]),
                                C("head_mask").unsqueeze(2).broadcast_to([P, GH, CHUNK]), ALU.mult)\
                 .then_inc(S("qe_bd"), 1)
            g.wait_ge(S("silu"), n + 1)
            g4 = gate[:, :, :].rearrange("p a (h d) -> p (a h) d", d=DV)
            g.tensor_tensor(g4, g4, W("norm_w").unsqueeze(1).broadcast_to([P, QT * GH, DV]), ALU.mult)\
             .then_inc(S("gw"), 1)

        UB = XH // 2
        UX = QB * UB

        def unit(e):
            return e // UB, 2 * (e % UB)

        ORDER = [("M", 0), ("M", 1), ("M", 2), ("M", 3), ("N", 0), ("M", 4), ("M", 5), ("E", 0), ("M", 6),
                 ("E", 1), ("M", 7), ("E", 2), ("N", 1), ("E", 3), ("E", 4), ("E", 5), ("E", 6), ("E", 7)]
        SCORES = [k for k in ORDER if k[0] != "N"]

        def pair(kind, e):
            return 2 * (SCORES.index((kind, e)) % 3)

        PACK_BANKS = {"k": (2, 4, 6, 7, 2, 4, 6, 7), "q": (6, 7, 4, 5, 6, 7, 6, 7)}

        def pe_project(pe, n):
            pe.wait_ge(S("ctx_in"), 16 * (n + 1))
            for half in range(2):
                i = pe.matmul(bank(3), W("x_k")[:, half * P:(half + 1) * P], ctxT[:, half, :],
                              start=(half == 0), stop=(half == 1))
            i.then_inc(S("xk_ps"), 1)
            for j in range(QT):
                o = bank(5)[:, j * P:(j + 1) * P]
                for half in range(2):
                    pe.matmul(o, ctxT[:, half, j * P:(j + 1) * P], W("x_v")[:, half * P:(half + 1) * P],
                              start=(half == 0), stop=False)
                i = pe.matmul(o, C("ones"), W("x_vb"), start=False, stop=True)
            i.then_inc(S("xv_ps"), 1)

        def pe_pack(pe, side, n, h):
            banks = PACK_BANKS[side]
            if h == 0:
                pe.wait_ge(S(side + "_part2"), n + 1)
            if banks[h] in banks[:h]:
                last = max(k for k in range(h) if banks[k] == banks[h])
                pe.wait_ge(S(side + "_slots"), XH * n + last + 1)
            if side == "q":
                for part, (lo, rows) in enumerate(((0, 64), (64, 32), (96, 16))):
                    i = pe.matmul(bank(banks[h], rows, lo), sel_qp[:, h, lo:lo + rows], q_parts[:, part, :],
                                  start=True, stop=True)
            else:
                for part in range(3):
                    i = pe.matmul(bank(banks[h]), sel_kp[:, part, h, :], k_parts[:, part, :],
                                  start=(part == 0), stop=(part == 2))
            i.then_inc(S(side + "_slots_ps"), 1)

        def pe_keys(pe, n):
            for h in range(XH):
                pe_pack(pe, "k", n, h)

        def pe_xattn(pe, n, layer):
            pe.wait_ge(S("ln_xnT"), 3 * n + 2)
            if layer == 0:
                pe.matmul(bank(1), W("x_q"), xnT[:, :], start=True, stop=True).then_inc(S("xq_ps"), 1)
            kl = ks[layer]

            def before(k):
                at = SCORES.index(k)
                if at == 0:
                    pe.wait_ge(S("mask_row_in"), 16 * (n + 1))
                if at < UB:
                    pe.wait_ge(S("q_slots"), XH * n + 2 * at + 2)
                if at >= 3:
                    kind, e = SCORES[at - 3]
                    pe.wait_ge(S("mx_read" if kind == "M" else "ex_read"), UX * n + e + 1)

            def max_scores(e):
                b, h0 = unit(e)
                before(("M", e))
                for jj in range(2):
                    for qt in range(2):
                        q0 = b * T + qt * P
                        i = pe.matmul(bank(pair("M", e) + jj)[:, qt * T:(qt + 1) * T],
                                      qs[0:SLOT_ROWS, h0 + jj, q0:q0 + P],
                                      kl[0:SLOT_ROWS, h0 + jj, b * T:(b + 1) * T], start=True, stop=True)
                i.then_inc(S("mx_ps"), 1)

            def exp_scores(e):
                b, h0 = unit(e)
                before(("E", e))
                if e % UB == 0:
                    pe.wait_ge(S("max_in"), 48 * (QB * n + b + 1))
                for jj in range(2):
                    for kt in range(2):
                        k0 = b * T + kt * P
                        i = pe.matmul(bank(pair("E", e) + jj)[:, kt * T:(kt + 1) * T],
                                      kl[0:SLOT_ROWS, h0 + jj, k0:k0 + P],
                                      qs[0:SLOT_ROWS, h0 + jj, b * T:(b + 1) * T], start=True, stop=True)
                i.then_inc(S("ex_ps"), 1)

            def max_rows(b):
                pe.wait_ge(S("nm_parts"), QB * n + b + 1)
                for t in range(2):
                    i = pe.matmul(bank(6 + b, 3 * XH)[:, t * P:(t + 1) * P],
                                  nm_parts[:, 2 * b + t, :, :].rearrange("p l h -> p (l h)"), ident_b[:, :],
                                  start=True, stop=True)
                i.then_inc(S("nm_ps"), 1)

            def values(e):
                b, h0 = unit(e)
                if e % UB == 0:
                    pe.wait_ge(S("nm_rows"), QB * n + b + 1)
                pe.wait_ge(S("ex_read"), UX * n + e + 1)
                if e == 0:
                    pe.wait_ge(S("xva"), n + 1)
                for jj in range(2):
                    g, r = (h0 + jj) // 4, STRIP * ((h0 + jj) % 4)
                    for kt in range(2):
                        i = pe.matmul(bank(6 + b, STRIP, r)[:, g * T:(g + 1) * T],
                                      xv[layer][:, 2 * b + kt, h0 + jj, :],
                                      pT[:, e % 3, jj * 512 + kt * T:jj * 512 + (kt + 1) * T],
                                      start=(kt == 0), stop=(kt == 1), skip_group_check=True)
                i.then_inc(S("pv"), 1)

            def to_tokens(b):
                pe.wait_ge(S("xo"), QB * n + b + 1)
                for t in range(2):
                    for g in range(XG):
                        i = pe.matmul(bank(2 + b)[:, t * X_COLS:(t + 1) * X_COLS],
                                      on[b][:, g * T + t * P:g * T + (t + 1) * P],
                                      C("x_sel")[:, g * X_COLS:(g + 1) * X_COLS], start=(g == 0), stop=(g == XG - 1))
                i.then_inc(S("x_tokens"), 1)

            for h in range(4):
                pe_pack(pe, "q", n, h)
            for kind, e in ORDER:
                if kind == "M":
                    max_scores(e)
                    if e < 2:
                        for h in range(2 * e + 4, 2 * e + 6):
                            pe_pack(pe, "q", n, h)
                elif kind == "N":
                    max_rows(e)
                else:
                    exp_scores(e)
                    if e >= 1:
                        values(e - 1)
            to_tokens(0)
            values(UX - 1)
            to_tokens(1)
            if layer == 0:
                for b in range(QB):
                    pe.wait_ge(S("xon"), QB * n + b + 1)
                    for t in range(2):
                        i = pe.transpose(bank(4 + b)[:, t * P:(t + 1) * P], gate[:, 2 * b + t, :], ident)
                    i.then_inc(S("xoT_ps"), 1)
                for b in range(QB):
                    pe.wait_ge(S("xoT"), QB * n + b + 1)
                    for t in range(2):
                        o, j = bank(b)[:, t * P:(t + 1) * P], 2 * b + t
                        pe.matmul(o, xnT[:, j * P:(j + 1) * P], W("x_out")[:, 0:P], start=True, stop=False)
                        pe.matmul(o, oT[:, j * P:(j + 1) * P], W("x_out")[:, P:2 * P], start=False, stop=False)
                        i = pe.matmul(o, C("ones"), W("x_ob"), start=False, stop=True)
                    i.then_inc(S("xout_ps"), 1)

        def act_parts(a, side, n, src, scale, ready, count):
            parts = q_parts if side == "q" else k_parts
            a.wait_ge(S(ready), count)
            a.activation(parts[:, 0, :], src, ACT.Copy, scale=scale).then_inc(S(side + "_part0"), 1)
            a.wait_ge(S(side + "_rest"), n + 1)
            a.activation(parts[:, 1, :], rest[side], ACT.Copy).then_inc(S(side + "_part1"), 1)

        def dve_rest(v, side, n, src, scale):
            parts = q_parts if side == "q" else k_parts
            v.wait_ge(S(side + "_part0"), n + 1)
            v.scalar_tensor_tensor(rest[side], src, scale, parts[:, 0, :], ALU.mult, ALU.subtract)\
             .then_inc(S(side + "_rest"), 1)

        def dve_last_part(v, side, n):
            parts = q_parts if side == "q" else k_parts
            v.wait_ge(S(side + "_rest"), n + 1)
            v.wait_ge(S(side + "_part1"), n + 1)
            v.tensor_tensor(parts[:, 2, :], rest[side], parts[:, 1, :], ALU.subtract)\
             .then_inc(S(side + "_part2"), 1)

        def act_slots(a, side, n, layer):
            out, ones = (qs, "q_one") if side == "q" else (ks[layer], "k_ones")
            for h in range(XH):
                a.wait_ge(S(side + "_slots_ps"), XH * n + h + 1)
                a.activation(out[0:SLOT_ROWS, h, :], bank(PACK_BANKS[side][h], SLOT_ROWS), ACT.Identity,
                             bias=C(ones, SLOT_ROWS)).then_inc(S(side + "_slots"), 1)

        def act_key_part(a, part, n, q, layer):
            if part == 1:
                a.wait_ge(S("k_rest"), n + 1)
                a.activation(k_parts[:, 1, :], rest["k"], ACT.Copy).then_inc(S("k_part1"), 1)
                return
            if layer == 0:
                a.wait_ge(S("kf"), n + 1)
            else:
                a.wait_ge(S("k_in"), 16 * (q + 1))
            a.activation(k_parts[:, 0, :], kf if layer == 0 else ctxT[:, 0, :], ACT.Copy)\
             .then_inc(S("k_part0"), 1)

        def dve_keys(v, n, q):
            v.wait_ge(S("xk_ps"), n + 1)
            v.scalar_tensor_tensor(kf, bank(3), W("x_kb"), mask_row[:, bass.ds(q * QN, QN)], ALU.add, ALU.mult)\
             .then_inc(S("kf"), 1)

        def dve_values(v, n, q):
            v.wait_ge(S("xv_ps"), n + 1)
            m = mask_col[:, bass.ds(q * QT, QT)].unsqueeze(2).unsqueeze(3).broadcast_to([P, QT, XH, XD])
            v.tensor_tensor(xv[0][:, :, :, 0:XD], bank(5).rearrange("p (a h d) -> p a h d", a=QT, h=XH), m,
                            ALU.mult).then_inc(S("xva"), 1)

        def pool_key_parts(g, n, q):
            g.wait_ge(S("k_part0"), n + 1)
            g.tensor_tensor(rest["k"], ctxT[:, 0, :], k_parts[:, 0, :], ALU.subtract).then_inc(S("k_rest"), 1)
            g.wait_ge(S("k_rest"), n + 1)
            g.wait_ge(S("k_part1"), n + 1)
            g.tensor_tensor(k_parts[:, 2, :], rest["k"], k_parts[:, 1, :], ALU.subtract)\
             .then_inc(S("k_part2"), 1)

        def act_xattn(a, n, q, layer):
            MX = QB * MH // 2
            act_parts(a, "q", n, qf, float(XD) ** -0.5, "qf", n + 1)
            act_slots(a, "q", n, layer)
            if layer == 1:
                a.wait_ge(S("v_in"), 16 * (q + 1))
                a.wait_ge(S("mpv"), MX * (q + 1))
                a.activation(vx[:, :, :, 0:XD], ctxT[:, 1, :].rearrange("p (a h d) -> p a h d", a=QT, h=XH),
                             ACT.Copy).then_inc(S("xva"), 1)

            def copy_values(b):
                a.wait_ge(S("pv"), UX * n + UB * (b + 1))
                a.activation(on[b], bank(6 + b), ACT.Copy).then_inc(S("xo"), 1)

            for kind, e in ORDER:
                if kind == "N":
                    a.wait_ge(S("nm_ps"), QB * n + e + 1)
                    a.activation(nm_rows[:, e * T:(e + 1) * T], bank(6 + e, 3 * XH)[:, 0:T], ACT.Copy)\
                     .then_inc(S("nm_rows"), 1)
                elif kind == "E":
                    if e >= 3:
                        a.wait_ge(S("pv"), UX * n + e - 2)
                    a.wait_ge(S("ex_ps"), UX * n + e + 1)
                    p = pair("E", e)
                    out, scores = pT[:, e % 3, :].rearrange("p (a b) -> p a b", a=2), ps[:, p:p + 2, :]
                    if layer == 0:
                        i = a.activation(out, scores, ACT.Exp)
                    else:
                        i = a.activation(out, scores, ACT.Exp, bias=W("x1_b"))
                    i.then_inc(S("ex_read"), 1)
                    if e == UB + 1:
                        copy_values(0)
            copy_values(1)
            if layer == 0:
                for b in range(QB):
                    a.wait_ge(S("xoT_ps"), QB * n + b + 1)
                    a.activation(oT[:, b * T:(b + 1) * T], bank(4 + b)[:, 0:T], ACT.Copy).then_inc(S("xoT"), 1)

        def dve_xattn(v, n, q, layer):
            cols = bass.ds(q * QN, QN)
            if layer == 0:
                v.wait_ge(S("xq_ps"), n + 1)
                v.scalar_tensor_tensor(qf, bank(1), W("x_qb"), mask_row[:, cols], ALU.add, ALU.mult)\
                 .then_inc(S("qf"), 1)
            else:
                v.wait_ge(S("ln_xnT"), 3 * n + 2)
                hb = has[:, bass.ds(q * QB, QB)].unsqueeze(2).broadcast_to([P, QB, T])
                v.tensor_tensor(tri3(qf, QB), tri3(xnT[:, :], QB), hb, ALU.mult).then_inc(S("qf"), 1)
            v.wait_ge(S("qf"), n + 1)
            dve_rest(v, "q", n, qf, float(XD) ** -0.5)
            dve_last_part(v, "q", n)
            STEPS = 4 + layer

            def minus_max(b):
                step = [layer * 4 * QB * QUADS + STEPS * (QB * q + b)]

                def done(i):
                    step[0] += 1
                    i.then_inc(S("nm_step"), 1)
                    v.wait_ge(S("nm_step"), step[0])

                t = slice(2 * b, 2 * b + 2)
                m, r, parts = neg_max[:, t, :], nm_rest[:, t, :], nm_parts[:, t, :, :]
                v.wait_ge(S("mx_read"), UX * n + UB * (b + 1))
                if layer == 1:
                    done(v.tensor_scalar(m, m, W("x1_b"), None, ALU.subtract))
                done(v.tensor_copy(parts[:, :, 0, :], m))
                done(v.tensor_tensor(r, m, parts[:, :, 0, :], ALU.subtract))
                done(v.tensor_copy(parts[:, :, 1, :], r))
                v.tensor_tensor(parts[:, :, 2, :], r, parts[:, :, 1, :], ALU.subtract)\
                 .then_inc(S("nm_parts"), 1)
                done(v.memset(unused[0:1, 0:1], 0.0))

            for b in range(QB):
                for e in range(UB * b, UB * (b + 1)):
                    _, h0 = unit(e)
                    v.wait_ge(S("mx_ps"), UX * n + e + 1)
                    p = pair("M", e)
                    v.tensor_reduce(neg_max[:, 2 * b:2 * b + 2, h0:h0 + 2].rearrange("p t j -> p j t"),
                                    ps[:, p:p + 2, :].rearrange("p j (t k) -> p j t k", t=2), AX.X, ALU.max,
                                    negate=True).then_inc(S("mx_read"), 1)
                minus_max(b)
            for b in range(QB):
                t = slice(2 * b, 2 * b + 2)
                v.wait_ge(S("x_tokens"), QB * n + b + 1)
                o = bank(2 + b)[:, 0:2 * X_COLS].rearrange("p (t c) -> p t c", t=2)
                v.reciprocal(rden[:, t, 0:XH], o[:, :, D:X_COLS]).then_inc(S("xden"), 1)
                v.wait_ge(S("xden"), QB * n + b + 1)
                v.tensor_tensor(gate[:, t, :].rearrange("p t (h d) -> p t h d", h=XH),
                                o[:, :, 0:D].rearrange("p t (h d) -> p t h d", h=XH),
                                rden[:, t, 0:XH].unsqueeze(3).broadcast_to([P, 2, XH, XD]), ALU.mult)\
                 .then_inc(S("xon"), 1)
            for b in range(QB):
                xb = xq[:, 2 * b:2 * b + 2, :]
                if layer == 0:
                    v.wait_ge(S("xout_ps"), QB * n + b + 1)
                    v.tensor_tensor(xb, xb, bank(b)[:, 0:T].rearrange("p (a d) -> p a d", a=2), ALU.add)\
                     .then_inc(S("x2"), 1)
                else:
                    v.wait_ge(S("xon"), QB * n + b + 1)
                    v.tensor_tensor(xb, xb, gate[:, 2 * b:2 * b + 2, :], ALU.add).then_inc(S("x2"), 1)
            v.wait_ge(S("x2"), QB * (n + 1))

        def sp_xattn(sp, n, q, layer):
            sp.wait_ge(S("k_slots"), XH * (n + 1))
            sp.dma_start(ks[layer][ROW_BIAS:ROW_BIAS + 1, :, :],
                         mask_bias[:, bass.ds(q * QN, QN)].unsqueeze(1).broadcast_to([1, XH, QN]))\
              .then_inc(S("mask_row_in"), 16)
            for b in range(QB):
                sp.wait_ge(S("nm_rows"), QB * n + b + 1)
                for part in range(3):
                    sp.dma_start(qs[ROW_MAX + part:ROW_MAX + part + 1, :, b * T:(b + 1) * T],
                                 nm_rows[part * XH:(part + 1) * XH, b * T:(b + 1) * T]).then_inc(S("max_in"), 16)

        MU = MH // 2
        MX = QB * MU
        p_part = [pT[:, c // 2, c % 2 * 512:(c % 2 + 1) * 512] for c in range(4)]
        m_on = [xo0, xo1] + [pT[:, 0, c * 512:(c + 1) * 512] for c in range(2)]

        M_RING = 4
        key_ring = w2[:, 0:M_RING * 2 * T].rearrange("p (u j t) -> p u j t", u=M_RING, j=2)

        def m_head(u, jj):
            hp = u % MU
            return u // MU, hp // 2, STRIP * (2 * (hp % 2) + jj)

        def m_pair(u):
            return 2 * (u % 2)

        def m_bank(b, g):
            return 4 + 2 * b + g // 2

        def pe_mla(pe, n):
            pe.wait_ge(S("ln_xnT"), 3 * (n + QUADS) + 1)
            pe.matmul(bank(1), W("m_lat"), xnT[:, :], start=True, stop=True).then_inc(S("lat_ps"), 1)
            pe.wait_ge(S("lat"), n + 1)
            pe.matmul(bank(2), W("m_qr"), lat[:, :], start=True, stop=True).then_inc(S("qr_ps"), 1)
            kb, qb = (3, 4, 6, 7), (0, 1, 2, 3)
            for g in range(MG):
                pe.matmul(bank(kb[g]), W("m_k")[:, g * P:(g + 1) * P], lat[:, :], start=True, stop=True)\
                  .then_inc(S("mk_ps"), 1)
            for j in range(QT):
                i = pe.matmul(bank(5)[:, j * P:(j + 1) * P], lat[:, j * P:(j + 1) * P], W("m_v"),
                              start=True, stop=True)
            i.then_inc(S("mv_ps"), 1)
            pe.wait_ge(S("tq"), n + 1)
            for g in range(MG):
                if g == MG - 1:
                    pe.wait_ge(S("mka"), MG * n + 1)
                pe.matmul(bank(qb[g]), W("m_q")[:, g * P:(g + 1) * P], lat[:, :], start=True, stop=False)
                pe.matmul(bank(qb[g]), C("sel_rope")[:, g * P:(g + 1) * P], tq[:, :], start=False, stop=True)\
                  .then_inc(S("mq_ps"), 1)

            def scores(u):
                b, hp = u // MU, u % MU
                if u == 0:
                    pe.wait_ge(S("mqa"), MG * (n + 1))
                    pe.wait_ge(S("mka"), MG * (n + 1))
                    pe.wait_ge(S("mva"), n + 1)
                if u >= 2:
                    pe.wait_ge(S("ms_read"), MX * n + u - 1)
                pe.wait_ge(S("key_ring"), MX * n + u + 1)
                for jj in range(2):
                    b, g, _ = m_head(u, jj)
                    o = bank(m_pair(u) + jj)
                    k, qq = key_ring[:, u % M_RING, jj, :], qa[:, g, :]
                    pe.matmul(o[:, 0:T], k[:, 0:P], qq[:, b * T:(b + 1) * T], start=True, stop=True)
                    i = pe.matmul(o[:, T:T + P], k[:, P:T], qq[:, b * T + P:(b + 1) * T],
                                  start=True, stop=True)
                i.then_inc(S("ms_ps"), 1)

            def values(u):
                b, hp = u // MU, u % MU
                pe.wait_ge(S("mp"), MX * n + u + 1)
                for jj in range(2):
                    r, g = STRIP * (2 * (hp % 2) + jj), hp // 2
                    o = bank(m_bank(b, g), STRIP, r)[:, g % 2 * T:(g % 2 + 1) * T]
                    p = pT[:, u % 3, jj * 512:jj * 512 + 3 * P]
                    pe.matmul(o, vm[:, 2 * b, 2 * hp + jj, :], p[:, 0:T], start=True, stop=False,
                              skip_group_check=True)
                    i = pe.matmul(o[:, P:T], vm[:, 2 * b + 1, 2 * hp + jj, :], p[:, T:T + P], start=False,
                                  stop=True, skip_group_check=True)
                i.then_inc(S("mpv"), 1)

            for u in range(MX + 2):
                if u < MX:
                    scores(u)
                if u >= 2:
                    values(u - 2)
            for b in range(QB):
                for c in range(2):
                    pe.wait_ge(S("mo"), 2 * (QB * n + b) + c + 1)
                    for t in range(2):
                        for g in range(2 * c, 2 * c + 2):
                            i = pe.matmul(bank(2 * b + t)[:, 0:M_COLS],
                                          m_on[2 * b + c][:, g % 2 * T + t * P:g % 2 * T + (t + 1) * P],
                                          C("m_sel")[:, g * M_COLS:(g + 1) * M_COLS], start=(g == 0),
                                          stop=(g == MG - 1))
                i.then_inc(S("m_tokens"), 1)
            for b in range(QB):
                pe.wait_ge(S("mon"), QB * n + b + 1)
                for t in range(2):
                    i = pe.transpose(bank(4 + b)[:, t * P:(t + 1) * P], gate[:, 2 * b + t, :], ident)
                i.then_inc(S("moT_ps"), 1)
            for b in range(QB):
                pe.wait_ge(S("moT"), QB * n + b + 1)
                for t in range(2):
                    j = 2 * b + t
                    i = pe.matmul(bank(6 + b)[:, t * P:(t + 1) * P], oT[:, j * P:(j + 1) * P], W("m_o"),
                                  start=True, stop=True)
                i.then_inc(S("mout_ps"), 1)

        def act_mla(a, n):
            kb = (3, 4, 6, 7)
            for g in range(MG):
                a.wait_ge(S("mk_ps"), MG * n + g + 1)
                a.activation(ka[:, g, :], bank(kb[g]), ACT.Copy).then_inc(S("mka"), 1)
            a.wait_ge(S("mv_ps"), n + 1)
            a.activation(vm[:, :, :, 0:MD], bank(5).rearrange("p (a h d) -> p a h d", a=QT, h=MH),
                         ACT.Copy).then_inc(S("mva"), 1)

            def copy_values(b):
                a.wait_ge(S("mpv"), MX * n + MU * (b + 1))
                for c in range(2 * b, 2 * b + 2):
                    a.activation(m_on[c], bank(4 + c), ACT.Copy).then_inc(S("mo"), 1)

            def ring(u):
                if u >= M_RING:
                    a.wait_ge(S("ms_ps"), MX * n + u - M_RING + 1)
                for jj in range(2):
                    b, g, r = m_head(u, jj)
                    i = a.activation(key_ring[r:r + STRIP, u % M_RING, jj, :],
                                     ka[r:r + STRIP, g, b * T:(b + 1) * T], ACT.Copy)
                i.then_inc(S("key_ring"), 1)

            a.wait_ge(S("mka"), MG * (n + 1))
            for u in range(3):
                ring(u)
            for u in range(MX):
                if u + 3 < MX:
                    ring(u + 3)
                if u >= 3:
                    a.wait_ge(S("mpv"), MX * n + u - 2)
                a.wait_ge(S("ms_read"), MX * n + u + 1)
                view = [t.rearrange("p (a b) -> p a b", a=2)[:, :, 0:3 * P] for t in (pT[:, u % 3, :], cl[:, u % 2, :])]
                a.activation(view[0], view[1], ACT.Exp, scale=float(MD + MR) ** -0.5).then_inc(S("mp"), 1)
                if u == MU + 2:
                    copy_values(0)
            copy_values(1)
            for b in range(QB):
                a.wait_ge(S("moT_ps"), QB * n + b + 1)
                a.activation(oT[:, b * T:(b + 1) * T], bank(4 + b)[:, 0:T], ACT.Copy).then_inc(S("moT"), 1)

        def dve_mla(v, n):
            v.wait_ge(S("lat_ps"), n + 1)

            def rope(name):
                return C(name).unsqueeze(1).broadcast_to([P, QB, T])

            v.tensor_tensor(tri3(lat[:, :], QB), tri3(bank(1), QB), rope("lat_rope"), ALU.mult)\
             .then_inc(S("lat"), 1)
            v.wait_ge(S("qr_ps"), n + 1)
            v.tensor_tensor(tri3(tq[:, :], QB), tri3(bank(2), QB), rope("q_rope"), ALU.mult)\
             .then_inc(S("tq"), 1)
            for g in range(MG):
                v.wait_ge(S("mq_ps"), MG * n + g + 1)
                v.tensor_copy(qa[:, g, :], bank((0, 1, 2, 3)[g])).then_inc(S("mqa"), 1)

            for u in range(MX):
                if u >= 2:
                    v.wait_ge(S("mp"), MX * n + u - 1)
                v.wait_ge(S("ms_ps"), MX * n + u + 1)
                p = m_pair(u)
                blocks = ps[:, p:p + 2, :].rearrange("p a (b c) -> p (a b) c", c=P)
                out = cl[:, u % 2, :].rearrange("p (a c) -> p a c", c=P)
                v.scalar_tensor_tensor(out[:, 0:8:2, :], blocks[:, 0:8:2, :], -CLIP,
                                       C("clip_mask").unsqueeze(1).broadcast_to([P, 4, P]), ALU.max, ALU.min)
                v.tensor_scalar(out[:, 1:8:4, :], blocks[:, 1:8:4, :], -CLIP, CLIP, ALU.max, ALU.min)\
                 .then_inc(S("ms_read"), 1)
            for b in range(QB):
                t = slice(2 * b, 2 * b + 2)
                v.wait_ge(S("m_tokens"), QB * n + b + 1)
                o = ps[:, 2 * b:2 * b + 2, :]
                v.reciprocal(rden[:, t, :], o[:, :, D:M_COLS]).then_inc(S("mden"), 1)
                v.wait_ge(S("mden"), QB * n + b + 1)
                v.tensor_tensor(gate[:, t, :].rearrange("p t (h d) -> p t h d", h=MH),
                                o[:, :, 0:D].rearrange("p t (h d) -> p t h d", h=MH),
                                rden[:, t, :].unsqueeze(3).broadcast_to([P, 2, MH, MD]), ALU.mult)\
                 .then_inc(S("mon"), 1)
            for b in range(QB):
                v.wait_ge(S("mout_ps"), QB * n + b + 1)
                xb = xq[:, 2 * b:2 * b + 2, :]
                v.tensor_tensor(xb, xb, bank(6 + b)[:, 0:T].rearrange("p (a d) -> p a d", a=2), ALU.add)\
                 .then_inc(S("x3"), 1)
            v.wait_ge(S("x3"), QB * (n + 1))

        def pe_router(pe, n, layer):
            pe.wait_ge(S("ln_xnT"), 3 * n + 3)
            for j in range(QT):
                i = pe.matmul(bank(1)[:, j * EXP:(j + 1) * EXP], xnT[:, j * P:(j + 1) * P],
                              W("r%d_w" % layer), start=True, stop=True)
            i.then_inc(S("lg_ps"), 1)

        def dve_router(v, n, q, layer):
            tiles = bass.ds(q * QT, QT)
            v.wait_ge(S("lg_ps"), n + 1)
            v.tensor_tensor(lg[:, tiles, :], bank(1)[:, 0:QT * EXP].rearrange("p (a e) -> p a e", a=QT),
                            W("r%d_b" % layer).unsqueeze(1).broadcast_to([P, QT, EXP]), ALU.add)\
             .then_inc(S("lg"), 1)
            v.tensor_copy(x_all[:, tiles, :], xq[:, :, :]).then_inc(S("x_saved"), 1)
            v.wait_ge(S("xn_saved"), n + 1)

        def act_router(a, n, q):
            a.wait_ge(S("ln_xn"), QT * 3 * (n + 1))
            a.activation(xn_all[:, bass.ds(q * QT, QT), :], xn[:, :, :], ACT.Copy).then_inc(S("xn_saved"), 1)

        def pe_sort(pe, layer):
            pe.wait_ge(S("onehot"), layer + 1)
            oh = onehot[:, :, :].rearrange("p t e -> p (t e)")
            pe.matmul(bank(0)[:, 0:P], C("tri"), oh, start=True, stop=True)
            pe.matmul(bank(1)[:, 0:P], C("ones"), oh, start=True, stop=True).then_inc(S("rank_ps"), 1)

        def act_sort(a, layer):
            a.wait_ge(S("lless"), layer + 1)
            a.activation(lex[:, :, :], lg[:, :, :], ACT.Exp).then_inc(S("lex"), 1)

        SORT_STEPS = 20

        def dve_sort(v, layer):
            step = [layer * SORT_STEPS]

            def done(i):
                step[0] += 1
                i.then_inc(S("sort"), 1)
                v.wait_ge(S("sort"), step[0])

            def over(ap, shape, axis):
                return ap.unsqueeze(axis).broadcast_to(shape)

            te = [P, TILES, EXP]
            v.wait_ge(S("lg"), QUADS * (layer + 1))
            done(v.tensor_reduce(lmax[:, :], lg[:, :, :], AX.X, ALU.max))
            v.tensor_tensor(lg[:, :, :], lg[:, :, :], over(lmax[:, :], te, 2), ALU.subtract)\
             .then_inc(S("lless"), 1)
            v.wait_ge(S("lless"), layer + 1)
            done(v.scalar_tensor_tensor(tie[:, :, :],
                                        lg[:, :, :], 0.0, over(C("iota8m"), te, 1), ALU.is_equal, ALU.mult))
            done(v.tensor_reduce(amin[:, :], tie[:, :, :],
                                 AX.X, ALU.min))
            v.tensor_tensor(onehot[:, :, :], over(C("iota8m"), te, 1), over(amin[:, :], te, 2), ALU.is_equal)\
             .then_inc(S("onehot"), 1)
            v.wait_ge(S("lex"), layer + 1)
            done(v.tensor_reduce(lsum[:, :], lex[:, :, :], AX.X, ALU.add))
            done(v.reciprocal(prob[:, :], lsum[:, :]))
            v.wait_ge(S("rank_ps"), layer + 1)
            done(v.tensor_copy(cnt[:, :, :], bank(1)[:, 0:P].rearrange("p (t e) -> p e t", e=EXP)))
            flat = [t[:, :, :].rearrange("p e t -> p (e t)") for t in (incl, cnt)]
            done(v.tensor_tensor_scan(flat[0], C("scan_reset"), flat[1], 0.0, ALU.mult, ALU.add))
            total = incl[:, :, TILES - 1]
            et = [P, EXP, TILES]
            done(v.tensor_tensor(more[:, :, :], over(total, et, 2), over(C("tile_starts"), et, 1), ALU.is_gt))
            done(v.tensor_reduce(ntile[:, :], more[:, :, :], AX.X, ALU.add))
            done(v.tensor_tensor_scan(ends[:, :], C("ones")[:, 0:EXP], ntile[:, :], 0.0, ALU.mult, ALU.add))
            done(v.tensor_tensor(starts[:, :], ends[:, :], ntile[:, :], ALU.subtract))
            done(v.tensor_tensor(incl[:, :, :], incl[:, :, :], cnt[:, :, :], ALU.subtract))
            done(v.scalar_tensor_tensor(incl[:, :, :], over(starts[:, :], et, 2), float(P), incl[:, :, :],
                                        ALU.mult, ALU.add))
            et_t = incl[:, :, :].rearrange("p e t -> p t e")
            done(v.tensor_tensor(lex[:, :, :], bank(0)[:, 0:P].rearrange("p (t e) -> p t e", e=EXP), et_t, ALU.add))
            done(v.tensor_tensor(lex[:, :, :], lex[:, :, :], onehot[:, :, :], ALU.mult))
            done(v.tensor_reduce(pos_f[:, :], lex[:, :, :], AX.X, ALU.add))
            v.tensor_copy(pos[:, :], pos_f[:, :]).then_inc(S("pos"), 1)
            if layer == 0:
                v.memset(slot_f[:, :], 0.0).then_inc(S("ys"), 2)
                v.wait_ge(S("ys"), 2)
            se = [P, SLOTS, EXP]
            done(v.tensor_tensor(slot_ge[:, :, :], over(C("slot_iota"), se, 2), over(ends[:, :], se, 1), ALU.is_ge))
            done(v.tensor_reduce(slot_f[:, :], slot_ge[:, :, :], AX.X, ALU.add))
            if layer == 0:
                for s in range(2):
                    v.memset(ys[:, 2 * s:2 * s + 2, :], 0.0).then_inc(S("y_out%d" % s), 16)
            done(v.tensor_scalar(slot_e[:, :], slot_f[:, :], float(EXP - 1), None, ALU.min))
            pairs = slot_f[:, 0:SLOTS // 2]
            done(v.scalar_tensor_tensor(pairs, slot_e[:, 0:SLOTS:2], float(EXP), slot_e[:, 1:SLOTS:2],
                                        ALU.mult, ALU.add))
            v.scalar_tensor_tensor(turn_e[:, :], pairs[:, 0:SLOTS // 2:2], float(EXP * EXP),
                                   pairs[:, 1:SLOTS // 2:2], ALU.mult, ALU.add).then_inc(S("slots"), 1)

        PER_TURN = 4
        TURNS = SLOTS // PER_TURN

        def pool_scatter(g, layer):
            g.wait_ge(S("pos"), layer + 1)
            g.wait_ge(S("xn_saved"), QUADS * (layer + 1))
            g.wait_ge(S("zeroed"), 16)
            for t in range(TILES):
                g.indirect_dma_start(A["sorted_x"], bass.IndirectOffsetOnAxis(ap=pos[:, t:t + 1], axis=0),
                                     xn_all[:, t, :], None).then_inc(S("scattered"), 16)

        def pool_gather(g, layer):
            for s in range(2):
                g.wait_ge(S("y_out%d" % s), 16 * ((layer + 1) * TURNS + 1))
            for t in range(TILES):
                g.indirect_dma_start(xn_all[:, t, :], None, A["sorted_y"],
                                     bass.IndirectOffsetOnAxis(ap=pos[:, t:t + 1], axis=0))\
                 .then_inc(S("gathered_first" if t < QT else "gathered"), 16)

        def lane(s):
            return 4 * (s % 2)

        def xsT_bank(s):
            return lane(s) + (3 if s < 2 else 0)

        def rows_of(name, slot, count):
            return A[name][bass.ds(slot * P, count * P), :].rearrange("(s p) d -> p s d", p=P)

        def sp_experts(sp, layer):
            sp.wait_ge(S("scattered"), 16 * TILES * (layer + 1))
            sp.dma_start(xs[:, :, :], rows_of("sorted_x", 0, PER_TURN)).then_inc(S("xs_in"), 16)

            def turn(i, last):
                n = i + layer * TURNS
                if not last:
                    sp.wait_ge(S("xsT_ps"), PER_TURN * (n + 1))
                    sp.dma_start(xs[:, :, :], rows_of("sorted_x", (i + 1) * PER_TURN, PER_TURN))\
                      .then_inc(S("xs_in"), 16)
                for p in range(2):
                    sp.wait_ge(S("ys"), PER_TURN * n + 2 * p + 4)
                    sp.dma_start(rows_of("sorted_y", i * PER_TURN + 2 * p, 2), ys[:, 2 * p:2 * p + 2, :])\
                      .then_inc(S("y_out%d" % p), 16)

            with sp.Fori(0, TURNS - 1) as i:
                turn(i, False)
            turn(TURNS - 1, True)

        def slot_experts(engine, i):
            word = engine.value_load(turn_e[0:1, bass.ds(i, 1)], min_val=0, max_val=EXP ** PER_TURN - 1)
            return [word // EXP ** (PER_TURN - 1 - s) % EXP if s else word // EXP ** (PER_TURN - 1)
                    for s in range(PER_TURN)]

        def pe_experts(pe, layer):
            pe.wait_ge(S("slots"), layer + 1)
            pe.wait_ge(S("w_in"), 32 * (layer + 1))
            wsrc = w2 if layer == 0 else w2b
            with pe.Fori(0, TURNS) as i:
                n = i + layer * TURNS

                def rows_in(s):
                    if s >= 2:
                        pe.wait_ge(S("ys"), PER_TURN * n + s - 1)
                    pe.transpose(bank(xsT_bank(s))[:, 0:P], xs[:, s, :], ident).then_inc(S("xsT_ps"), 1)

                def hidden(s):
                    pe.wait_ge(S("xsT"), PER_TURN * n + s + 1)
                    if layer == 0:
                        for half in range(2):
                            k = pe.matmul(bank(lane(s) + 1 + half), xsT[:, s, :],
                                          w1[:, bass.ds(es[s] * (2 * F) + half * F, F)], start=True, stop=True)
                    else:
                        k = pe.matmul(bank(lane(s) + 1), xsT[:, s, :], w1b[:, bass.ds(es[s] * F, F)],
                                      start=True, stop=True)
                    k.then_inc(S("h_ps"), 1)

                def turned(s):
                    pe.wait_ge(S("hid"), PER_TURN * n + s + 1)
                    for j in range(4):
                        k = pe.transpose(bank(lane(s) + 3)[:, j * P:(j + 1) * P], hid[:, s % 2, j * P:(j + 1) * P],
                                         ident)
                    k.then_inc(S("hT_ps"), 1)

                def rows_out(s):
                    pe.wait_ge(S("hidT"), PER_TURN * n + s + 1)
                    if s >= 2:
                        pe.wait_ge(S("ys"), PER_TURN * n + s + 1)
                    for j in range(4):
                        k = pe.matmul(bank(lane(s))[:, 0:D], hidT[:, s % 2, j * P:(j + 1) * P],
                                      wsrc[:, bass.ds(es[s] * (4 * D) + j * D, D)], start=(j == 0), stop=(j == 3))
                    k.then_inc(S("y_ps"), 1)

                pe.wait_ge(S("xs_in"), 16 * (n + 1))
                rows_in(0)
                rows_in(1)
                es = slot_experts(pe, i)
                hidden(0)
                hidden(1)
                rows_in(2)
                rows_in(3)
                turned(0)
                turned(1)
                hidden(2)
                hidden(3)
                rows_out(0)
                rows_out(1)
                turned(2)
                turned(3)
                rows_out(2)
                rows_out(3)

        def act_experts(a, layer):
            a.wait_ge(S("slots"), layer + 1)
            with a.Fori(0, TURNS) as i:
                n = i + layer * TURNS
                if layer == 1:
                    es = slot_experts(a, i)

                def rows_in(s):
                    a.wait_ge(S("xsT_ps"), PER_TURN * n + s + 1)
                    a.activation(xsT[:, s, :], bank(xsT_bank(s))[:, 0:P], ACT.Copy).then_inc(S("xsT"), 1)

                def hidden(s):
                    a.wait_ge(S("h_ps"), PER_TURN * n + s + 1)
                    if layer == 0:
                        a.activation(act_a[:, s % 2, :], bank(lane(s) + 1), ACT.Silu).then_inc(S("silu_a"), 1)
                    else:
                        a.activation(hid[:, s % 2, :], bank(lane(s) + 1), ACT.Copy).then_inc(S("hid"), 1)

                def turned(s):
                    a.wait_ge(S("hT_ps"), PER_TURN * n + s + 1)
                    if layer == 0:
                        a.activation(hidT[:, s % 2, :], bank(lane(s) + 3), ACT.Copy).then_inc(S("hidT"), 1)
                    else:
                        for j in range(4):
                            k = a.activation(hidT[:, s % 2, j * P:(j + 1) * P],
                                             bank(lane(s) + 3)[:, j * P:(j + 1) * P],
                                             ACT.Relu, bias=W("b1")[:, bass.ds(es[s] * 4 + j, 1)])
                        k.then_inc(S("hidT"), 1)

                for pair_of, more in ((0, True), (2, False)):
                    if pair_of == 0:
                        rows_in(0)
                        rows_in(1)
                    hidden(pair_of)
                    hidden(pair_of + 1)
                    if more:
                        rows_in(2)
                        rows_in(3)
                    turned(pair_of)
                    turned(pair_of + 1)

        def dve_experts(v, layer):
            v.wait_ge(S("slots"), layer + 1)
            with v.Fori(0, TURNS) as i:
                n = i + layer * TURNS
                if layer == 1:
                    es = slot_experts(v, i)
                if layer == 0:
                    for s in range(PER_TURN):
                        v.wait_ge(S("silu_a"), PER_TURN * n + s + 1)
                        v.tensor_tensor(hid[:, s % 2, :], bank(lane(s) + 2), act_a[:, s % 2, :], ALU.mult)\
                         .then_inc(S("hid"), 1)
                for s in range(PER_TURN):
                    v.wait_ge(S("y_ps"), PER_TURN * n + s + 1)
                    v.wait_ge(S("y_out%d" % (s // 2)), 16 * (n + 1))
                    if layer == 0:
                        v.tensor_copy(ys[:, s, :], bank(lane(s))[:, 0:D]).then_inc(S("ys"), 1)
                    else:
                        v.tensor_tensor(ys[:, s, :], bank(lane(s))[:, 0:D], W("b2")[:, bass.ds(es[s] * D, D)],
                                        ALU.add).then_inc(S("ys"), 1)

        def dve_combine(v, q, layer, first=False):
            tiles = bass.ds(q * QT, QT)
            y = xn_all[:, tiles, :]
            p = prob[:, tiles].unsqueeze(2).broadcast_to([P, QT, D])
            if first:
                v.wait_ge(S("gathered_first"), 16 * QT * (layer + 1))
            else:
                v.wait_ge(S("gathered"), 16 * (TILES - QT) * (layer + 1))
            if layer == 0:
                v.wait_ge(S("x_saved"), QUADS + q)
            v.tensor_tensor(y, y, p, ALU.mult).then_inc(S("yp"), 1)
            v.wait_ge(S("yp"), q + layer * QUADS + 1)
            out = xq[:, :, :] if layer == 0 else x_all[:, tiles, :]
            v.tensor_tensor(out, y, x_all[:, tiles, :], ALU.add).then_inc(S("x_next"), 1)
            if layer == 0:
                v.wait_ge(S("x_next"), q + 1)

        def sp_context(sp, q):
            sp.wait_ge(S("k_part2"), QUADS + q)
            sp.wait_ge(S("xva"), QUADS + q)
            sp.dma_start(ctxT[:, 0, :], A["ctxT"][:, 0, bass.ds(q * QN, QN)]).then_inc(S("k_in"), 16)
            sp.dma_start(ctxT[:, 1, :].rearrange("p (a d) -> p a d", a=QT),
                         A["ctxv"][:, bass.ds(q * QT, QT), :]).then_inc(S("v_in"), 16)

        @block.sync
        def _(sp):
            sp.dma_start(xq[:, :, :], A["x"][:, 0:QT, :]).then_inc(S("x_in"), 16)
            sp.dma_start(cst[:, 0:C_LATE], A["consts"][:, 0:C_LATE]).then_inc(S("consts_in"), 16)
            sp.dma_start(wts[:, 0:W_LATE], A["weights"][:, 0:W_LATE]).then_inc(S("weights_in"), 16)
            sp.dma_start(ctxT[:, :, :], A["ctxT"][:, :, 0:QN]).then_inc(S("ctx_in"), 16)
            sp.dma_start(mask_row[:, :], A["mask"].broadcast_to([P, B * T])).then_inc(S("mask_in"), 16)
            sp.dma_start(mask_col[:, :], A["mask_col"]).then_inc(S("mask_in"), 16)
            sp.dma_start(x_all[:, QT:, :], A["x"][:, QT:, :]).then_inc(S("x_in"), 16)
            with sp.Fori(0, QUADS - 1) as q:
                sp.wait_ge(S("xv_ps"), q + 1)
                sp.dma_start(ctxT[:, :, :], A["ctxT"][:, :, bass.ds((q + 1) * QN, QN)]).then_inc(S("ctx_in"), 16)
                sp_xattn(sp, q, q, 0)
            sp_xattn(sp, QUADS - 1, QUADS - 1, 0)
            sp_context(sp, 0)
            sp.wait_ge(S("x_saved"), QUADS)
            sp.dma_start(mask_i[:, :],
                         A["mask_i"].broadcast_to([P, B * T])).then_inc(S("mask_in"), 16)
            sp_experts(sp, 0)
            with sp.Fori(0, QUADS - 1) as q:
                sp_xattn(sp, q + QUADS, q, 1)
                sp_context(sp, q + 1)
            sp_xattn(sp, 2 * QUADS - 1, QUADS - 1, 1)
            sp_experts(sp, 1)
            with sp.Fori(0, QUADS) as q:
                sp.wait_ge(S("x_next"), QUADS + q + 1)
                sp.dma_start(A["out"][:, bass.ds(q * QT, QT), :], x_all[:, bass.ds(q * QT, QT), :]).then_inc(S("out_written"), 16)
            sp.wait_ge(S("out_written"), 16 * QUADS)

        @block.gpsimd
        def _(g):
            g.memset(zeros[:, :], 0.0).then_inc(S("zeros"), 1)
            g.memset(am[:, :, :, :], 0.0).then_inc(S("cleared"), 1)
            g.memset(ke_bd[:, :, :], 0.0).then_inc(S("cleared"), 1)
            g.memset(sel_kp[:, :, :, :], 0.0).then_inc(S("cleared"), 1)
            g.memset(sel_qp[:, :, :], 0.0).then_inc(S("cleared"), 1)
            g.memset(vm[:, :, :, :], 1.0).then_inc(S("filled"), 1)
            g.wait_ge(S("consts_in"), 16)
            g.wait_ge(S("weights_in"), 16)
            with g.Fori(0, QUADS) as q:
                pool_ln(g, 3 * q)
                pool_gla(g, q)
                pool_ln(g, 3 * q + 1)
                pool_ln(g, 3 * q + 2)
            g.wait_ge(S("x2"), QB * QUADS)
            pool_key_parts(g, QUADS, 0)
            pool_scatter(g, 0)
            g.wait_ge(S("y_ps"), SLOTS)
            g.memset(w2[:, 0:8 * T], 0.0).then_inc(S("ring_clear"), 1)
            pool_gather(g, 0)

            def quad(q, last):
                n = q + QUADS
                for k in range(3):
                    pool_ln(g, 3 * n + k)
                if not last:
                    g.wait_ge(S("x2"), QB * (n + 1))
                    pool_key_parts(g, n + 1, q + 1)

            with g.Fori(0, QUADS - 1) as q:
                quad(q, False)
            quad(QUADS - 1, True)
            pool_scatter(g, 1)
            pool_gather(g, 1)

        @block.scalar
        def _(a):
            a.wait_ge(S("consts_in"), 16)
            a.wait_ge(S("weights_in"), 16)
            a.wait_ge(S("cleared"), 2)

            a.dma_start(w1[:, :], A["w1_0"]).then_inc(S("w_in"), 16)
            a.dma_start(w2[:, :], A["w2_0"]).then_inc(S("w_in"), 16)
            a.wait_ge(S("zeros"), 1)
            a.dma_start(A["sorted_x"].rearrange("(s p) d -> p s d", p=P),
                        zeros[:, :].unsqueeze(1).broadcast_to([P, SLOTS, D])).then_inc(S("zeroed"), 16)
            a.dma_start(cst[:, C_LATE:], A["consts"][:, C_LATE:]).then_inc(S("late_in"), 16)
            a.dma_start(wts[:, W_LATE:], A["weights"][:, W_LATE:]).then_inc(S("late_in"), 16)
            a.preload_act_table_set(LN_EXP)

            def quad(q, layer, last):
                n = q + layer * QUADS
                act_slots(a, "k", n, layer)
                act_ln(a, 3 * n, 0)
                act_gla(a, q) if layer == 0 else act_mla(a, q)
                act_ln(a, 3 * n + 1, 0)
                act_xattn(a, n, q, layer)
                if not last:
                    act_key_part(a, 0, n + 1, q + 1, layer)
                act_ln(a, 3 * n + 2, 0)
                if not last:
                    act_key_part(a, 1, n + 1, q + 1, layer)
                act_router(a, n, q)

            for part in range(2):
                act_key_part(a, part, 0, 0, 0)
            for layer in range(2):
                with a.Fori(0, QUADS - 1) as q:
                    quad(q, layer, False)
                quad(QUADS - 1, layer, True)
                if layer == 0:
                    for part in range(2):
                        act_key_part(a, part, QUADS, 0, 1)
                act_sort(a, layer)
                if layer == 0:
                    a.preload_act_table_set(SILU)
                act_experts(a, layer)
                if layer == 0:
                    a.preload_act_table_set(LN_EXP)
                    a.wait_ge(S("y_ps"), SLOTS)
                    a.dma_start(w1b, A["w1_1"]).then_inc(S("w_in"), 16)
                    a.dma_start(w2b, A["w2_1"]).then_inc(S("w_in"), 16)
                    a.wait_ge(S("late_in"), 32)
                if layer == 0:
                    a.wait_ge(S("ring_clear"), 1)

        @block.tensor
        def _(pe):
            pe.wait_ge(S("consts_in"), 16)
            pe.wait_ge(S("weights_in"), 16)
            pe.wait_ge(S("selections"), 8)

            def quad(q, layer, last):
                n = q + layer * QUADS
                pe_keys(pe, n)
                pe_ln(pe, 3 * n, 0)
                pe_gla(pe, q) if layer == 0 else pe_mla(pe, q)
                pe_ln(pe, 3 * n + 1, 0)
                pe_xattn(pe, n, layer)
                if layer == 0 and not last:
                    pe_project(pe, n + 1)
                pe_ln(pe, 3 * n + 2, 0)
                pe_router(pe, n, layer)

            pe_project(pe, 0)
            for layer in range(2):
                with pe.Fori(0, QUADS - 1) as q:
                    quad(q, layer, False)
                quad(QUADS - 1, layer, True)
                pe_sort(pe, layer)
                pe_experts(pe, layer)
                if layer == 0:
                    pe.wait_ge(S("ys"), SLOTS + 2)
                    pe.wait_ge(S("late_in"), 32)

        @block.vector
        def _(v):
            v.wait_ge(S("filled"), 1)
            v.wait_ge(S("consts_in"), 16)
            v.wait_ge(S("weights_in"), 16)
            v.wait_ge(S("cleared"), 4)
            v.tensor_copy(ident_b[:, :], ident).then_inc(S("selections"), 1)
            dims = ident.rearrange("p (h d) -> p h d", h=XH)
            for slot, (qp, kp) in enumerate(zip(Q_PARTS, K_PARTS)):
                if qp is not None:
                    at = slice(slot * XD, (slot + 1) * XD)
                    v.tensor_copy(sel_qp[:, :, at], dims)
                    v.tensor_copy(sel_kp[:, kp, :, at], dims).then_inc(S("selections"), 1)
            v.wait_ge(S("mask_in"), 32)
            v.tensor_scalar(mask_bias[:, :], mask_row[0:1, :], 1.0, BIG, ALU.subtract, ALU.mult)\
             .then_inc(S("selections"), 1)
            v.wait_ge(S("selections"), 8)
            dve_keys(v, 0, 0)
            dve_rest(v, "k", 0, kf, 1.0)
            dve_last_part(v, "k", 0)
            v.wait_ge(S("x_in"), 32)

            def quad(q, last):
                dve_ln(v, 3 * q)
                dve_values(v, q, q)
                dve_gla(v, q)
                dve_ln(v, 3 * q + 1)
                dve_xattn(v, q, q, 0)
                dve_ln(v, 3 * q + 2, None if last else lambda: dve_keys(v, q + 1, q + 1))
                if not last:
                    dve_rest(v, "k", q + 1, kf, 1.0)
                dve_router(v, q, q, 0)
                if not last:
                    v.wait_ge(S("x_saved"), q + 1)
                    v.tensor_copy(xq[:, :, :], x_all[:, bass.ds((q + 1) * QT, QT), :]).then_inc(S("x_out"), 1)
                    dve_last_part(v, "k", q + 1)
                    v.wait_ge(S("x_out"), q + 1)

            with v.Fori(0, QUADS - 1) as q:
                quad(q, False)
            quad(QUADS - 1, True)
            dve_sort(v, 0)
            v.wait_ge(S("mask_in"), 48)
            v.tensor_copy(mask_row[:, :], mask_i[:, :]).then_inc(S("mask1"), 1)
            v.wait_ge(S("mask1"), 1)
            m3 = mask_row[:, :].rearrange("p (b t) -> p b t", b=B)
            v.tensor_reduce(has[:, :], m3, AX.X, ALU.max).then_inc(S("mask1"), 1)
            v.wait_ge(S("mask1"), 2)
            v.tensor_scalar(nothas[:, :], has[:, :], -1.0, 1.0, ALU.mult, ALU.add).then_inc(S("mask1"), 1)
            v.wait_ge(S("mask1"), 3)
            v.tensor_tensor(m3[0:1], m3[0:1], nothas[0:1, :].unsqueeze(2).broadcast_to([1, B, T]), ALU.max)\
             .then_inc(S("mask1"), 1)
            v.wait_ge(S("mask1"), 4)
            v.tensor_scalar(mask_bias[:, :], mask_row[0:1, :], 1.0, BIG, ALU.subtract, ALU.mult)\
             .then_inc(S("mask1"), 1)
            dve_experts(v, 0)
            v.wait_ge(S("late_in"), 32)
            dve_combine(v, 0, 0, True)

            def quad1(q, last):
                n = q + QUADS
                dve_ln(v, 3 * n)
                dve_mla(v, q)
                dve_ln(v, 3 * n + 1)
                dve_xattn(v, n, q, 1)
                dve_ln(v, 3 * n + 2)
                dve_router(v, n, q, 1)
                if not last:
                    dve_combine(v, q + 1, 0)

            with v.Fori(0, QUADS - 1) as q:
                quad1(q, False)
            quad1(QUADS - 1, True)
            dve_sort(v, 1)
            dve_experts(v, 1)
            dve_combine(v, 0, 1, True)
            with v.Fori(0, QUADS - 1) as q:
                dve_combine(v, q + 1, 1)


def constants():
    c = np.zeros((P, CN), np.float32)

    def put(name, a, r0=0):
        at, n = CC[name]
        a = np.asarray(a, np.float32)
        c[r0:r0 + a.shape[0], at:at + n] = a.reshape(a.shape[0], n)

    p = np.arange(P)
    put("ident", np.eye(P))
    put("chunk_mask", (p[:, None] <= p[None]) & (p[:, None] // CHUNK == p[None] // CHUNK))
    put("tri", p[:, None] < p[None])
    put("ones", np.ones((P, P)))
    k = p % 64
    put("head_mask", k[:, None] // DK == np.arange(GH)[None])
    put("block_mask", k[:, None] // DK == (p // DV)[None])
    put("reset", np.broadcast_to(np.arange(QN) % CHUNK != 0, (P, QN)))
    lim = np.where(p[:, None] <= p[None], CLIP, -BIG)
    put("clip_mask", lim)
    inv = (np.float32(10000.0) ** (-np.arange(0, MR, 2, dtype=np.float32) / MR)).astype(np.float32)
    ang = np.arange(T, dtype=np.float32)[None] * inv[:, None]
    cos, sin = np.cos(ang).astype(np.float32), np.sin(ang).astype(np.float32)
    r = np.arange(MR)
    cos4, sin4 = cos[r // 2], sin[r // 2] * np.where(r % 2 == 0, -1.0, 1.0)[:, None]
    lat = np.zeros((P, T), np.float32)
    lat[0:64] = 1.0
    lat[64:64 + MR], lat[96:96 + MR] = cos4, sin4
    put("lat_rope", lat)
    put("q_rope", np.concatenate([np.tile(cos4, (MH, 1)), np.tile(sin4, (MH, 1))]))

    def to_tokens(heads, size):
        sel = np.zeros((P, heads // 4, D + heads), np.float32)
        for h in range(heads):
            for d in range(size):
                sel[STRIP * (h % 4) + d, h // 4, h * size + d] = 1.0
            sel[STRIP * (h % 4) + XD, h // 4, D + h] = 1.0
        return sel

    put("x_sel", to_tokens(XH, XD))
    put("m_sel", to_tokens(MH, MD))
    sel = np.zeros((P, MG, P), np.float32)
    for h in range(MH):
        for d in range(MR):
            for half in range(2):
                sel[64 * half + h * MR + d, h // 4, STRIP * (h % 4) + MD + d] = 1.0
    put("sel_rope", sel)
    e = np.arange(EXP)
    put("iota8", np.broadcast_to(e, (P, EXP)))
    put("iota8m", np.broadcast_to(e - EXP, (P, EXP)))
    put("slot_iota", np.broadcast_to(np.arange(SLOTS), (P, SLOTS)))
    put("scan_reset", np.broadcast_to(np.arange(P) % TILES != 0, (P, P)))
    put("neg_half", np.full((P, 32), -0.5))
    put("eps", np.full((P, 32), EPS))
    put("tile_starts", np.broadcast_to(P * np.arange(TILES), (P, TILES)))
    put("q_one", p[:, None] == ROW_BIAS)
    put("k_ones", (p[:, None] >= ROW_MAX) & (p[:, None] < ROW_MAX + 3))
    return c


def weights(I):
    w = np.zeros((P, WN), np.float32)

    def put(name, a):
        at, n = WC[name]
        w[0:a.shape[0], at:at + n] = a.reshape(a.shape[0], n)

    def strips(m, heads, size, rows=P, r0=0):
        out = np.zeros((rows, heads // 4, 4, STRIP), np.float32)
        out[r0:r0 + m.shape[0], :, :, 0:size] = m.reshape(m.shape[0], heads // 4, 4, size)
        return out.reshape(rows, heads // 4, P)

    swap = np.arange(MR) ^ 1
    put("wq", np.tile(I["L0_attn_Wq"], (1, 2)))
    put("wk", np.tile(I["L0_attn_Wk"], (1, 2)))
    put("wv", I["L0_attn_Wv"])
    put("wg", I["L0_attn_Wg"])
    put("wgk1", np.pad(I["L0_attn_Wgk1"], ((0, 0), (0, 112))))
    put("wgk2", np.tile(I["L0_attn_Wgk2"], (1, 2)))
    put("bgk", np.tile(I["L0_attn_bgk2"], 2)[:, None])
    put("norm_w", np.broadcast_to(I["L0_attn_norm_w"], (P, DV)))
    put("wo", I["L0_attn_Wo"])
    put("x_q", I["L0_xattn_W_tgt"].T)
    src = I["L0_xattn_W_src"]
    kt = src[0:D].T
    put("x_k", np.stack([kt[0:P], kt[P:]], 1))
    put("x_v", np.stack([src[D:].T[0:P], src[D:].T[P:]], 1))
    put("x_qb", I["L0_xattn_b_tgt"][:, None])
    put("x_kb", I["L0_xattn_b_src"][0:D, None])
    put("x_vb", I["L0_xattn_b_src"][None, D:])
    wo = I["L0_xattn_W_out"].T
    put("x_out", np.stack([wo[0:P], wo[P:]], 1))
    put("x_ob", I["L0_xattn_b_out"][None])
    put("r0_w", I["L0_ffn_router_w"])
    put("r0_b", np.broadcast_to(I["L0_ffn_router_b"], (P, EXP)))
    m = np.zeros((P, P), np.float32)
    m[:, 0:ML], m[:, ML:2 * ML] = I["L1_attn_W_DQ"], I["L1_attn_W_DKV"]
    m[:, 64:64 + MR], m[:, 96:96 + MR] = I["L1_attn_W_KR"], I["L1_attn_W_KR"][:, swap]
    put("m_lat", m)
    qr = I["L1_attn_W_QR"].reshape(ML, MH, MR)
    put("m_qr", np.concatenate([qr.reshape(ML, -1), qr[:, :, swap].reshape(ML, -1)], 1))
    put("m_q", strips(I["L1_attn_W_UQ"], MH, MD))
    mk = strips(I["L1_attn_W_UK"], MH, MD, r0=ML).reshape(P, MG, 4, STRIP)
    for d in range(MR):
        mk[64 + d, :, :, MD + d] = 1.0
        mk[96 + d, :, :, MD + d] = 1.0
    put("m_k", mk)
    m = np.zeros((P, P), np.float32)
    m[ML:2 * ML] = I["L1_attn_W_UV"]
    put("m_v", m)
    put("m_o", I["L1_attn_W_O"])
    put("x1_b", np.broadcast_to(I["L1_xattn_b"], (P, 1)))
    put("r1_w", I["L1_ffn_w_gate"])
    put("r1_b", np.broadcast_to(I["L1_ffn_b_gate"], (P, EXP)))
    put("b1", I["L1_ffn_b1"].reshape(EXP, 4, P).transpose(2, 0, 1))
    put("b2", np.broadcast_to(I["L1_ffn_b2"].reshape(1, -1), (P, EXP * D)))
    return w


def kernel(**inputs):
    import numpy as np
    import concourse.bacc as bacc
    from concourse import mybir
    from concourse.bass_utils import run_bass_kernel_spmd

    I = {k: np.asarray(v) for k, v in inputs.items()}
    ctx = I["ctx_2048"].reshape(TILES, P, DC)
    ctxT = I["ctx_2048"].reshape(B * T, 2, P).transpose(2, 1, 0)
    arrays = {
        "x": I["x"].reshape(TILES, P, D).transpose(1, 0, 2),
        "ctxT": ctxT,
        "ctxv": ctx[:, :, D:].transpose(1, 0, 2),
        "mask": I["mask_BxS2_fk1"].reshape(1, B * T),
        "mask_col": I["mask_BxS2_fk1"].reshape(TILES, P).T,
        "mask_i": I["mask_BxS2_ik0"].reshape(1, B * T),
        "w1_0": I["L0_ffn_w1"].transpose(1, 0, 2).reshape(P, -1),
        "w2_0": I["L0_ffn_w2"].reshape(EXP, 4, P, D).transpose(2, 0, 1, 3).reshape(P, -1),
        "w1_1": I["L1_ffn_W1"].transpose(1, 0, 2).reshape(P, -1),
        "w2_1": I["L1_ffn_W2"].reshape(EXP, 4, P, D).transpose(2, 0, 1, 3).reshape(P, -1),
        "consts": constants(),
        "weights": weights(I),
    }
    nc = bacc.Bacc("TRN2", target_bir_lowering=False, num_devices=1)
    feed, A = {}, {}
    for name, a in arrays.items():
        a = np.ascontiguousarray(a)
        feed["in_" + name] = a
        A[name] = nc.dram_tensor("in_" + name, a.shape, mybir.dt.from_np(a.dtype), kind="ExternalInput").ap()
    for name in ("sorted_x", "sorted_y"):
        A[name] = nc.dram_tensor(name, (SLOTS * P, D), mybir.dt.float32, kind="Internal").ap()
    A["out"] = nc.dram_tensor("out_x", (P, TILES, D), mybir.dt.float32, kind="ExternalOutput").ap()
    build(nc, A)
    r = run_bass_kernel_spmd(nc, [feed], core_ids=[0])
    out = r.results[0]["out_x"]
    return out.transpose(1, 0, 2).reshape(B, T, D)
```
